# Optimizing a Trainium2 kernel written in Bass

```python
import numpy as np
import jax
import jax.numpy as jnp

def _softmax(x, axis=-1):
    return jax.nn.softmax(x, axis=axis)

def _gelu(x):
    return jax.nn.gelu(x, approximate=True)

def _silu(x):
    return jax.nn.silu(x)

def _sigmoid(x):
    return jax.nn.sigmoid(x)

def _layernorm(x, axis=-1, eps=1e-05):
    m = jnp.mean(x, axis=axis, keepdims=True)
    v = jnp.var(x, axis=axis, keepdims=True)
    return (x - m) / jnp.sqrt(v + eps)

def _scatter_add(tgt, idx, src, axis=0):
    return tgt.at[idx].add(src)

def _segment_sum(src, seg, n):
    return jax.ops.segment_sum(src, seg, n)
kernel_name = 'mk_macaron_d2_jaxref_r8_2ab22f'

def setup_inputs(seed: int=0):
    np.random.seed(seed)
    _w = jnp.asarray

    def _L0_attn_setup():
        import jax, jax.numpy as jnp
        import numpy as np
        DIM, HEADS, LAYERS, HID = (128, 16, 6, 512)
        PAST_CTX, MAX_PERIOD = (125, 10000.0)
        HEAD_DIM = DIM // HEADS

        def _ln(x, g, b, eps=1e-05):
            m = jnp.mean(x, axis=-1, keepdims=True)
            v = jnp.mean((x - m) ** 2, axis=-1, keepdims=True)
            return (x - m) * jax.lax.rsqrt(v + eps) * g + b

        def _forward(x, norm_in_g, norm_in_b, Wqkv, bqkv, Wo, bo, ln1_g, ln1_b, ln2_g, ln2_b, W1, b1, W2, b2):
            B, T, C = x.shape
            H = 1
            half = C // 2
            positions = jnp.arange(T, dtype=jnp.float32)[None, :, None]
            adim = jnp.arange(half, dtype=jnp.float32)[None, None, :]
            phase = positions / MAX_PERIOD ** (adim / (half - 1))
            pos_emb = jnp.concatenate([jnp.cos(phase), jnp.sin(phase)], axis=-1)
            x = _ln(x, norm_in_g, norm_in_b) + pos_emb
            q_pos = jnp.arange(H, T + H)[:, None]
            k_pos = jnp.arange(T + H)[None, :]
            delta = q_pos - k_pos
            valid = (delta >= 0) & (delta <= PAST_CTX)
            neg = jnp.finfo(x.dtype).min
            past = jnp.zeros((B, H, C), x.dtype)
            for l in range(LAYERS):
                keys = jnp.concatenate([past, x], axis=1)
                Wq, Wk, Wv = (Wqkv[l][:C], Wqkv[l][C:2 * C], Wqkv[l][2 * C:])
                bq, bk, bv = (bqkv[l][:C], bqkv[l][C:2 * C], bqkv[l][2 * C:])
                q = (x @ Wq.T + bq).reshape(B, T, HEADS, HEAD_DIM)
                k = (keys @ Wk.T + bk).reshape(B, T + H, HEADS, HEAD_DIM)
                v = (keys @ Wv.T + bv).reshape(B, T + H, HEADS, HEAD_DIM)
                scores = jnp.einsum('bqhd,bkhd->bhqk', q, k) / jnp.sqrt(jnp.asarray(HEAD_DIM, x.dtype))
                scores = jnp.where(valid[None, None], scores, neg)
                attn = jax.nn.softmax(scores, axis=-1)
                o = jnp.einsum('bhqk,bkhd->bqhd', attn, v).reshape(B, T, C)
                o = o @ Wo[l].T + bo[l]
                x = _ln(x + o, ln1_g[l], ln1_b[l])
                ff = jax.nn.gelu(x @ W1[l].T + b1[l], approximate=False) @ W2[l].T + b2[l]
                x = _ln(x + ff, ln2_g[l], ln2_b[l])
            return x
        key = jax.random.key(seed)
        ks = jax.random.split(key, 8)
        s = 0.02
        inp = {'x': jax.random.normal(ks[0], (2, 256, DIM), jnp.float32), 'norm_in_g': jnp.ones((DIM,), jnp.float32), 'norm_in_b': jnp.zeros((DIM,), jnp.float32), 'Wqkv': jax.random.normal(ks[1], (LAYERS, 3 * DIM, DIM), jnp.float32) * s, 'bqkv': jnp.zeros((LAYERS, 3 * DIM), jnp.float32), 'Wo': jax.random.normal(ks[2], (LAYERS, DIM, DIM), jnp.float32) * s, 'bo': jnp.zeros((LAYERS, DIM), jnp.float32), 'ln1_g': jnp.ones((LAYERS, DIM), jnp.float32), 'ln1_b': jnp.zeros((LAYERS, DIM), jnp.float32), 'ln2_g': jnp.ones((LAYERS, DIM), jnp.float32), 'ln2_b': jnp.zeros((LAYERS, DIM), jnp.float32), 'W1': jax.random.normal(ks[3], (LAYERS, HID, DIM), jnp.float32) * s, 'b1': jnp.zeros((LAYERS, HID), jnp.float32), 'W2': jax.random.normal(ks[4], (LAYERS, DIM, HID), jnp.float32) * s, 'b2': jnp.zeros((LAYERS, DIM), jnp.float32)}
        return inp
    _L0_attn_in = _L0_attn_setup()

    def _L0_ffn_setup():
        import jax, jax.numpy as jnp
        import numpy as np
        NUM_EXPERTS = 8
        N_EMBD = 128
        D_FF = 4 * N_EMBD
        B, S = (4, 256)
        key = jax.random.key(seed)
        ks = jax.random.split(key, 6)
        x = jax.random.normal(ks[0], (B, S, N_EMBD), dtype=jnp.float32)
        gate_w = jax.random.normal(ks[1], (N_EMBD, NUM_EXPERTS), dtype=jnp.float32) * 0.02
        w1 = jax.random.normal(ks[2], (NUM_EXPERTS, N_EMBD, D_FF), dtype=jnp.float32) * 0.02
        b1 = jnp.zeros((NUM_EXPERTS, D_FF), dtype=jnp.float32)
        w2 = jax.random.normal(ks[3], (NUM_EXPERTS, D_FF, N_EMBD), dtype=jnp.float32) * 0.02
        b2 = jnp.zeros((NUM_EXPERTS, N_EMBD), dtype=jnp.float32)
        return {'x': x, 'gate_w': gate_w, 'w1': w1, 'b1': b1, 'w2': w2, 'b2': b2}
    _L0_ffn_in = _L0_ffn_setup()

    def _L1_attn_setup():
        import jax, jax.numpy as jnp
        import numpy as np
        NUM_HEADS = 16
        LN_EPS = 1e-05
        NORM_EPS = 1e-12

        def _l2norm(t):
            return t / jnp.maximum(jnp.linalg.norm(t, axis=-1, keepdims=True), NORM_EPS)

        def _forward(x, Wq, Wk, Wv, Wf1, Wf2, Wg, Wo1, Wo2, ln_w, Wout):
            B, N, D = x.shape
            H = NUM_HEADS
            HD = D // H
            q = jax.nn.silu(x @ Wq)
            k = jax.nn.silu(x @ Wk)
            v = jax.nn.silu(x @ Wv)
            log_f = jax.nn.log_sigmoid(x @ Wf1 @ Wf2)
            gamma = -jax.nn.sigmoid(x @ Wg)
            q = q.reshape(B, N, H, HD)
            k = k.reshape(B, N, H, HD)
            v = v.reshape(B, N, H, HD)
            log_f = log_f.reshape(B, N, H, HD)
            k = _l2norm(k)
            a = k * gamma[..., None]

            def step(S, inp):
                qt, kt, vt, at, gft = inp
                bs1 = jnp.einsum('bhk,bhkv->bhv', kt, S)
                S1 = S + at[..., :, None] * bs1[..., None, :]
                S2 = jnp.exp(gft)[..., None] * S1
                bs2 = jnp.einsum('bhk,bhkv->bhv', kt, S2)
                S3 = S2 + at[..., :, None] * bs2[..., None, :] + kt[..., :, None] * vt[..., None, :]
                o = jnp.einsum('bhk,bhkv->bhv', qt, S3)
                return (S3, o)
            to_time = lambda t: jnp.moveaxis(t, 1, 0)
            S0 = jnp.zeros((B, H, HD, HD), dtype=x.dtype)
            _, o = jax.lax.scan(step, S0, (to_time(q), to_time(k), to_time(v), to_time(a), to_time(log_f)))
            o = jnp.moveaxis(o, 0, 1)
            z = jnp.zeros_like(o)
            out3 = jnp.stack([z, z, o], axis=2).reshape(B, 3 * N, H, HD)
            out = out3[:, -N:]
            out = out.reshape(B, N, D)
            gate = jax.nn.sigmoid(x @ Wo1 @ Wo2)
            out = out * gate
            mu = jnp.mean(out, axis=-1, keepdims=True)
            var = jnp.mean((out - mu) ** 2, axis=-1, keepdims=True)
            out = (out - mu) * jax.lax.rsqrt(var + LN_EPS) * ln_w
            return out @ Wout
        key = jax.random.key(seed)
        ks = jax.random.split(key, 12)
        B, N, D = (2, 128, 128)
        HD = D // NUM_HEADS
        s = 0.02
        inp = {'x': jax.random.normal(ks[0], (B, N, D), dtype=jnp.float32), 'Wq': jax.random.normal(ks[1], (D, D), dtype=jnp.float32) * s, 'Wk': jax.random.normal(ks[2], (D, D), dtype=jnp.float32) * s, 'Wv': jax.random.normal(ks[3], (D, D), dtype=jnp.float32) * s, 'Wf1': jax.random.normal(ks[4], (D, HD), dtype=jnp.float32) * s, 'Wf2': jax.random.normal(ks[5], (HD, D), dtype=jnp.float32) * s, 'Wg': jax.random.normal(ks[6], (D, NUM_HEADS), dtype=jnp.float32) * s, 'Wo1': jax.random.normal(ks[7], (D, HD), dtype=jnp.float32) * s, 'Wo2': jax.random.normal(ks[8], (HD, D), dtype=jnp.float32) * s, 'ln_w': jnp.ones((D,), dtype=jnp.float32), 'Wout': jax.random.normal(ks[9], (D, D), dtype=jnp.float32) * s}
        return inp
    _L1_attn_in = _L1_attn_setup()

    def _L1_ffn_setup():
        import jax, jax.numpy as jnp
        import numpy as np
        EPS = 1e-05
        N_HEADS = 16
        TOP_K = 2

        def _ln(x, g, b):
            m = x.mean(-1, keepdims=True)
            v = ((x - m) ** 2).mean(-1, keepdims=True)
            return (x - m) / jnp.sqrt(v + EPS) * g + b

        def _block_fwd(x, ln1_g, ln1_b, ln2_g, ln2_b, Wq, bq, Wk, bk, Wv, bv, Wo, bo, Wr, br, e_w1, e_b1, e_w2, e_b2):
            B, S, D = x.shape
            H = N_HEADS
            hd = D // H
            h = _ln(x, ln1_g, ln1_b)
            q = (h @ Wq + bq).reshape(B, S, H, hd).transpose(0, 2, 1, 3)
            k = (h @ Wk + bk).reshape(B, S, H, hd).transpose(0, 2, 1, 3)
            v = (h @ Wv + bv).reshape(B, S, H, hd).transpose(0, 2, 1, 3)
            scores = jnp.einsum('bhqd,bhkd->bhqk', q, k) / hd ** 0.5
            causal = jnp.tril(jnp.ones((S, S), dtype=bool))
            scores = jnp.where(causal, scores, -jnp.inf)
            attn = jax.nn.softmax(scores, axis=-1)
            o = jnp.einsum('bhqk,bhkd->bhqd', attn, v).transpose(0, 2, 1, 3).reshape(B, S, D)
            a = o @ Wo + bo + x
            h2 = _ln(a, ln2_g, ln2_b)
            logits = h2 @ Wr + br
            topv = jax.lax.top_k(logits, TOP_K)[0]
            kmask = logits >= topv[..., -1:]
            w = jax.nn.softmax(jnp.where(kmask, logits, -jnp.inf), axis=-1)
            mid = jax.nn.gelu(jnp.einsum('bsd,edf->bsef', h2, e_w1) + e_b1, approximate=False)
            eo = jnp.einsum('bsef,efd->bsed', mid, e_w2) + e_b2
            moe = jnp.einsum('bse,bsed->bsd', w, eo)
            return moe + a
        key = jax.random.key(seed)
        B, S, D, E = (1, 256, 128, 8)
        F = 4 * D
        ks = jax.random.split(key, 8)

        def n(k, shape):
            return jax.random.normal(k, shape, jnp.float32) * 0.02
        return dict(x=jax.random.normal(ks[0], (B, S, D), jnp.float32), ln1_g=jnp.ones((D,), jnp.float32), ln1_b=jnp.zeros((D,), jnp.float32), ln2_g=jnp.ones((D,), jnp.float32), ln2_b=jnp.zeros((D,), jnp.float32), Wq=n(ks[1], (D, D)), bq=jnp.zeros((D,), jnp.float32), Wk=n(ks[2], (D, D)), bk=jnp.zeros((D,), jnp.float32), Wv=n(ks[3], (D, D)), bv=jnp.zeros((D,), jnp.float32), Wo=n(ks[4], (D, D)), bo=jnp.zeros((D,), jnp.float32), Wr=n(ks[5], (D, E)), br=jnp.zeros((E,), jnp.float32), e_w1=n(ks[6], (E, D, F)), e_b1=jnp.zeros((E, F), jnp.float32), e_w2=n(ks[7], (E, F, D)), e_b2=jnp.zeros((E, D), jnp.float32))
    _L1_ffn_in = _L1_ffn_setup()
    _d = {'L0_attn_x': _L0_attn_in['x'], 'L0_attn_norm_in_g': _L0_attn_in['norm_in_g'], 'L0_attn_norm_in_b': _L0_attn_in['norm_in_b'], 'L0_attn_Wqkv': _L0_attn_in['Wqkv'], 'L0_attn_bqkv': _L0_attn_in['bqkv'], 'L0_attn_Wo': _L0_attn_in['Wo'], 'L0_attn_bo': _L0_attn_in['bo'], 'L0_attn_ln1_g': _L0_attn_in['ln1_g'], 'L0_attn_ln1_b': _L0_attn_in['ln1_b'], 'L0_attn_ln2_g': _L0_attn_in['ln2_g'], 'L0_attn_ln2_b': _L0_attn_in['ln2_b'], 'L0_attn_W1': _L0_attn_in['W1'], 'L0_attn_b1': _L0_attn_in['b1'], 'L0_attn_W2': _L0_attn_in['W2'], 'L0_attn_b2': _L0_attn_in['b2'], 'L0_ffn_gate_w': _L0_ffn_in['gate_w'], 'L0_ffn_w1': _L0_ffn_in['w1'], 'L0_ffn_b1': _L0_ffn_in['b1'], 'L0_ffn_w2': _L0_ffn_in['w2'], 'L0_ffn_b2': _L0_ffn_in['b2'], 'L1_attn_Wq': _L1_attn_in['Wq'], 'L1_attn_Wk': _L1_attn_in['Wk'], 'L1_attn_Wv': _L1_attn_in['Wv'], 'L1_attn_Wf1': _L1_attn_in['Wf1'], 'L1_attn_Wf2': _L1_attn_in['Wf2'], 'L1_attn_Wg': _L1_attn_in['Wg'], 'L1_attn_Wo1': _L1_attn_in['Wo1'], 'L1_attn_Wo2': _L1_attn_in['Wo2'], 'L1_attn_ln_w': _L1_attn_in['ln_w'], 'L1_attn_Wout': _L1_attn_in['Wout'], 'L1_ffn_ln1_g': _L1_ffn_in['ln1_g'], 'L1_ffn_ln1_b': _L1_ffn_in['ln1_b'], 'L1_ffn_ln2_g': _L1_ffn_in['ln2_g'], 'L1_ffn_ln2_b': _L1_ffn_in['ln2_b'], 'L1_ffn_Wq': _L1_ffn_in['Wq'], 'L1_ffn_bq': _L1_ffn_in['bq'], 'L1_ffn_Wk': _L1_ffn_in['Wk'], 'L1_ffn_bk': _L1_ffn_in['bk'], 'L1_ffn_Wv': _L1_ffn_in['Wv'], 'L1_ffn_bv': _L1_ffn_in['bv'], 'L1_ffn_Wo': _L1_ffn_in['Wo'], 'L1_ffn_bo': _L1_ffn_in['bo'], 'L1_ffn_Wr': _L1_ffn_in['Wr'], 'L1_ffn_br': _L1_ffn_in['br'], 'L1_ffn_e_w1': _L1_ffn_in['e_w1'], 'L1_ffn_e_b1': _L1_ffn_in['e_b1'], 'L1_ffn_e_w2': _L1_ffn_in['e_w2'], 'L1_ffn_e_b2': _L1_ffn_in['e_b2']}
    _x0 = _d['L0_attn_x']
    _d['L0_attn_x'] = jax.random.normal(jax.random.fold_in(jax.random.key(seed), 1), (8, 512, 128), dtype=_x0.dtype)
    del _x0
    return _d

def reference(L0_attn_x, L0_attn_norm_in_g, L0_attn_norm_in_b, L0_attn_Wqkv, L0_attn_bqkv, L0_attn_Wo, L0_attn_bo, L0_attn_ln1_g, L0_attn_ln1_b, L0_attn_ln2_g, L0_attn_ln2_b, L0_attn_W1, L0_attn_b1, L0_attn_W2, L0_attn_b2, L0_ffn_gate_w, L0_ffn_w1, L0_ffn_b1, L0_ffn_w2, L0_ffn_b2, L1_attn_Wq, L1_attn_Wk, L1_attn_Wv, L1_attn_Wf1, L1_attn_Wf2, L1_attn_Wg, L1_attn_Wo1, L1_attn_Wo2, L1_attn_ln_w, L1_attn_Wout, L1_ffn_ln1_g, L1_ffn_ln1_b, L1_ffn_ln2_g, L1_ffn_ln2_b, L1_ffn_Wq, L1_ffn_bq, L1_ffn_Wk, L1_ffn_bk, L1_ffn_Wv, L1_ffn_bv, L1_ffn_Wo, L1_ffn_bo, L1_ffn_Wr, L1_ffn_br, L1_ffn_e_w1, L1_ffn_e_b1, L1_ffn_e_w2, L1_ffn_e_b2):

    def _L0_attn_ref(x, norm_in_g, norm_in_b, Wqkv, bqkv, Wo, bo, ln1_g, ln1_b, ln2_g, ln2_b, W1, b1, W2, b2):
        import jax, jax.numpy as jnp
        import numpy as np
        DIM, HEADS, LAYERS, HID = (128, 16, 6, 512)
        PAST_CTX, MAX_PERIOD = (125, 10000.0)
        HEAD_DIM = DIM // HEADS

        def _ln(x, g, b, eps=1e-05):
            m = jnp.mean(x, axis=-1, keepdims=True)
            v = jnp.mean((x - m) ** 2, axis=-1, keepdims=True)
            return (x - m) * jax.lax.rsqrt(v + eps) * g + b

        def _forward(x, norm_in_g, norm_in_b, Wqkv, bqkv, Wo, bo, ln1_g, ln1_b, ln2_g, ln2_b, W1, b1, W2, b2):
            B, T, C = x.shape
            H = 1
            half = C // 2
            positions = jnp.arange(T, dtype=jnp.float32)[None, :, None]
            adim = jnp.arange(half, dtype=jnp.float32)[None, None, :]
            phase = positions / MAX_PERIOD ** (adim / (half - 1))
            pos_emb = jnp.concatenate([jnp.cos(phase), jnp.sin(phase)], axis=-1)
            x = _ln(x, norm_in_g, norm_in_b) + pos_emb
            q_pos = jnp.arange(H, T + H)[:, None]
            k_pos = jnp.arange(T + H)[None, :]
            delta = q_pos - k_pos
            valid = (delta >= 0) & (delta <= PAST_CTX)
            neg = jnp.finfo(x.dtype).min
            past = jnp.zeros((B, H, C), x.dtype)
            for l in range(LAYERS):
                keys = jnp.concatenate([past, x], axis=1)
                Wq, Wk, Wv = (Wqkv[l][:C], Wqkv[l][C:2 * C], Wqkv[l][2 * C:])
                bq, bk, bv = (bqkv[l][:C], bqkv[l][C:2 * C], bqkv[l][2 * C:])
                q = (x @ Wq.T + bq).reshape(B, T, HEADS, HEAD_DIM)
                k = (keys @ Wk.T + bk).reshape(B, T + H, HEADS, HEAD_DIM)
                v = (keys @ Wv.T + bv).reshape(B, T + H, HEADS, HEAD_DIM)
                scores = jnp.einsum('bqhd,bkhd->bhqk', q, k) / jnp.sqrt(jnp.asarray(HEAD_DIM, x.dtype))
                scores = jnp.where(valid[None, None], scores, neg)
                attn = jax.nn.softmax(scores, axis=-1)
                o = jnp.einsum('bhqk,bkhd->bqhd', attn, v).reshape(B, T, C)
                o = o @ Wo[l].T + bo[l]
                x = _ln(x + o, ln1_g[l], ln1_b[l])
                ff = jax.nn.gelu(x @ W1[l].T + b1[l], approximate=False) @ W2[l].T + b2[l]
                x = _ln(x + ff, ln2_g[l], ln2_b[l])
            return x
        return _forward(x, norm_in_g, norm_in_b, Wqkv, bqkv, Wo, bo, ln1_g, ln1_b, ln2_g, ln2_b, W1, b1, W2, b2)

    def _L0_ffn_ref(x, gate_w, w1, b1, w2, b2):
        import jax, jax.numpy as jnp
        import numpy as np
        NUM_EXPERTS = 8
        N_EMBD = 128
        D_FF = 4 * N_EMBD
        B, S = (4, 256)
        Bb, Ss, D = x.shape
        x_flat = x.reshape(-1, D)
        router_logits = x_flat @ gate_w
        router_probs = jax.nn.softmax(router_logits, axis=-1)
        expert_idx = jnp.argmax(router_probs, axis=-1)
        expert_w = jnp.take_along_axis(router_probs, expert_idx[:, None], axis=1)[:, 0]
        out = jnp.zeros_like(x_flat)
        for e in range(NUM_EXPERTS):
            h = jax.nn.gelu(x_flat @ w1[e] + b1[e], approximate=False)
            y = h @ w2[e] + b2[e]
            sel = expert_idx == e
            out = out + jnp.where(sel, expert_w, 0.0)[:, None] * y
        return out.reshape(Bb, Ss, D)

    def _L1_attn_ref(x, Wq, Wk, Wv, Wf1, Wf2, Wg, Wo1, Wo2, ln_w, Wout):
        import jax, jax.numpy as jnp
        import numpy as np
        NUM_HEADS = 16
        LN_EPS = 1e-05
        NORM_EPS = 1e-12

        def _l2norm(t):
            return t / jnp.maximum(jnp.linalg.norm(t, axis=-1, keepdims=True), NORM_EPS)

        def _forward(x, Wq, Wk, Wv, Wf1, Wf2, Wg, Wo1, Wo2, ln_w, Wout):
            B, N, D = x.shape
            H = NUM_HEADS
            HD = D // H
            q = jax.nn.silu(x @ Wq)
            k = jax.nn.silu(x @ Wk)
            v = jax.nn.silu(x @ Wv)
            log_f = jax.nn.log_sigmoid(x @ Wf1 @ Wf2)
            gamma = -jax.nn.sigmoid(x @ Wg)
            q = q.reshape(B, N, H, HD)
            k = k.reshape(B, N, H, HD)
            v = v.reshape(B, N, H, HD)
            log_f = log_f.reshape(B, N, H, HD)
            k = _l2norm(k)
            a = k * gamma[..., None]

            def step(S, inp):
                qt, kt, vt, at, gft = inp
                bs1 = jnp.einsum('bhk,bhkv->bhv', kt, S)
                S1 = S + at[..., :, None] * bs1[..., None, :]
                S2 = jnp.exp(gft)[..., None] * S1
                bs2 = jnp.einsum('bhk,bhkv->bhv', kt, S2)
                S3 = S2 + at[..., :, None] * bs2[..., None, :] + kt[..., :, None] * vt[..., None, :]
                o = jnp.einsum('bhk,bhkv->bhv', qt, S3)
                return (S3, o)
            to_time = lambda t: jnp.moveaxis(t, 1, 0)
            S0 = jnp.zeros((B, H, HD, HD), dtype=x.dtype)
            _, o = jax.lax.scan(step, S0, (to_time(q), to_time(k), to_time(v), to_time(a), to_time(log_f)))
            o = jnp.moveaxis(o, 0, 1)
            z = jnp.zeros_like(o)
            out3 = jnp.stack([z, z, o], axis=2).reshape(B, 3 * N, H, HD)
            out = out3[:, -N:]
            out = out.reshape(B, N, D)
            gate = jax.nn.sigmoid(x @ Wo1 @ Wo2)
            out = out * gate
            mu = jnp.mean(out, axis=-1, keepdims=True)
            var = jnp.mean((out - mu) ** 2, axis=-1, keepdims=True)
            out = (out - mu) * jax.lax.rsqrt(var + LN_EPS) * ln_w
            return out @ Wout
        return _forward(x, Wq, Wk, Wv, Wf1, Wf2, Wg, Wo1, Wo2, ln_w, Wout)

    def _L1_ffn_ref(x, ln1_g, ln1_b, ln2_g, ln2_b, Wq, bq, Wk, bk, Wv, bv, Wo, bo, Wr, br, e_w1, e_b1, e_w2, e_b2):
        import jax, jax.numpy as jnp
        import numpy as np
        EPS = 1e-05
        N_HEADS = 16
        TOP_K = 2

        def _ln(x, g, b):
            m = x.mean(-1, keepdims=True)
            v = ((x - m) ** 2).mean(-1, keepdims=True)
            return (x - m) / jnp.sqrt(v + EPS) * g + b

        def _block_fwd(x, ln1_g, ln1_b, ln2_g, ln2_b, Wq, bq, Wk, bk, Wv, bv, Wo, bo, Wr, br, e_w1, e_b1, e_w2, e_b2):
            B, S, D = x.shape
            H = N_HEADS
            hd = D // H
            h = _ln(x, ln1_g, ln1_b)
            q = (h @ Wq + bq).reshape(B, S, H, hd).transpose(0, 2, 1, 3)
            k = (h @ Wk + bk).reshape(B, S, H, hd).transpose(0, 2, 1, 3)
            v = (h @ Wv + bv).reshape(B, S, H, hd).transpose(0, 2, 1, 3)
            scores = jnp.einsum('bhqd,bhkd->bhqk', q, k) / hd ** 0.5
            causal = jnp.tril(jnp.ones((S, S), dtype=bool))
            scores = jnp.where(causal, scores, -jnp.inf)
            attn = jax.nn.softmax(scores, axis=-1)
            o = jnp.einsum('bhqk,bhkd->bhqd', attn, v).transpose(0, 2, 1, 3).reshape(B, S, D)
            a = o @ Wo + bo + x
            h2 = _ln(a, ln2_g, ln2_b)
            logits = h2 @ Wr + br
            topv = jax.lax.top_k(logits, TOP_K)[0]
            kmask = logits >= topv[..., -1:]
            w = jax.nn.softmax(jnp.where(kmask, logits, -jnp.inf), axis=-1)
            mid = jax.nn.gelu(jnp.einsum('bsd,edf->bsef', h2, e_w1) + e_b1, approximate=False)
            eo = jnp.einsum('bsef,efd->bsed', mid, e_w2) + e_b2
            moe = jnp.einsum('bse,bsed->bsd', w, eo)
            return moe + a
        return _block_fwd(x, ln1_g, ln1_b, ln2_g, ln2_b, Wq, bq, Wk, bk, Wv, bv, Wo, bo, Wr, br, e_w1, e_b1, e_w2, e_b2)
    x = L0_attn_x
    x = x + 0.5 * _L0_ffn_ref(_layernorm(x, axis=-1), L0_ffn_gate_w, L0_ffn_w1, L0_ffn_b1, L0_ffn_w2, L0_ffn_b2)
    x = x + _L0_attn_ref(_layernorm(x, axis=-1), L0_attn_norm_in_g, L0_attn_norm_in_b, L0_attn_Wqkv, L0_attn_bqkv, L0_attn_Wo, L0_attn_bo, L0_attn_ln1_g, L0_attn_ln1_b, L0_attn_ln2_g, L0_attn_ln2_b, L0_attn_W1, L0_attn_b1, L0_attn_W2, L0_attn_b2)
    x = x + 0.5 * _L0_ffn_ref(_layernorm(x, axis=-1), L0_ffn_gate_w, L0_ffn_w1, L0_ffn_b1, L0_ffn_w2, L0_ffn_b2)
    x = x + 0.5 * _L1_ffn_ref(_layernorm(x, axis=-1), L1_ffn_ln1_g, L1_ffn_ln1_b, L1_ffn_ln2_g, L1_ffn_ln2_b, L1_ffn_Wq, L1_ffn_bq, L1_ffn_Wk, L1_ffn_bk, L1_ffn_Wv, L1_ffn_bv, L1_ffn_Wo, L1_ffn_bo, L1_ffn_Wr, L1_ffn_br, L1_ffn_e_w1, L1_ffn_e_b1, L1_ffn_e_w2, L1_ffn_e_b2)
    x = x + _L1_attn_ref(_layernorm(x, axis=-1), L1_attn_Wq, L1_attn_Wk, L1_attn_Wv, L1_attn_Wf1, L1_attn_Wf2, L1_attn_Wg, L1_attn_Wo1, L1_attn_Wo2, L1_attn_ln_w, L1_attn_Wout)
    x = x + 0.5 * _L1_ffn_ref(_layernorm(x, axis=-1), L1_ffn_ln1_g, L1_ffn_ln1_b, L1_ffn_ln2_g, L1_ffn_ln2_b, L1_ffn_Wq, L1_ffn_bq, L1_ffn_Wk, L1_ffn_bk, L1_ffn_Wv, L1_ffn_bv, L1_ffn_Wo, L1_ffn_bo, L1_ffn_Wr, L1_ffn_br, L1_ffn_e_w1, L1_ffn_e_b1, L1_ffn_e_w2, L1_ffn_e_b2)
    return x

_drawn_inputs = setup_inputs


def setup_inputs(seed=0):
    import zlib

    import numpy as np

    out = dict(_drawn_inputs(seed))
    spreads = {'L0_attn_norm_in_g': (1.0, 0.2),
     'L0_attn_norm_in_b': (0.0, 0.1),
     'L0_attn_bqkv': (0.0, 0.294),
     'L0_attn_bo': (0.0, 0.1),
     'L0_attn_ln1_g': (1.0, 0.2),
     'L0_attn_ln1_b': (0.0, 0.1),
     'L0_attn_ln2_g': (1.0, 0.2),
     'L0_attn_ln2_b': (0.0, 0.1),
     'L0_attn_b1': (0.0, 0.275),
     'L0_attn_b2': (0.0, 0.1),
     'L0_ffn_b1': (0.0, 0.8),
     'L0_ffn_b2': (0.0, 0.667),
     'L1_attn_ln_w': (1.0, 0.6),
     'L1_ffn_ln1_g': (1.0, 0.6),
     'L1_ffn_ln1_b': (0.0, 0.8),
     'L1_ffn_ln2_g': (1.0, 0.6),
     'L1_ffn_ln2_b': (0.0, 0.8),
     'L1_ffn_bq': (0.0, 0.8),
     'L1_ffn_bk': (0.0, 2.0),
     'L1_ffn_bv': (0.0, 0.8),
     'L1_ffn_bo': (0.0, 0.1),
     'L1_ffn_br': (0.0, 0.441),
     'L1_ffn_e_b1': (0.0, 0.8),
     'L1_ffn_e_b2': (0.0, 0.296)}
    factors = {'L0_ffn_gate_w': 4.462,
     'L0_ffn_w1': 8.0,
     'L0_ffn_w2': 8.0,
     'L1_attn_Wf1': 26.985,
     'L1_attn_Wf2': 25.092,
     'L1_attn_Wg': 113.904,
     'L1_attn_Wo1': 8.0,
     'L1_attn_Wo2': 8.0,
     'L1_ffn_Wq': 8.0,
     'L1_ffn_Wk': 8.0,
     'L1_ffn_Wv': 7.507,
     'L1_ffn_Wo': 5.263,
     'L1_ffn_e_w1': 3.833,
     'L1_ffn_e_w2': 3.441}
    for name, (base, spread) in spreads.items():
        noise = np.random.default_rng([zlib.crc32(name.encode()), seed]).standard_normal(out[name].shape)
        drawn = base * np.exp(spread * noise) if base else spread * noise
        out[name] = jnp.asarray(drawn.astype(out[name].dtype))
    for name, factor in factors.items():
        out[name] = (out[name] * factor).astype(out[name].dtype)
    return out
```

```python
from contextlib import ExitStack, contextmanager

import numpy as np

import concourse.bass as bass
from concourse import mybir

F32 = mybir.dt.float32
BF16 = mybir.dt.bfloat16
I32 = mybir.dt.int32
ALU = mybir.AluOpType
ACT = mybir.ActivationFunctionType
AX_X = mybir.AxisListType.X

P = 128
BATCHES, TOKENS = 8, 512
TPB = TOKENS // P
TILES = BATCHES * TPB
HEADS, HD = 16, 8
LAYERS = 6
HID = 512
CHUNKS = HID // P
EXPERTS = 8
PAST = 125
EPS = 1e-5
BIG = 1e30
MAGIC = 1597463007.0
SEEN = 176
OUT = 171
TURN_LAG = 2
START = 1
STEP_RING = 8

PER_TURN = {'pool window': (26, 2), 'pool ffn': (26, 2), 'dve window': (28, 2), 'dve ffn': (22, 2), 'dve causal': (8, 0), 'scan': (32,), 'scan seen': (34,),
            'pool layer': (208, 16), 'dve layer': (200, 16)}


class Tally:

    def __init__(self):
        self.base, self.n = 0, 0

    def value(self):
        return self.base + self.n


class Chain(Tally):

    def __init__(self, eng, sem):
        super().__init__()
        self.eng, self.sem = eng, sem

    def add(self, ins):
        ins.then_inc(self.sem, 1)
        self.n += 1

    def join(self):
        self.eng.wait_ge(self.sem, self.value())

    def link(self, ins):
        self.add(ins)
        self.join()


wrong = {}


@contextmanager
def counted_loop(eng, name, count, tallies):
    per = PER_TURN.get(name, (0,) * len(tallies))
    before = [(t.base, t.n) for t in tallies]
    with eng.Fori(0, count) as i:
        for t, k in zip(tallies, per):
            t.base = t.base + i * k
        yield i
        got = tuple(t.n - n for t, (_, n) in zip(tallies, before))
        if got != tuple(per):
            wrong[name] = got
    for t, (base, n), k in zip(tallies, before, got):
        t.base, t.n = base, n + count * k


class Group:

    def __init__(self, tile, heads, blocks, windowed, last_of_tile):
        self.tile, self.heads, self.blocks = tile, heads, blocks
        self.windowed, self.last_of_tile = windowed, last_of_tile
        self.first = tile == 0


def windowed_groups():
    return [Group(i, [[4 * g + 2 * j, 4 * g + 2 * j + 1] for g in range(4)], [i, i + 1], True, j == 1)
            for i in range(TPB) for j in range(2)]


def causal_groups():
    return [Group(i, [[4 * g + j] for g in range(4)], list(range(1, i + 2)), False, j == 3)
            for i in range(TPB) for j in range(4)]


class AttentionPhase:

    def __init__(self, sem, tag, groups, src):
        self.groups = groups
        self.units = [(p, k, g) for p in range(2) for k in range(len(groups)) for g in range(4)]
        self.src = src
        self.zs_ready = sem(tag + "zs_ready")
        self.zT_done = sem(tag + "zT_done")
        self.zT_ev = sem(tag + "zT_ev")
        self.q_done = sem(tag + "q_done")
        self.q_ev = sem(tag + "q_ev")
        self.k_done = sem(tag + "k_done")
        self.k_ev = sem(tag + "k_ev")
        self.v_done = sem(tag + "v_done")
        self.v_ev = sem(tag + "v_ev")
        self.pad_done = sem(tag + "pad_done")
        self.scores_done = sem(tag + "scores_done")
        self.max_done = sem(tag + "max_done")
        self.exp_done = sem(tag + "exp_done")
        self.t_done = sem(tag + "t_done")
        self.evac_act = sem(tag + "evac_act")
        self.evac_dve = sem(tag + "evac_dve")
        self.av_done = sem(tag + "av_done")
        self.norm_done = sem(tag + "norm_done")
        self.oT_done = sem(tag + "oT_done")
        self.oT_ev = sem(tag + "oT_ev")
        self.wo_done = sem(tag + "wo_done")
        self.wo_ev = sem(tag + "wo_ev")
        self.post_done = sem(tag + "post_done")


class ExpertPhase:

    def __init__(self, sem, tag, experts, src):
        self.experts = experts
        self.src = src
        self.pre_turns = 0
        self.x_ready = sem(tag + "x_ready")
        self.T_done = sem(tag + "T_done")
        self.T_ev = sem(tag + "T_ev")
        self.up_done = sem(tag + "up_done")
        self.gelu_done = sem(tag + "gelu_done")
        self.y_done = sem(tag + "y_done")
        self.acc_done = sem(tag + "acc_done")


class RecurrencePhase:

    def __init__(self, sem):
        self.h_ready = sem("r_h_ready")
        self.x_ready = sem("r_x_ready")
        self.T_done = sem("r_T_done")
        self.T_ev = sem("r_T_ev")
        self.kvqg_done = sem("r_kvqg_done")
        self.f1_ev = sem("r_f1_ev")
        self.g1_ev = sem("r_g1_ev")
        self.f_done = sem("r_f_done")
        self.gate_done = sem("r_gate_done")
        self.sg_ready = sem("r_sg_ready")
        self.fg_ready = sem("r_fg_ready")
        self.psum_free = sem("r_psum_free")
        self.st_ready = sem("r_st_ready")
        self.st_out = sem("r_st_out")
        self.scan_in = sem("r_scan_in")
        self.kv_ready = sem("r_kv_ready")
        self.step = sem("r_step")
        self.od_ready = sem("r_od_ready")
        self.o_out = sem("r_o_out")
        self.of_in = sem("r_of_in")
        self.o1_ready = sem("r_o1_ready")
        self.mean_done = sem("r_mean_done")
        self.sq_ready = sem("r_sq_ready")
        self.msq_done = sem("r_msq_done")
        self.ex_ready = sem("r_ex_ready")
        self.y_done = sem("r_y_done")
        self.x_done = sem("r_x_done")


def build(nc, d, out):
    ctx = ExitStack()
    with ctx:
        def sb(name, shape, dt=F32):
            return ctx.enter_context(nc.sbuf_tensor(name, shape, dt))

        def sem(name):
            return ctx.enter_context(nc.semaphore(name))

        ps = ctx.enter_context(nc.psum_tensor("ps", [P, 8, 512], F32))
        X = sb("X", [P, TILES, P])
        w1 = sb("w1", [P, EXPERTS, HID])
        w2 = sb("w2", [P, EXPERTS, CHUNKS, P])
        eb1 = sb("eb1", [P, EXPERTS, CHUNKS])
        eb2 = sb("eb2", [EXPERTS, P])
        gate_w = sb("gate_w", [P, EXPERTS])
        brow = sb("brow", [P, EXPERTS])
        aw = sb("aw", [P, 4, P])
        arow = sb("arow", [P, 4, P])
        acol = sb("acol", [P, 2])
        fw1 = sb("fw1", [P, HID])
        fw2 = sb("fw2", [P, CHUNKS, P])
        frow = sb("frow", [P, 3, P])
        fcol = sb("fcol", [P, CHUNKS])
        crow = sb("crow", [P, 4, P])
        pos = sb("pos", [P, TPB, P])
        ident = sb("ident", [P, P])
        identb = sb("identb", [P, P], BF16)
        mask_win = sb("mask_win", [P, 2, 2 * P], BF16)
        mask_win0 = sb("mask_win0", [P, 2, 2 * P], BF16)
        mask_diag = sb("mask_diag", [P, P], BF16)
        hm = sb("hm", [P, 4])
        rev = sb("rev", [P, EXPERTS])
        zero = sb("zero", [P, P])
        ones = sb("ones", [P, P])
        rt = [sb(f"rt{i}", [P, TILES, EXPERTS]) for i in range(4)]
        C = sb("C", [P, TILES, EXPERTS])
        LG = sb("LG", [P, TILES, EXPERTS])
        r1 = sb("r1", [P, TILES])
        r2 = sb("r2", [P, TILES])
        stats = sb("stats", [P, TILES, 6])
        mv = sb("mv", [P, TILES, 2])
        rstd = sb("rstd", [P, TILES])
        nv = sb("nv", [P, TILES])
        nt = sb("nt", [P, TILES])
        nmax = sb("nmax", [P, 8, 2])
        orec = sb("orec", [P, HEADS])

        arena = sb("arena", [P, 34048])
        at = [0]

        def take(*shape):
            n = int(np.prod(shape))
            v = arena[:, at[0]:at[0] + n]
            at[0] += n
            assert at[0] <= 34048
            if len(shape) == 2:
                v = v.rearrange("p (a b) -> p a b", b=shape[1])
            if len(shape) == 3:
                v = v.rearrange("p (a b c) -> p a b c", b=shape[1], c=shape[2])
            return v

        A = take(TILES, P)
        H = take(TILES, P)
        Pr = take(8, 512)
        PT = take(4, 512)
        Qe = [take(4, TOKENS) for _ in range(2)]
        Ke = [take(4, P + TOKENS) for _ in range(2)]
        Vx = [take(TPB + 1, HEADS, HD + 1) for _ in range(2)]
        On = [take(TPB, P) for _ in range(2)]
        OT = take(TPB, P)
        zs = [take(TPB, P) for _ in range(2)]
        zT = [take(TPB * P) for _ in range(2)]
        hid = [take(512) for _ in range(2)]
        at[0] = 0
        KW = take(TOKENS, 2, HD)
        UA = take(TOKENS, 2, HD)
        FD = take(HD, TOKENS)
        VD = take(HD, TOKENS)
        TMP = take(HD, TOKENS)
        QD = take(HD, SEEN)
        G1 = take(TOKENS)
        N2 = take(TOKENS)
        RN = take(TOKENS)
        T1 = take(TOKENS)
        C1 = take(TOKENS)
        GATE = take(BATCHES, OUT)
        KD = UA.rearrange("p a b c -> p (a b c)")[:, 0:HD * TOKENS].rearrange("p (a b) -> p a b", b=TOKENS)
        at[0] = 4 * HD * TOKENS + 2 * HD * TOKENS
        MM = take(STEP_RING, HD * HD, 4)
        SH = take(STEP_RING, HD, HD)
        M1 = take(2 * HD, HD)
        XY = take(2, HD)
        OQ = take(STEP_RING, HD, HD)
        at[0] = 4 * HD * TOKENS + 3 * HD * TOKENS + HD * SEEN
        OD = take(HD, SEEN)
        at[0] = 0
        OF = take(BATCHES, SEEN)
        O1 = take(BATCHES, OUT)
        O2 = take(BATCHES, OUT)
        O3 = take(BATCHES, OUT)
        O4 = take(BATCHES, OUT)
        at[0] = 2 * HD * TOKENS * 2
        EX = take(BATCHES, TOKENS)
        at[0] = 2 * TILES * P
        sgk, sgv, sgq, stf, stg = (take(TOKENS) for _ in range(5))
        stk, stv, stq = (take(TOKENS) for _ in range(3))
        f1s, g1s = take(TOKENS), take(TOKENS)

        scr_k = nc.dram_tensor("scr_k", [BATCHES, P, TOKENS], F32, kind="Internal").ap()
        scr_v = nc.dram_tensor("scr_v", [BATCHES, P, TOKENS], F32, kind="Internal").ap()
        scr_f = nc.dram_tensor("scr_f", [BATCHES, P, TOKENS], F32, kind="Internal").ap()
        scr_q = nc.dram_tensor("scr_q", [BATCHES, P, SEEN], F32, kind="Internal").ap()
        scr_g = nc.dram_tensor("scr_g", [BATCHES, HEADS, TOKENS], F32, kind="Internal").ap()
        scr_o = nc.dram_tensor("scr_o", [BATCHES, P, SEEN], F32, kind="Internal").ap()

        loaded = sem("loaded")
        stored = sem("stored")
        phase = sem("phase")
        const_ready = sem("const_ready")
        sink = sem("sink")
        v_chain = sem("v_chain")
        g_chain = sem("g_chain")
        a_chain = sem("a_chain")
        var_ready = sem("var_ready")
        rstd_ready = sem("rstd_ready")
        win = AttentionPhase(sem, "w_", windowed_groups(), A)
        cau = AttentionPhase(sem, "c_", causal_groups(), H)
        ffn = ExpertPhase(sem, "f_", 1, A)
        moe = ExpertPhase(sem, "m_", EXPERTS, H)
        h_ready = sem("h_ready")
        pT_done = sem("pT_done")
        pT_ev = sem("pT_ev")
        lg_done = sem("lg_done")
        lg_ev = sem("lg_ev")
        d_ready = sem("d_ready")
        e_ready = sem("e_ready")
        c_ready = sem("c_ready")
        cT_done = sem("cT_done")
        cT_ev = sem("cT_ev")
        yb_done = sem("yb_done")
        yb_ev = sem("yb_ev")
        R = RecurrencePhase(sem)

        ENGINES = 5

        def gate(eng):
            eng.sem_inc(sink, 1)

        def barrier(eng, n):
            gate(eng)
            eng.drain().then_inc(phase, 1)
            eng.wait_ge(phase, (n + 1) * ENGINES)
            gate(eng)

        PH_SETUP = 0
        PH_MOE1 = 1
        PH_INIT = 3
        PH_LAYER = 4
        PH_MOE2 = PH_LAYER + 2 * LAYERS
        PH_CAUSAL1 = PH_MOE2 + 2
        PH_REC = PH_CAUSAL1 + 4
        PH_CAUSAL2 = PH_REC + 3
        PH_END = PH_CAUSAL2 + 4

        def tiles(arr, b):
            return arr[:, bass.ts(b, TPB), :]

        def row(r):
            return r.unsqueeze(1).broadcast_to([P, TPB, P])

        block = ctx.enter_context(nc.Block())

        @block.sync
        def _(sp):
            n = [0]

            def load(dst, src):
                sp.dma_start(dst, src).then_inc(loaded, 16)
                n[0] += 16

            def load_attention(layer):
                load(aw[:], d["attn_w"][layer])
                load(arow[:], d["attn_row"][layer].partition_broadcast(P))
                load(acol[:], d["attn_col"][layer])

            def load_experts(a):
                load(w1[:], d[a + "_w1"].rearrange("e d f -> d e f"))
                load(w2[:], d[a + "_w2"].rearrange("e (c f) d -> f e c d", f=P))
                with nc.allow_non_contiguous_dma(reason="small bias columns"):
                    load(eb1[:], d[a + "_b1"].rearrange("e (c f) -> f e c", f=P))
                load(eb2[:], d[a + "_b2"])
                load(gate_w[:], d[a + "_gate"])

            load(X[:], d["x"].rearrange("b (i p) f -> p (b i) f", p=P))
            load_experts("L0")
            load(crow[:], d["crow"].partition_broadcast(P))
            load(pos[:], d["pos"].rearrange("(i p) f -> p i f", p=P))
            load(hm[:], d["hm"])
            load(rev[:], d["rev"].partition_broadcast(P))
            load(brow[:], d["L1_br"].partition_broadcast(P))
            sp.wait_ge(loaded, n[0])
            barrier(sp, PH_SETUP)
            barrier(sp, PH_MOE1)
            barrier(sp, PH_MOE1 + 1)
            load_attention(0)
            sp.wait_ge(loaded, n[0])
            barrier(sp, PH_INIT)
            base = n[0]
            with sp.Fori(0, LAYERS) as l:
                n[0] = 0
                load(fw1[:], d["ffn_w1"][l])
                load(fw2[:], d["ffn_w2"][l])
                load(frow[:], d["ffn_row"][l].partition_broadcast(P))
                load(fcol[:], d["ffn_col"][l])
                per = n[0] + 48
                sp.wait_ge(loaded, base + l * per + n[0])
                barrier(sp, PH_LAYER + 2 * l)
                load_attention(l + 1)
                sp.wait_ge(loaded, base + l * per + n[0])
                barrier(sp, PH_LAYER + 2 * l + 1)
                assert n[0] == per
            n[0] = base + LAYERS * per
            barrier(sp, PH_MOE2)
            barrier(sp, PH_MOE2 + 1)
            load_experts("L1")
            sp.wait_ge(loaded, n[0])
            barrier(sp, PH_CAUSAL1)
            barrier(sp, PH_CAUSAL1 + 1)
            load(aw[:], d["rec_w"])
            load(fw1[:, 0:8], d["rec_f1"])
            load(fw1[:, 8:16], d["rec_o1"])
            load(fw1[:, 16:32], d["rec_g"])
            load(fw2[0:8, 0, :], d["rec_f2"])
            load(fw2[0:8, 1, :], d["rec_o2"])
            load(fcol[:, 0:1], d["rec_lnw"].rearrange("(p a) -> p a", a=1))
            sp.wait_ge(loaded, n[0])
            barrier(sp, PH_CAUSAL1 + 2)
            barrier(sp, PH_CAUSAL1 + 3)
            with sp.Fori(0, BATCHES) as b:
                sp.wait_ge(R.st_ready, 3 * b + 3 + START)
                sp.wait_ge(R.fg_ready, 2 * b + 2 + START)
                sp.dma_start(scr_k[b], stk).then_inc(R.st_out, 16)
                sp.dma_start(scr_v[b], stv).then_inc(R.st_out, 16)
                sp.dma_start(scr_q[b], stq[:, 0:SEEN]).then_inc(R.st_out, 16)
                sp.dma_start(scr_f[b], stf).then_inc(R.st_out, 16)
                sp.dma_start(scr_g[b], stg[0:HEADS, :]).then_inc(R.st_out, 16)
                sp.wait_ge(R.st_out, 80 * b + 80 + START)
                gate(sp)
            barrier(sp, PH_REC)
            for dst, src in ((KD, scr_k), (FD, scr_f), (VD, scr_v), (QD, scr_q)):
                sp.dma_start(dst, src.rearrange("b (h k) t -> (b h) k t", k=HD)).then_inc(R.scan_in, 16)
            sp.dma_start(G1, scr_g.rearrange("b h t -> (b h) t")).then_inc(R.scan_in, 16)
            sp.wait_ge(R.od_ready, 1)
            sp.dma_start(scr_o.rearrange("b (h k) t -> (b h) k t", k=HD), OD).then_inc(R.o_out, 16)
            sp.wait_ge(R.o_out, 16)
            sp.dma_start(OF, scr_o.rearrange("b p t -> p b t")).then_inc(R.of_in, 16)
            sp.wait_ge(R.of_in, 16)
            barrier(sp, PH_REC + 1)
            barrier(sp, PH_REC + 2)
            load(aw[:], d["attn_w"][LAYERS])
            sp.wait_ge(loaded, n[0])
            for k in range(4):
                barrier(sp, PH_CAUSAL2 + k)
            sp.dma_start(out.rearrange("b (i p) f -> p (b i) f", p=P), X[:]).then_inc(stored, 16)
            sp.wait_ge(stored, 16)

        @block.gpsimd
        def _(pool):
            chain = Chain(pool, g_chain)
            norms = Tally()

            pool.memset(ident[:], 0.0).then_inc(const_ready, 1)
            pool.memset(identb[:], 0.0).then_inc(const_ready, 1)
            pool.memset(mask_win[:], 0.0).then_inc(const_ready, 1)
            pool.memset(mask_win0[:, :, 0:P - 1], BIG).then_inc(const_ready, 1)
            pool.memset(mask_win0[:, :, P - 1:], 0.0).then_inc(const_ready, 1)
            pool.memset(mask_diag[:], 0.0).then_inc(const_ready, 1)
            pool.memset(zero[:], 0.0).then_inc(const_ready, 1)

            def constant_parts():
                for k in Ke:
                    pool.memset(k, 0.0).then_inc(const_ready, 1)
                for v in Vx:
                    pool.memset(v[:, :, :, HD:], 1.0).then_inc(const_ready, 1)

            constant_parts()
            pool.wait_ge(const_ready, 11)
            for m in (ident, identb):
                pool.affine_select(out=m[:], in_=m[:], compare_op=ALU.not_equal, fill=1.0, base=0,
                                   pattern=[[-1, P]], channel_multiplier=1).then_inc(const_ready, 1)
            m = mask_win[:, :, 0:P]
            pool.affine_select(out=m, in_=m, compare_op=ALU.is_ge, fill=BIG, base=PAST - P,
                               pattern=[[0, 2], [1, P]], channel_multiplier=-1).then_inc(const_ready, 1)
            m = mask_win0[:, :, P - 1:P]
            pool.affine_select(out=m, in_=m, compare_op=ALU.is_ge, fill=BIG, base=PAST - 1,
                               pattern=[[0, 2], [0, 1]], channel_multiplier=-1).then_inc(const_ready, 1)
            for m in (mask_win[:, :, P:], mask_win0[:, :, P:]):
                pool.affine_select(out=m, in_=m, compare_op=ALU.is_ge, fill=BIG, base=0,
                                   pattern=[[0, 2], [-1, P]], channel_multiplier=1).then_inc(const_ready, 1)
            pool.affine_select(out=mask_diag[:], in_=mask_diag[:], compare_op=ALU.is_ge, fill=BIG, base=0,
                               pattern=[[-1, P]], channel_multiplier=1).then_inc(const_ready, 1)
            pool.wait_ge(const_ready, 18)
            gate(pool)

            def rsqrt(n):
                pool.wait_ge(var_ready, norms.value() + 1)
                gate(pool)
                w, t, y = nv[:, 0:n], nt[:, 0:n], rstd[:, 0:n]
                chain.add(pool.tensor_scalar(w, mv[:, 0:n, 1], EPS, None, ALU.add))
                chain.join()
                gate(pool)
                chain.add(pool.tensor_scalar(y.bitcast(I32), w.bitcast(I32), -0.5, MAGIC, ALU.mult, ALU.add))
                for k in range(3):
                    chain.join()
                    chain.link(pool.tensor_tensor(t, y, y, ALU.mult))
                    chain.add(pool.tensor_tensor(t, t, w, ALU.mult))
                    chain.join()
                    gate(pool)
                    chain.link(pool.tensor_scalar(t, t, -0.5, 1.5, ALU.mult, ALU.add))
                    if k < 2:
                        chain.add(pool.tensor_tensor(y, y, t, ALU.mult))
                    else:
                        pool.tensor_tensor(y, y, t, ALU.mult).then_inc(rstd_ready, 1)
                norms.n += 1

            def attention(S, u0, name):
                with counted_loop(pool, name, BATCHES // 2, (chain, norms)) as it:
                    u = u0 + 2 * it
                    for p in range(2):
                        pool.wait_ge(S.wo_ev, u + START)
                        gate(pool)
                        pool.tensor_copy(zs[p], tiles(S.src, 2 * it + p)).then_inc(S.zs_ready, 1)
                    if S is win:
                        for p in range(2):
                            rsqrt(TPB)

            def expert_main(S, v0, name):
                with counted_loop(pool, name, BATCHES // 2, (chain, norms)) as it:
                    for p in range(2):
                        pool.wait_ge(S.acc_done, (v0 + 2 * it) * S.experts + START)
                        gate(pool)
                        pool.tensor_copy(zs[p], tiles(S.src, 2 * it + p)).then_inc(S.x_ready, 1)
                    if S is ffn:
                        for p in range(2):
                            rsqrt(TPB)

            def expert_pre(v0):
                rsqrt(TILES)
                with pool.Fori(0, BATCHES) as b:
                    pool.wait_ge(lg_ev, v0 + b + START)
                    pool.wait_ge(h_ready, v0 + b + 1)
                    gate(pool)
                    pool.tensor_copy(zs[0], tiles(H, b)).then_inc(moe.x_ready, 1)

            for S in (win, cau):
                for s in (S.wo_ev, S.norm_done, S.evac_act, S.evac_dve):
                    pool.sem_inc(s, START)
            for S in (ffn, moe):
                for s in (S.T_ev, S.gelu_done, S.acc_done):
                    pool.sem_inc(s, START)
            for s in (lg_ev, R.T_done, R.st_ready, R.fg_ready, R.st_out):
                pool.sem_inc(s, START)
            barrier(pool, PH_SETUP)
            expert_pre(0)
            barrier(pool, PH_MOE1)
            expert_main(moe, 0, "pool moe")
            barrier(pool, PH_MOE1 + 1)
            rsqrt(TILES)
            rsqrt(TILES)
            barrier(pool, PH_INIT)
            with counted_loop(pool, "pool layer", LAYERS, (chain, norms)) as l:
                attention(win, l * BATCHES, "pool window")
                barrier(pool, PH_LAYER + 2 * l)
                expert_main(ffn, l * BATCHES, "pool ffn")
                barrier(pool, PH_LAYER + 2 * l + 1)
            expert_pre(BATCHES)
            barrier(pool, PH_MOE2)
            expert_main(moe, BATCHES, "pool moe")
            barrier(pool, PH_MOE2 + 1)

            def causal_block(use, ph):
                rsqrt(TILES)
                rsqrt(TILES)
                barrier(pool, ph)
                attention(cau, use * BATCHES, "pool causal")
                barrier(pool, ph + 1)
                expert_pre((2 + use) * BATCHES)
                barrier(pool, ph + 2)
                expert_main(moe, (2 + use) * BATCHES, "pool moe")
                barrier(pool, ph + 3)

            causal_block(0, PH_CAUSAL1)
            rsqrt(TILES)
            with pool.Fori(0, BATCHES) as b:
                pool.wait_ge(R.T_done, b + START)
                pool.wait_ge(R.h_ready, 1)
                gate(pool)
                pool.tensor_copy(zs[0], tiles(H, b)).then_inc(R.x_ready, 1)
            barrier(pool, PH_REC)
            half = STEP_RING // 2
            pool.wait_ge(R.scan_in, 80)
            pool.wait_ge(R.step, 1)
            gate(pool)
            with pool.Fori(0, TOKENS // STEP_RING) as it:
                for c in range(2):
                    pool.wait_ge(R.step, STEP_RING * it + half * c + 1)
                    gate(pool)
                    t0 = STEP_RING * it + half * c
                    slot = MM[:, half * c:half * (c + 1), :, 0].rearrange("p s (v k) -> p s v k", k=HD)
                    vv = VD[:, :, bass.ds(t0, half)].rearrange("p v t -> p t v").unsqueeze(3)\
                        .broadcast_to([P, half, HD, HD])
                    kk = KW[:, bass.ds(t0, half), 0, :].unsqueeze(2).broadcast_to([P, half, HD, HD])
                    pool.tensor_tensor(slot, vv, kk, ALU.mult).then_inc(R.kv_ready, 1)
            barrier(pool, PH_REC + 1)
            barrier(pool, PH_REC + 2)
            constant_parts()
            causal_block(1, PH_CAUSAL2)

        @block.tensor
        def _(pe):
            def turn_rows(bank, rows, done):
                for i in range(TPB):
                    m = pe.transpose(ps[:, bank, i * P:(i + 1) * P], rows[:, i, :], ident[:])
                m.then_inc(done, 1)

            def attention(S, u0):
                G = len(S.groups)
                with pe.Fori(0, BATCHES // 2) as it:
                    u = [u0 + 2 * it, u0 + 2 * it + 1]

                    def prep_turn(p):
                        pe.wait_ge(S.zs_ready, u[p] + 1)
                        if p:
                            pe.wait_ge(S.v_ev, u[0] + 1)
                        else:
                            pe.wait_ge(S.wo_ev, u[0] + START)
                        turn_rows(7, zs[p], S.zT_done)

                    def prep_queries(p):
                        pe.wait_ge(S.zT_ev, u[p] + 1)
                        pe.matmul(ps[:, 7, :], aw[:, 0, :], zT[p], start=True, stop=True).then_inc(S.q_done, 1)

                    def prep_keys(p):
                        pe.wait_ge(S.q_ev, u[p] + 1)
                        pe.matmul(ps[:, 7, :], aw[:, 1, :], zT[p], start=True, stop=True).then_inc(S.k_done, 1)

                    def prep_values(p):
                        pe.wait_ge(S.k_ev, u[p] + 1)
                        for i in range(TPB):
                            m = pe.matmul(ps[:, 7, i * P:(i + 1) * P], zT[p][:, i * P:(i + 1) * P],
                                          aw[:, 2, :], start=(i == 0), stop=(i == TPB - 1),
                                          skip_group_check=True)
                        m.then_inc(S.v_done, 1)

                    def post_turn(p):
                        pe.wait_ge(S.norm_done, (u[p] + 1) * TPB + START)
                        if p:
                            pe.wait_ge(S.wo_ev, u[0] + 1 + START)
                        else:
                            pe.wait_ge(S.v_ev, u[1] + 1)
                        turn_rows(7, On[p], S.oT_done)

                    def post_project(p):
                        pe.wait_ge(S.oT_ev, u[p] + 1)
                        for i in range(TPB):
                            m = pe.matmul(ps[:, 7, i * P:(i + 1) * P], OT[:, i, :], aw[:, 3, :],
                                          start=(i == 0), stop=(i == TPB - 1), skip_group_check=True)
                        m.then_inc(S.wo_done, 1)

                    def scores(p, k, g):
                        gr = S.groups[k]
                        kw = P * len(gr.blocks)
                        k0 = P * gr.blocks[0]
                        q0 = P * gr.tile
                        pe.wait_ge(S.exp_done, (u[p] * G + k) * 4 + g + 1)
                        if gr.windowed:
                            mask = mask_win0 if gr.first else mask_win
                            pe.matmul(ps[:, g, :], identb[:], mask[:].rearrange("p a b -> p (a b)"),
                                      start=True, stop=False, skip_group_check=True)
                        for j, h in enumerate(gr.heads[g]):
                            m = pe.matmul(ps[:, g, j * kw:(j + 1) * kw], Qe[p][:, h % 4, q0:q0 + P],
                                          Ke[p][:, g, k0:k0 + kw], start=not gr.windowed,
                                          stop=gr.windowed, skip_group_check=True)
                        if not gr.windowed:
                            m = pe.matmul(ps[:, g, kw - P:kw], identb[:], mask_diag[:], start=False, stop=True,
                                          skip_group_check=True)
                        m.then_inc(S.scores_done, 1)

                    def turn_probs(p, k, g):
                        gr = S.groups[k]
                        n = (u[p] * G + k) * 4 + g
                        half = (u[p] * G + k) * 2 + g // 2
                        pe.wait_ge(S.exp_done, n + 5)
                        pe.wait_ge(S.evac_dve if g % 2 else S.evac_act, half + START)
                        nb = len(gr.heads[g]) * len(gr.blocks)
                        for c in range(nb):
                            m = pe.transpose(ps[:, 4 + g % 2, c * P:(c + 1) * P],
                                             Pr[:, 4 * (k % 2) + g, c * P:(c + 1) * P], ident[:])
                        m.then_inc(S.t_done, 1)

                    def values(p, k, g):
                        gr = S.groups[k]
                        tile = u[p] * TPB + gr.tile
                        half = (u[p] * G + k) * 2 + g // 2
                        pe.wait_ge(S.evac_dve if g % 2 else S.evac_act, half + 1 + START)
                        first = g == 0 and (k == 0 or S.groups[k - 1].tile != gr.tile)
                        if first:
                            pe.wait_ge(S.norm_done, tile + START)
                        for j, h in enumerate(gr.heads[g]):
                            for c, blk in enumerate(gr.blocks):
                                cc = j * len(gr.blocks) + c
                                m = pe.matmul(ps[:, 6, h * (HD + 1):(h + 1) * (HD + 1)],
                                              PT[:, g, cc * P:(cc + 1) * P], Vx[p][:, blk, h, :],
                                              start=first and cc == 0, stop=True, skip_group_check=True)
                        if gr.last_of_tile and g == 3:
                            m.then_inc(S.av_done, 1)

                    units = S.units
                    n = len(units) // 2
                    hooks = {4: lambda: prep_turn(1), 8: lambda: prep_queries(1), 12: lambda: prep_keys(1),
                             16: lambda: prep_values(1), n + 8: lambda: post_turn(0),
                             n + 12: lambda: post_project(0)}
                    prep_turn(0)
                    prep_queries(0)
                    prep_keys(0)
                    prep_values(0)
                    for s in range(2 * n + TURN_LAG + 1):
                        if s in hooks:
                            hooks[s]()
                        if s in (0, n):
                            pe.wait_ge(S.v_ev, u[s // n] + 1)
                            pe.wait_ge(S.pad_done, 2 * u[s // n] + 2)
                        if s < 2 * n:
                            scores(*units[s])
                        if 0 <= s - TURN_LAG < 2 * n:
                            turn_probs(*units[s - TURN_LAG])
                        if s > TURN_LAG:
                            values(*units[s - TURN_LAG - 1])
                    post_turn(1)
                    post_project(1)

            def expert_main(S, v0, W1, W2):
                E = S.experts
                with pe.Fori(0, BATCHES // 2) as it:
                    v = [v0 + 2 * it, v0 + 2 * it + 1]

                    def turn(p):
                        pe.wait_ge(S.x_ready, v[p] + 1 + S.pre_turns)
                        pe.wait_ge(S.T_ev, v[p] + START)
                        turn_rows(5, zs[p], S.T_done)

                    def up(p, e, c):
                        n = (v[p] * E + e) * CHUNKS + c
                        if e == 0 and c == 0:
                            pe.wait_ge(S.T_ev, v[p] + 1 + START)
                        pe.wait_ge(S.gelu_done, n + START)
                        pe.matmul(ps[:, c % 2, :], W1(e)[:, c * P:(c + 1) * P], zT[p], start=True, stop=True)\
                            .then_inc(S.up_done, 1)

                    def down(p, e, c):
                        n = (v[p] * E + e) * CHUNKS + c
                        pe.wait_ge(S.gelu_done, n + 2 + START)
                        if c == 0:
                            pe.wait_ge(S.acc_done, v[p] * E + e + START)
                        for i in range(TPB):
                            m = pe.matmul(ps[:, 2 + (p * E + e) % 2, i * P:(i + 1) * P],
                                          hid[c % 2][:, i * P:(i + 1) * P], W2(e)[:, c, :],
                                          start=(c == 0 and i == 0), stop=(c == CHUNKS - 1),
                                          skip_group_check=True)
                        if c == CHUNKS - 1:
                            m.then_inc(S.y_done, 1)

                    turn(0)
                    order = [(p, e, c) for p in range(2) for e in range(E) for c in range(CHUNKS)]
                    for s, (p, e, c) in enumerate(order):
                        up(p, e, c)
                        if s == 1:
                            turn(1)
                        if s:
                            down(*order[s - 1])
                    down(*order[-1])

            def expert_pre(v0):
                with pe.Fori(0, BATCHES) as b:
                    pe.wait_ge(moe.x_ready, 2 * v0 + b + 1)
                    turn_rows(5, zs[0], pT_done)
                    pe.wait_ge(pT_ev, v0 + b + 1)
                    for i in range(TPB):
                        m = pe.matmul(ps[:, 6, i * EXPERTS:(i + 1) * EXPERTS], zT[0][:, i * P:(i + 1) * P],
                                      gate_w[:], start=(i == 0), stop=(i == TPB - 1), skip_group_check=True)
                    m.then_inc(lg_done, 1)
                    pe.wait_ge(lg_ev, v0 + b + 1 + START)
                    gate(pe)
                pe.wait_ge(c_ready, v0 // BATCHES + 1)
                for b in range(BATCHES):
                    for i in range(TPB):
                        m = pe.transpose(ps[0:EXPERTS, b % 2, i * P:(i + 1) * P], C[:, TPB * b + i, :], ident[:])
                    m.then_inc(cT_done, 1)
                    pe.wait_ge(cT_ev, v0 + b + 1)
                    if b >= 2:
                        pe.wait_ge(yb_ev, v0 + b - 1)
                    for i in range(TPB):
                        m = pe.matmul(ps[:, 2 + b % 2, i * P:(i + 1) * P],
                                      zT[b % 2][0:EXPERTS, i * P:(i + 1) * P], eb2[:],
                                      start=(i == 0), stop=(i == TPB - 1), skip_group_check=True)
                    m.then_inc(yb_done, 1)

            E1, E2 = (lambda e: w1[:, e, :]), (lambda e: w2[:, e])
            pe.wait_ge(const_ready, 16)
            barrier(pe, PH_SETUP)
            expert_pre(0)
            barrier(pe, PH_MOE1)
            moe.pre_turns = BATCHES
            expert_main(moe, 0, E1, E2)
            barrier(pe, PH_MOE1 + 1)
            barrier(pe, PH_INIT)
            ffn.pre_turns = 0
            with pe.Fori(0, LAYERS) as l:
                attention(win, l * BATCHES)
                barrier(pe, PH_LAYER + 2 * l)
                expert_main(ffn, l * BATCHES, lambda e: fw1[:], lambda e: fw2[:])
                barrier(pe, PH_LAYER + 2 * l + 1)
            expert_pre(BATCHES)
            barrier(pe, PH_MOE2)
            moe.pre_turns = 2 * BATCHES
            expert_main(moe, BATCHES, E1, E2)
            barrier(pe, PH_MOE2 + 1)

            def causal_block(use, ph):
                barrier(pe, ph)
                attention(cau, use * BATCHES)
                barrier(pe, ph + 1)
                expert_pre((2 + use) * BATCHES)
                barrier(pe, ph + 2)
                moe.pre_turns = (3 + use) * BATCHES
                expert_main(moe, (2 + use) * BATCHES, E1, E2)
                barrier(pe, ph + 3)

            causal_block(0, PH_CAUSAL1)
            with pe.Fori(0, BATCHES) as b:
                pe.wait_ge(R.x_ready, b + 1)
                turn_rows(5, zs[0], R.T_done)
                pe.wait_ge(R.T_ev, b + 1)
                pe.wait_ge(R.st_ready, 3 * b + START)
                pe.wait_ge(R.fg_ready, 2 * b + START)
                pe.matmul(ps[:, 0, :], aw[:, 1, :], zT[0], start=True, stop=True).then_inc(R.kvqg_done, 1)
                pe.matmul(ps[:, 1, :], aw[:, 2, :], zT[0], start=True, stop=True).then_inc(R.kvqg_done, 1)
                pe.matmul(ps[:, 2, 0:SEEN], aw[:, 0, :], zT[0][:, TOKENS - SEEN:], start=True, stop=True)\
                    .then_inc(R.kvqg_done, 1)
                pe.matmul(ps[0:8, 3, :], fw1[:, 0:8], zT[0], start=True, stop=True).then_inc(R.kvqg_done, 1)
                pe.matmul(ps[0:8, 4, 0:OUT], fw1[:, 8:16], zT[0][:, 1::3], start=True, stop=True)\
                    .then_inc(R.kvqg_done, 1)
                pe.matmul(ps[0:HEADS, 6, :], fw1[:, 16:32], zT[0], start=True, stop=True).then_inc(R.kvqg_done, 1)
                pe.wait_ge(R.f1_ev, b + 1)
                pe.matmul(ps[:, 3, :], fw2[0:8, 0, :], f1s[0:8, :], start=True, stop=True).then_inc(R.f_done, 1)
                pe.wait_ge(R.g1_ev, b + 1)
                pe.matmul(ps[:, 7, 0:OUT], fw2[0:8, 1, :], g1s[0:8, 0:OUT], start=True, stop=True)\
                    .then_inc(R.gate_done, 1)
            barrier(pe, PH_REC)
            barrier(pe, PH_REC + 1)
            for src, ready, done, bank in ((O1, R.o1_ready, R.mean_done, 0), (O3, R.sq_ready, R.msq_done, 4)):
                pe.wait_ge(ready, 1)
                for k in range(4):
                    m = pe.matmul(ps[:, bank + k, 0:2 * OUT], ones[:], src[:, 2 * k:2 * k + 2, :]
                                  .rearrange("p a b -> p (a b)"), start=True, stop=True)
                m.then_inc(done, 1)
            pe.wait_ge(R.ex_ready, 1)
            for b in range(BATCHES):
                if b >= 2:
                    pe.wait_ge(R.x_done, b - 1)
                for i in range(TPB):
                    m = pe.matmul(ps[:, b % 2, i * P:(i + 1) * P], EX[:, b, i * P:(i + 1) * P], aw[:, 3, :],
                                  start=(i == 0), stop=(i == TPB - 1), skip_group_check=True)
                m.then_inc(R.y_done, 1)
            barrier(pe, PH_REC + 2)
            causal_block(1, PH_CAUSAL2)

        @block.scalar
        def _(act):
            chain = Chain(act, a_chain)
            copy, exp, gelu, sigmoid = ACT.Copy, ACT.Exp, ACT.Gelu, ACT.Sigmoid
            act.sem_inc(win.exp_done, 4)
            act.sem_inc(cau.exp_done, 4)
            act.sem_inc(ffn.gelu_done, 1)
            act.sem_inc(moe.gelu_done, 1)

            def attention(S, u0):
                G = len(S.groups)
                with act.Fori(0, BATCHES // 2) as it:
                    u = [u0 + 2 * it, u0 + 2 * it + 1]

                    def prep_turn(p):
                        act.wait_ge(S.zT_done, u[p] + 1)
                        act.activation(zT[p], ps[:, 7, :], copy).then_inc(S.zT_ev, 1)

                    def prep_keys(p):
                        act.wait_ge(S.k_done, u[p] + 1)
                        for g in range(4):
                            rows = slice(32 * g, 32 * g + 32)
                            m = act.activation(Ke[p][rows, g, P:], ps[rows, 7, :], ACT.Identity,
                                               bias=acol[rows, 1:2])
                        m.then_inc(S.k_ev, 1)
                        for g in range(4):
                            rows = slice(32 * g, 32 * g + 32)
                            m = act.activation(Ke[p][rows, g, 0:P], zero[rows, :], ACT.Identity,
                                               bias=acol[rows, 1:2])
                        m.then_inc(S.pad_done, 1)

                    def post_turn(p):
                        act.wait_ge(S.oT_done, u[p] + 1)
                        act.activation(OT.rearrange("p a b -> p (a b)"), ps[:, 7, :], copy).then_inc(S.oT_ev, 1)

                    def probs(p, k, g):
                        gr = S.groups[k]
                        n = (u[p] * G + k) * 4 + g
                        kw = P * len(gr.blocks)
                        act.wait_ge(S.max_done, n + 1)
                        slot = 4 * (k % 2) + g
                        for j in range(len(gr.heads[g])):
                            m = act.activation(Pr[:, slot, j * kw:(j + 1) * kw], ps[:, g, j * kw:(j + 1) * kw],
                                               exp, bias=nmax[:, slot, j:j + 1], scale=-1.0)
                        m.then_inc(S.exp_done, 1)

                    def evac(p, k, g):
                        gr = S.groups[k]
                        act.wait_ge(S.t_done, (u[p] * G + k) * 4 + g + 1)
                        w = P * len(gr.blocks) * len(gr.heads[g])
                        act.activation(PT[:, g, 0:w], ps[:, 4 + g % 2, 0:w], copy).then_inc(S.evac_act, 1)

                    units = S.units
                    n = len(units) // 2
                    hooks = {4: lambda: prep_turn(1), 12: lambda: prep_keys(1), n + 8: lambda: post_turn(0)}
                    prep_turn(0)
                    prep_keys(0)
                    for s in range(2 * n + TURN_LAG):
                        if s in hooks:
                            hooks[s]()
                        if s >= TURN_LAG and units[s - TURN_LAG][2] % 2 == 0:
                            evac(*units[s - TURN_LAG])
                        if s < 2 * n:
                            probs(*units[s])
                    post_turn(1)

            def expert_main(S, v0, b1):
                E = S.experts
                with act.Fori(0, BATCHES // 2) as it:
                    v = [v0 + 2 * it, v0 + 2 * it + 1]

                    def turn(p):
                        act.wait_ge(S.T_done, v[p] + 1)
                        act.activation(zT[p], ps[:, 5, :], copy).then_inc(S.T_ev, 1)

                    turn(0)
                    for p in range(2):
                        for e in range(E):
                            for c in range(CHUNKS):
                                act.wait_ge(S.up_done, (v[p] * E + e) * CHUNKS + c + 1)
                                act.activation(hid[c % 2], ps[:, c % 2, :], gelu, bias=b1(e)[:, c:c + 1])\
                                    .then_inc(S.gelu_done, 1)
                                if (p, e, c) == (0, 0, 1):
                                    turn(1)

            def expert_pre(v0):
                with act.Fori(0, BATCHES) as b:
                    act.wait_ge(pT_done, v0 + b + 1)
                    act.activation(zT[0], ps[:, 5, :], copy).then_inc(pT_ev, 1)
                act.wait_ge(d_ready, v0 // BATCHES + 1)
                act.activation(rt[1][:], rt[0][:], exp).then_inc(e_ready, 1)
                for b in range(BATCHES):
                    act.wait_ge(cT_done, v0 + b + 1)
                    act.activation(zT[b % 2][0:EXPERTS, :], ps[0:EXPERTS, b % 2, :], copy).then_inc(cT_ev, 1)

            B1 = lambda e: eb1[:, e, :]
            barrier(act, PH_SETUP)
            expert_pre(0)
            barrier(act, PH_MOE1)
            expert_main(moe, 0, B1)
            barrier(act, PH_MOE1 + 1)
            barrier(act, PH_INIT)
            with act.Fori(0, LAYERS) as l:
                attention(win, l * BATCHES)
                barrier(act, PH_LAYER + 2 * l)
                expert_main(ffn, l * BATCHES, lambda e: fcol[:])
                barrier(act, PH_LAYER + 2 * l + 1)
            expert_pre(BATCHES)
            barrier(act, PH_MOE2)
            expert_main(moe, BATCHES, B1)
            barrier(act, PH_MOE2 + 1)

            def causal_block(use, ph):
                barrier(act, ph)
                attention(cau, use * BATCHES)
                barrier(act, ph + 1)
                expert_pre((2 + use) * BATCHES)
                barrier(act, ph + 2)
                expert_main(moe, (2 + use) * BATCHES, B1)
                barrier(act, ph + 3)

            causal_block(0, PH_CAUSAL1)
            with act.Fori(0, BATCHES) as b:
                act.wait_ge(R.T_done, b + 1 + START)
                act.activation(zT[0], ps[:, 5, :], copy).then_inc(R.T_ev, 1)
                act.wait_ge(R.kvqg_done, 6 * b + 5)
                act.wait_ge(R.st_out, 80 * b + START)
                act.activation(f1s[0:8, :], ps[0:8, 3, :], copy).then_inc(R.f1_ev, 1)
                act.activation(g1s[0:8, 0:OUT], ps[0:8, 4, 0:OUT], copy).then_inc(R.g1_ev, 1)
                for s, bank, w in ((sgk, 0, TOKENS), (sgv, 1, TOKENS), (sgq, 2, SEEN)):
                    act.activation(s[:, 0:w], ps[:, bank, 0:w], sigmoid).then_inc(R.sg_ready, 1)
                act.wait_ge(R.kvqg_done, 6 * b + 6)
                act.activation(stg[0:HEADS, :], ps[0:HEADS, 6, :], sigmoid).then_inc(R.fg_ready, 1)
                act.wait_ge(R.gate_done, b + 1)
                gate(act)
                act.activation(GATE[:, b, :], ps[:, 7, 0:OUT], sigmoid).then_inc(R.psum_free, 1)
                act.wait_ge(R.f_done, b + 1)
                act.activation(stf, ps[:, 3, :], sigmoid).then_inc(R.fg_ready, 1)
            barrier(act, PH_REC)
            barrier(act, PH_REC + 1)
            barrier(act, PH_REC + 2)
            causal_block(1, PH_CAUSAL2)

        @block.vector
        def _(dve):
            chain = Chain(dve, v_chain)
            norms = Tally()
            for S in (ffn, moe):
                dve.sem_inc(S.acc_done, 1)

            def norm_stats(get, n):
                gate(dve)
                for t in range(n):
                    chain.add(dve.bn_stats(stats[:, t, :], get(t)))
                chain.join()
                gate(dve)
                for t in range(n):
                    m = dve.bn_aggr(mv[:, t, :], stats[:, t, :])
                m.then_inc(var_ready, 1)
                dve.wait_ge(rstd_ready, norms.value() + 1)
                gate(dve)
                norms.n += 1

            def norm_apply(dst, get, n):
                for t in range(n):
                    chain.add(dve.tensor_scalar(dst(t), get(t), mv[:, t, 0:1], rstd[:, t:t + 1],
                                                ALU.subtract, ALU.mult))
                chain.join()

            def affine(dst, src, g, b):
                chain.link(dve.tensor_tensor(dst, src, row(g), ALU.mult))
                return dve.tensor_tensor(dst, dst, row(b), ALU.add)

            def norm_all(src, dst):
                norm_stats(lambda t: src[:, t, :], TILES)
                norm_apply(lambda t: dst[:, t, :], lambda t: src[:, t, :], TILES)

            def attention(S, u0, name):
                G = len(S.groups)
                with counted_loop(dve, name, BATCHES // 2, (chain, norms)) as it:
                    u = [u0 + 2 * it, u0 + 2 * it + 1]

                    def prep_queries(p):
                        dve.wait_ge(S.q_done, u[p] + 1)
                        for j in range(4):
                            m = dve.tensor_scalar(Qe[p][:, j, :], ps[:, 7, :], acol[:, 0:1], hm[:, j:j + 1],
                                                  ALU.add, ALU.mult)
                        m.then_inc(S.q_ev, 1)

                    def prep_values(p):
                        bv = arow[:, 0, :].rearrange("p (h k) -> p h k", k=HD)
                        dve.tensor_tensor(Vx[p][:, 0, :, 0:HD], bv,
                                          zero[:].rearrange("p (h k) -> p h k", k=HD), ALU.add).then_inc(S.pad_done, 1)
                        dve.wait_ge(S.v_done, u[p] + 1)
                        dve.tensor_tensor(Vx[p][:, 1:, :, 0:HD],
                                          ps[:, 7, :].rearrange("p (i h k) -> p i h k", h=HEADS, k=HD),
                                          bv.unsqueeze(1).broadcast_to([P, TPB, HEADS, HD]), ALU.add)\
                            .then_inc(S.v_ev, 1)

                    def post(p):
                        b = 2 * it + p
                        x = tiles(A, b)
                        dve.wait_ge(S.wo_done, u[p] + 1)
                        dve.tensor_tensor(x, ps[:, 7, :].rearrange("p (i k) -> p i k", k=P), x, ALU.add)\
                            .then_inc(S.wo_ev, 1)
                        dve.wait_ge(S.wo_ev, u[p] + 1 + START)
                        if S is cau:
                            dve.tensor_tensor(x, x, row(arow[:, 1, :]), ALU.add).then_inc(S.post_done, 1)
                            return
                        chain.link(dve.tensor_tensor(x, x, row(arow[:, 1, :]), ALU.add))
                        norm_stats(lambda t: A[:, b * TPB + t, :], TPB)
                        norm_apply(lambda t: A[:, b * TPB + t, :], lambda t: A[:, b * TPB + t, :], TPB)
                        affine(x, x, arow[:, 2, :], arow[:, 3, :]).then_inc(S.post_done, 1)

                    def maxima(p, k, g):
                        gr = S.groups[k]
                        kw = P * len(gr.blocks)
                        nh = len(gr.heads[g])
                        dve.wait_ge(S.scores_done, (u[p] * G + k) * 4 + g + 1)
                        dve.tensor_reduce(nmax[:, 4 * (k % 2) + g, 0:nh],
                                          ps[:, g, 0:nh * kw].rearrange("p (a b) -> p a b", b=kw),
                                          AX_X, ALU.min).then_inc(S.max_done, 1)

                    def evac(p, k, g):
                        gr = S.groups[k]
                        dve.wait_ge(S.t_done, (u[p] * G + k) * 4 + g + 1)
                        w = P * len(gr.blocks) * len(gr.heads[g])
                        dve.tensor_copy(PT[:, g, 0:w], ps[:, 4 + g % 2, 0:w]).then_inc(S.evac_dve, 1)

                    def normalise(p, i):
                        dve.wait_ge(S.av_done, u[p] * TPB + i + 1)
                        o = ps[:, 6, 0:HEADS * (HD + 1)].rearrange("p (h k) -> p h k", k=HD + 1)
                        chain.link(dve.reciprocal(orec[:], o[:, :, HD]))
                        dve.tensor_tensor(On[p][:, i, :].rearrange("p (h k) -> p h k", k=HD), o[:, :, 0:HD],
                                          orec[:].unsqueeze(2).broadcast_to([P, HEADS, HD]), ALU.mult)\
                            .then_inc(S.norm_done, 1)

                    units = S.units
                    n = len(units) // 2
                    hooks = {8: lambda: prep_queries(1), 16: lambda: prep_values(1), n + 12: lambda: post(0)}
                    prep_queries(0)
                    prep_values(0)
                    for s in range(2 * n + TURN_LAG + 2):
                        if s in hooks:
                            hooks[s]()
                        last = s - TURN_LAG - 2
                        if last >= 0 and units[last][2] == 3 and S.groups[units[last][1]].last_of_tile:
                            normalise(units[last][0], S.groups[units[last][1]].tile)
                        if s < 2 * n:
                            maxima(*units[s])
                        if 0 <= s - TURN_LAG < 2 * n and units[s - TURN_LAG][2] % 2:
                            evac(*units[s - TURN_LAG])
                    post(1)

            def feed_forward(v0):
                S = ffn
                with counted_loop(dve, "dve ffn", BATCHES // 2, (chain, norms)) as it:
                    for p in range(2):
                        b = 2 * it + p
                        x = tiles(A, b)
                        dve.wait_ge(S.y_done, v0 + b + 1)
                        dve.tensor_tensor(x, ps[:, 2 + p, :].rearrange("p (i k) -> p i k", k=P), x, ALU.add)\
                            .then_inc(S.acc_done, 1)
                        dve.wait_ge(S.acc_done, v0 + b + 2 + START)
                        chain.link(dve.tensor_tensor(x, x, row(frow[:, 0, :]), ALU.add))
                        norm_stats(lambda t: A[:, b * TPB + t, :], TPB)
                        norm_apply(lambda t: A[:, b * TPB + t, :], lambda t: A[:, b * TPB + t, :], TPB)
                        chain.link(affine(x, x, frow[:, 1, :], frow[:, 2, :]))

            def expert_main(v0):
                S = moe
                with dve.Fori(0, BATCHES // 2) as it:
                    for p in range(2):
                        for e in range(EXPERTS):
                            n = (v0 + 2 * it + p) * EXPERTS + e
                            dve.wait_ge(S.y_done, n + 1)
                            dve.wait_ge(S.acc_done, n + 1 + START)
                            gate(dve)
                            for i in range(TPB):
                                t = (2 * it + p) * TPB + i
                                m = dve.scalar_tensor_tensor(
                                    out=X[:, t, :], in0=ps[:, 2 + e % 2, i * P:(i + 1) * P],
                                    scalar=C[:, t, e:e + 1], in1=X[:, t, :], op0=ALU.mult, op1=ALU.add)
                            m.then_inc(S.acc_done, 1)

            def expert_pre(v0, first):
                use = v0 // BATCHES
                top1 = use < 2
                if not first:
                    chain.link(dve.scalar_tensor_tensor(out=X[:], in0=A, scalar=1.0 if top1 else 0.5, in1=X[:],
                                                        op0=ALU.mult, op1=ALU.add))
                src = X if top1 else A
                norm_stats(lambda t: src[:, t, :], TILES)
                norm_apply(lambda t: H[:, t, :], lambda t: src[:, t, :], TILES)
                for b in range(BATCHES):
                    x = H[:, TPB * b:TPB * (b + 1), :]
                    if top1:
                        dve.engine_nop().then_inc(h_ready, 1)
                    else:
                        affine(x, x, crow[:, 2, :], crow[:, 3, :]).then_inc(h_ready, 1)
                with dve.Fori(0, BATCHES) as b:
                    dve.wait_ge(lg_done, v0 + b + 1)
                    gate(dve)
                    lg = ps[:, 6, 0:TPB * EXPERTS].rearrange("p (a b) -> p a b", b=EXPERTS)
                    if top1:
                        dve.tensor_copy(LG[:, bass.ts(b, TPB), :], lg).then_inc(lg_ev, 1)
                    else:
                        dve.tensor_tensor(LG[:, bass.ts(b, TPB), :], lg,
                                          brow[:].unsqueeze(1).broadcast_to([P, TPB, EXPERTS]), ALU.add)\
                            .then_inc(lg_ev, 1)
                dve.wait_ge(lg_ev, v0 + BATCHES + START)
                wide = lambda a: a[:].unsqueeze(2).broadcast_to([P, TILES, EXPERTS])
                chain.link(dve.tensor_reduce(r1[:], LG[:], AX_X, ALU.max))
                dve.tensor_tensor(rt[0][:], LG[:], wide(r1), ALU.subtract).then_inc(d_ready, 1)
                chain.link(dve.tensor_tensor(rt[2][:], LG[:], wide(r1), ALU.is_equal))
                chain.link(dve.tensor_tensor(rt[2][:], rt[2][:], rev[:].unsqueeze(1)
                                             .broadcast_to([P, TILES, EXPERTS]), ALU.mult))
                chain.link(dve.tensor_reduce(r2[:], rt[2][:], AX_X, ALU.max))
                chain.link(dve.tensor_tensor(rt[3][:], rt[2][:], wide(r2), ALU.is_equal))
                dve.wait_ge(e_ready, use + 1)
                if top1:
                    chain.link(dve.tensor_reduce(r1[:], rt[1][:], AX_X, ALU.add))
                    chain.link(dve.reciprocal(r2[:], r1[:]))
                else:
                    chain.link(dve.scalar_tensor_tensor(out=rt[2][:], in0=rt[3][:], scalar=-BIG, in1=LG[:],
                                                        op0=ALU.mult, op1=ALU.add))
                    chain.link(dve.tensor_reduce(r2[:], rt[2][:], AX_X, ALU.max))
                    chain.link(dve.tensor_tensor(rt[2][:], LG[:], wide(r2), ALU.is_ge))
                    chain.link(dve.tensor_tensor(rt[3][:], rt[1][:], rt[2][:], ALU.mult))
                    chain.link(dve.tensor_reduce(r1[:], rt[3][:], AX_X, ALU.add))
                    chain.link(dve.reciprocal(r2[:], r1[:]))
                chain.link(dve.tensor_scalar(r1[:], r2[:], 0.5, None, ALU.mult))
                dve.tensor_tensor(C[:], rt[3][:], wide(r1), ALU.mult).then_inc(c_ready, 1)
                for b in range(BATCHES):
                    dve.wait_ge(yb_done, v0 + b + 1)
                    x = X[:, TPB * b:TPB * (b + 1), :]
                    dve.tensor_tensor(x, ps[:, 2 + b % 2, :].rearrange("p (i k) -> p i k", k=P), x, ALU.add)\
                        .then_inc(yb_ev, 1)

            dve.memset(ones[:], 1.0 / P).then_inc(v_chain, 1)
            chain.n += 1
            barrier(dve, PH_SETUP)
            expert_pre(0, True)
            barrier(dve, PH_MOE1)
            expert_main(0)
            barrier(dve, PH_MOE1 + 1)
            norm_all(X, A)
            norm_all(A, A)
            for b in range(BATCHES):
                x = A[:, TPB * b:TPB * (b + 1), :]
                chain.link(affine(x, x, crow[:, 0, :], crow[:, 1, :]))
                chain.link(dve.tensor_tensor(x, x, pos[:], ALU.add))
            barrier(dve, PH_INIT)
            with counted_loop(dve, "dve layer", LAYERS, (chain, norms)) as l:
                attention(win, l * BATCHES, "dve window")
                barrier(dve, PH_LAYER + 2 * l)
                feed_forward(l * BATCHES)
                barrier(dve, PH_LAYER + 2 * l + 1)
            expert_pre(BATCHES, False)
            barrier(dve, PH_MOE2)
            expert_main(BATCHES)
            barrier(dve, PH_MOE2 + 1)

            def causal_block(use, ph):
                norm_all(X, A)
                norm_stats(lambda t: A[:, t, :], TILES)
                norm_apply(lambda t: H[:, t, :], lambda t: A[:, t, :], TILES)
                for b in range(BATCHES):
                    x = H[:, TPB * b:TPB * (b + 1), :]
                    chain.link(affine(x, x, arow[:, 2, :], arow[:, 3, :]))
                barrier(dve, ph)
                attention(cau, use * BATCHES, "dve causal")
                barrier(dve, ph + 1)
                expert_pre((2 + use) * BATCHES, False)
                barrier(dve, ph + 2)
                expert_main((2 + use) * BATCHES)
                barrier(dve, ph + 3)

            causal_block(0, PH_CAUSAL1)
            norm_stats(lambda t: X[:, t, :], TILES)
            norm_apply(lambda t: H[:, t, :], lambda t: X[:, t, :], TILES)
            dve.engine_nop().then_inc(R.h_ready, 1)
            with dve.Fori(0, BATCHES) as b:
                dve.wait_ge(R.st_out, 80 * b + START)
                for n, (s, sg, bank, w) in enumerate(((stk, sgk, 0, TOKENS), (stv, sgv, 1, TOKENS),
                                                      (stq, sgq, 2, SEEN))):
                    dve.wait_ge(R.sg_ready, 3 * b + n + 1)
                    dve.tensor_tensor(s[:, 0:w], ps[:, bank, 0:w], sg[:, 0:w], ALU.mult).then_inc(R.st_ready, 1)
            barrier(dve, PH_REC)
            dve.wait_ge(R.scan_in, 80)
            gate(dve)
            by_time = lambda a: a.rearrange("p k t -> p t k")
            over_k = lambda a: a.unsqueeze(1).broadcast_to([P, HD, TOKENS])
            kn, wv, ua, av = KW[:, :, 0, :], KW[:, :, 1, :], UA[:, :, 0, :], UA[:, :, 1, :]
            chain.link(dve.tensor_tensor(TMP, KD, KD, ALU.mult))
            chain.link(dve.tensor_reduce(N2, by_time(TMP), AX_X, ALU.add))
            chain.link(dve.tensor_scalar(N2, N2, 1e-24, None, ALU.max))
            newton(dve, chain, RN, N2, T1)
            chain.link(dve.tensor_tensor(TMP, KD, over_k(RN), ALU.mult))
            chain.link(dve.tensor_copy(kn, by_time(TMP)))
            chain.link(dve.tensor_scalar(G1, G1, -1.0, None, ALU.mult))
            chain.link(dve.tensor_tensor(av, kn, G1.unsqueeze(2).broadcast_to([P, TOKENS, HD]), ALU.mult))
            chain.link(dve.tensor_tensor(wv, kn, by_time(FD), ALU.mult))
            chain.link(dve.tensor_tensor(ua, av, by_time(FD), ALU.mult))
            chain.link(dve.tensor_tensor(by_time(TMP), kn, ua, ALU.mult))
            chain.link(dve.tensor_reduce(C1, by_time(TMP), AX_X, ALU.add))
            chain.link(dve.tensor_tensor(by_time(TMP), av, C1.unsqueeze(2).broadcast_to([P, TOKENS, HD]), ALU.mult))
            chain.link(dve.tensor_tensor(ua, ua, by_time(TMP), ALU.add))
            dve.memset(SH[:, STEP_RING - 1], 0.0).then_inc(R.step, 1)
            dve.wait_ge(R.step, 1)
            dve.sem_inc(R.step, STEP_RING // 2)
            last_turn = TOKENS // STEP_RING
            seen_turn = (TOKENS - SEEN) // STEP_RING
            for lo, hi, name in ((0, seen_turn, "scan"), (seen_turn, last_turn, "scan seen")):
                with counted_loop(dve, name, hi - lo, (chain,)) as i:
                    it = lo + i
                    for j in range(STEP_RING):
                        t = STEP_RING * it + j
                        s = SH[:, (j - 1) % STEP_RING]
                        new = SH[:, j]
                        mj = MM[:, j]
                        at_t = lambda a: a[:, bass.ds(t, 1), :, :].rearrange("p a b c -> p (a b) c")
                        if j % 4 == 0:
                            dve.wait_ge(R.kv_ready, 2 * it + j // 4 + 1)
                        chain.add(dve.tensor_tensor(
                            M1.rearrange("p (a v) k -> p a v k", a=2),
                            s.unsqueeze(1).broadcast_to([P, 2, HD, HD]),
                            at_t(KW).unsqueeze(2).broadcast_to([P, 2, HD, HD]), ALU.mult))
                        chain.add(dve.tensor_tensor(
                            mj[:, :, 1].rearrange("p (v k) -> p v k", k=HD), s,
                            FD[:, :, bass.ds(t, 1)].rearrange("p k a -> p (a k)").unsqueeze(1)
                            .broadcast_to([P, HD, HD]), ALU.mult))
                        dve.wait_ge(v_chain, chain.value() - 1)
                        chain.link(dve.tensor_reduce(XY.rearrange("p a b -> p (a b)"), M1, AX_X, ALU.add))
                        chain.link(dve.tensor_tensor(
                            mj[:, :, 2:4].rearrange("p (v k) r -> p r v k", k=HD),
                            at_t(UA).unsqueeze(2).broadcast_to([P, 2, HD, HD]),
                            XY.unsqueeze(3).broadcast_to([P, 2, HD, HD]), ALU.mult))
                        dve.tensor_reduce(new.rearrange("p v k -> p (v k)"), mj, AX_X, ALU.add).then_inc(R.step, 1)
                        dve.wait_ge(R.step, t + 2 + STEP_RING // 2)
                    if lo:
                        q = QD[:, :, bass.ds(STEP_RING * i, STEP_RING)].rearrange("p k t -> p t k").unsqueeze(2)\
                            .broadcast_to([P, STEP_RING, HD, HD])
                        chain.link(dve.tensor_tensor(OQ, SH, q, ALU.mult))
                        gate(dve)
                        chain.link(dve.tensor_reduce(
                            OD[:, :, bass.ds(STEP_RING * i, STEP_RING)].rearrange("p v t -> p t v"),
                            OQ, AX_X, ALU.add))
            dve.engine_nop().then_inc(R.od_ready, 1)
            barrier(dve, PH_REC + 1)
            half_banks = lambda b0: ps[:, b0:b0 + 4, 0:2 * OUT]
            quad = lambda a: a.rearrange("p (c a) b -> p c (a b)", a=2)
            dve.tensor_tensor(O1, OF[:, :, SEEN - OUT:], GATE, ALU.mult).then_inc(R.o1_ready, 1)
            chain.link(dve.memset(EX, 0.0))
            dve.wait_ge(R.o1_ready, 1)
            dve.wait_ge(R.mean_done, 1)
            chain.link(dve.tensor_tensor(quad(O2), quad(O1), half_banks(0), ALU.subtract))
            dve.tensor_tensor(O3, O2, O2, ALU.mult).then_inc(R.sq_ready, 1)
            dve.wait_ge(R.msq_done, 1)
            chain.link(dve.tensor_scalar(quad(O1), half_banks(4), EPS, None, ALU.add))
            flat = lambda a: a.rearrange("p a b -> p (a b)")
            newton(dve, chain, flat(O4), flat(O1), flat(O3))
            dve.scalar_tensor_tensor(out=EX[:, :, 1::3], in0=O2, scalar=fcol[:, 0:1], in1=O4,
                                     op0=ALU.mult, op1=ALU.mult).then_inc(R.ex_ready, 1)
            for b in range(BATCHES):
                dve.wait_ge(R.y_done, b + 1)
                x = X[:, TPB * b:TPB * (b + 1), :]
                dve.tensor_tensor(x, ps[:, b % 2, :].rearrange("p (i k) -> p i k", k=P), x, ALU.add)\
                    .then_inc(R.x_done, 1)
            barrier(dve, PH_REC + 2)
            causal_block(1, PH_CAUSAL2)

    if wrong:
        raise AssertionError(f"PER_TURN: {wrong}")


def newton(eng, chain, y, w, t):
    chain.link(eng.tensor_scalar(y.bitcast(I32), w.bitcast(I32), -0.5, MAGIC, ALU.mult, ALU.add))
    for _ in range(3):
        chain.link(eng.tensor_tensor(t, y, y, ALU.mult))
        chain.link(eng.tensor_tensor(t, t, w, ALU.mult))
        chain.link(eng.tensor_scalar(t, t, -0.5, 1.5, ALU.mult, ALU.add))
        chain.link(eng.tensor_tensor(y, y, t, ALU.mult))


def _lay_out(x):
    a = {k: np.asarray(v) for k, v in x.items()}
    d = {"x": a["L0_attn_x"]}
    wqkv = a["L0_attn_Wqkv"].reshape(LAYERS, 3, P, P).transpose(0, 3, 1, 2)
    wo = a["L0_attn_Wo"].transpose(0, 2, 1)[:, :, None, :]
    causal = np.stack([a["L1_ffn_" + n] for n in ("Wq", "Wk", "Wv", "Wo")], 1)[None]
    d["attn_w"] = np.concatenate([np.concatenate([wqkv, wo], 2), causal])
    bqkv = a["L0_attn_bqkv"].reshape(LAYERS, 3, P)
    row = np.stack([bqkv[:, 2], a["L0_attn_bo"], a["L0_attn_ln1_g"], a["L0_attn_ln1_b"]], 1)
    crow = np.stack([a["L1_ffn_" + n] for n in ("bv", "bo", "ln1_g", "ln1_b")])[None]
    d["attn_row"] = np.concatenate([row, crow])
    col = np.stack([bqkv[:, 0], bqkv[:, 1]], 2)
    ccol = np.stack([a["L1_ffn_bq"], a["L1_ffn_bk"]], 1)[None]
    d["attn_col"] = np.concatenate([col, ccol])
    d["ffn_w1"] = a["L0_attn_W1"].transpose(0, 2, 1)
    d["ffn_w2"] = a["L0_attn_W2"].transpose(0, 2, 1).reshape(LAYERS, CHUNKS, P, P).transpose(0, 2, 1, 3)
    d["ffn_row"] = np.stack([a["L0_attn_b2"], a["L0_attn_ln2_g"], a["L0_attn_ln2_b"]], 1)
    d["ffn_col"] = a["L0_attn_b1"].reshape(LAYERS, CHUNKS, P).transpose(0, 2, 1)
    d["crow"] = np.stack([a["L0_attn_norm_in_g"], a["L0_attn_norm_in_b"], a["L1_ffn_ln2_g"], a["L1_ffn_ln2_b"]])
    for n in ("w1", "w2", "b1", "b2"):
        d["L0_" + n], d["L1_" + n] = a["L0_ffn_" + n], a["L1_ffn_e_" + n]
    d["L0_gate"], d["L1_gate"], d["L1_br"] = a["L0_ffn_gate_w"], a["L1_ffn_Wr"], a["L1_ffn_br"]
    d["rec_w"] = np.stack([a["L1_attn_" + n] for n in ("Wq", "Wk", "Wv", "Wout")], 1)
    for n, m in (("f1", "Wf1"), ("f2", "Wf2"), ("o1", "Wo1"), ("o2", "Wo2"), ("g", "Wg"), ("lnw", "ln_w")):
        d["rec_" + n] = a["L1_attn_" + m]
    half = P // 2
    where = np.arange(TOKENS, dtype=np.float32)[:, None]
    turn = where / np.float32(10000.0) ** (np.arange(half, dtype=np.float32)[None] / np.float32(half - 1))
    d["pos"] = np.concatenate([np.cos(turn), np.sin(turn)], 1).astype(np.float32)
    own = (np.arange(P)[:, None] // HD) % 4 == np.arange(4)[None]
    d["hm"] = np.where(own, -1.0 / np.sqrt(HD), 0.0).astype(np.float32)
    d["rev"] = np.arange(EXPERTS, 0, -1).astype(np.float32)
    return {k: np.ascontiguousarray(v) for k, v in d.items()}


def kernel(**inputs):
    import concourse.bacc as _bacc
    from concourse.bass_utils import run_bass_kernel_spmd as _run

    nc = _bacc.Bacc("TRN2", target_bir_lowering=False, num_devices=1)
    arrays = {f"in_{k}_dram": v for k, v in _lay_out(inputs).items()}
    d = {k[3:-5]: nc.dram_tensor(k, v.shape, mybir.dt.from_np(v.dtype), kind="ExternalInput").ap()
         for k, v in arrays.items()}
    out = nc.dram_tensor("out_0_dram", (BATCHES, TOKENS, P), F32, kind="ExternalOutput").ap()
    build(nc, d, out)
    r = _run(nc, [arrays], core_ids=[0])
    return r.results[0]["out_0_dram"]
```

```python
from contextlib import ExitStack, contextmanager

import numpy as np

import concourse.bass as bass
from concourse import mybir

F32 = mybir.dt.float32
BF16 = mybir.dt.bfloat16
I32 = mybir.dt.int32
ALU = mybir.AluOpType
ACT = mybir.ActivationFunctionType
AX_X = mybir.AxisListType.X

P = 128
BATCHES, TOKENS = 8, 512
TPB = TOKENS // P
TILES = BATCHES * TPB
HEADS, HD = 16, 8
LAYERS = 6
HID = 512
CHUNKS = HID // P
EXPERTS = 8
PAST = 125
EPS = 1e-5
BIG = 1e30
NO_SCORE = 3e38
MAGIC = 1597463007.0
SEEN = 176
OUT = 171
TURN_LAG = 2
POST_TURN, POST_PROJECT = 5, 8
PREP_TURN, PREP_QUERIES, PREP_KEYS, PREP_VALUES = 12, 15, 19, 22
START = 1
STEP_RING = 8

PER_TURN = {'pool window': (26, 2), 'pool ffn': (26, 2), 'dve window': (30, 2), 'dve ffn': (22, 2), 'dve causal': (10, 0), 'scan': (32,), 'scan seen': (34,),
            'pool layer': (208, 16), 'dve layer': (208, 16)}


class Tally:

    def __init__(self):
        self.base, self.n = 0, 0

    def value(self):
        return self.base + self.n


class Chain(Tally):

    def __init__(self, eng, sem):
        super().__init__()
        self.eng, self.sem = eng, sem

    def add(self, ins):
        ins.then_inc(self.sem, 1)
        self.n += 1

    def join(self):
        self.eng.wait_ge(self.sem, self.value())

    def link(self, ins):
        self.add(ins)
        self.join()


def lagged(units, b, p, s, lag, first):
    i = s - lag
    if i >= len(units) or (i < 0 and first):
        return None
    return (b, p, *units[i]) if i >= 0 else (b - 1, 1 - p, *units[i])


wrong = {}


@contextmanager
def counted_loop(eng, name, count, tallies):
    per = PER_TURN.get(name, (0,) * len(tallies))
    before = [(t.base, t.n) for t in tallies]
    with eng.Fori(0, count) as i:
        for t, k in zip(tallies, per):
            t.base = t.base + i * k
        yield i
        got = tuple(t.n - n for t, (_, n) in zip(tallies, before))
        if got != tuple(per):
            wrong[name] = got
    for t, (base, n), k in zip(tallies, before, got):
        t.base, t.n = base, n + count * k


def run_batches(eng, name, tallies, stage):
    stage(0, 0, first=True)
    with counted_loop(eng, name, BATCHES // 2 - 1, tallies) as it:
        stage(2 * it + 1, 1)
        stage(2 * it + 2, 0)
    stage(BATCHES - 1, 1, last=True)


class Group:

    def __init__(self, tile, heads, blocks, windowed, last_of_tile):
        self.tile, self.heads, self.blocks = tile, heads, blocks
        self.windowed, self.last_of_tile = windowed, last_of_tile
        self.first = tile == 0


def windowed_groups():
    return [Group(i, [[4 * g + 2 * j, 4 * g + 2 * j + 1] for g in range(4)], [i, i + 1], True, j == 1)
            for i in range(TPB) for j in range(2)]


def causal_groups():
    return [Group(i, [[4 * g + j] for g in range(4)], list(range(1, i + 2)), False, j == 3)
            for i in range(TPB) for j in range(4)]


class AttentionPhase:

    def __init__(self, sem, tag, groups, src):
        self.groups = groups
        self.units = [(k, g) for k in range(len(groups)) for g in range(4)]
        self.src = src
        self.zs_ready = sem(tag + "zs_ready")
        self.zT_done = sem(tag + "zT_done")
        self.zT_ev = sem(tag + "zT_ev")
        self.q_done = sem(tag + "q_done")
        self.q_ev = sem(tag + "q_ev")
        self.k_done = sem(tag + "k_done")
        self.k_ev = sem(tag + "k_ev")
        self.v_done = sem(tag + "v_done")
        self.v_ev = sem(tag + "v_ev")
        self.pad_done = sem(tag + "pad_done")
        self.scores_done = sem(tag + "scores_done")
        self.max_done = sem(tag + "max_done")
        self.exp_done = sem(tag + "exp_done")
        self.t_done = sem(tag + "t_done")
        self.evac_act = sem(tag + "evac_act")
        self.evac_dve = sem(tag + "evac_dve")
        self.av_done = sem(tag + "av_done")
        self.norm_done = sem(tag + "norm_done")
        self.oT_done = sem(tag + "oT_done")
        self.oT_ev = sem(tag + "oT_ev")
        self.wo_done = sem(tag + "wo_done")
        self.wo_ev = sem(tag + "wo_ev")
        self.post_done = sem(tag + "post_done")


class ExpertPhase:

    def __init__(self, sem, tag, experts, src):
        self.experts = experts
        self.src = src
        self.x_ready = sem(tag + "x_ready")
        self.T_done = sem(tag + "T_done")
        self.T_ev = sem(tag + "T_ev")
        self.up_done = sem(tag + "up_done")
        self.gelu_done = sem(tag + "gelu_done")
        self.y_done = sem(tag + "y_done")
        self.acc_done = sem(tag + "acc_done")


class RecurrencePhase:

    def __init__(self, sem):
        self.h_ready = sem("r_h_ready")
        self.x_ready = sem("r_x_ready")
        self.T_done = sem("r_T_done")
        self.T_ev = sem("r_T_ev")
        self.kvqg_done = sem("r_kvqg_done")
        self.f1_ev = sem("r_f1_ev")
        self.g1_ev = sem("r_g1_ev")
        self.f_done = sem("r_f_done")
        self.gate_done = sem("r_gate_done")
        self.sg_ready = sem("r_sg_ready")
        self.fg_ready = sem("r_fg_ready")
        self.psum_free = sem("r_psum_free")
        self.st_ready = sem("r_st_ready")
        self.st_out = sem("r_st_out")
        self.scan_in = sem("r_scan_in")
        self.kv_ready = sem("r_kv_ready")
        self.step = sem("r_step")
        self.od_ready = sem("r_od_ready")
        self.o_out = sem("r_o_out")
        self.of_in = sem("r_of_in")
        self.o1_ready = sem("r_o1_ready")
        self.mean_done = sem("r_mean_done")
        self.sq_ready = sem("r_sq_ready")
        self.msq_done = sem("r_msq_done")
        self.ex_ready = sem("r_ex_ready")
        self.y_done = sem("r_y_done")
        self.x_done = sem("r_x_done")


def build(nc, d, out):
    ctx = ExitStack()
    with ctx:
        def sb(name, shape, dt=F32):
            return ctx.enter_context(nc.sbuf_tensor(name, shape, dt))

        def sem(name):
            return ctx.enter_context(nc.semaphore(name))

        ps = ctx.enter_context(nc.psum_tensor("ps", [P, 8, 512], F32))
        X = sb("X", [P, TILES, P])
        w1 = sb("w1", [P, EXPERTS, HID])
        w2 = sb("w2", [P, EXPERTS, CHUNKS, P])
        eb1 = sb("eb1", [P, EXPERTS, CHUNKS])
        eb2 = sb("eb2", [EXPERTS, P])
        gate_w = sb("gate_w", [P, EXPERTS])
        brow = sb("brow", [P, EXPERTS])
        aw = sb("aw", [P, 4, P])
        arow = sb("arow", [P, 4, P])
        acol = sb("acol", [P, 2])
        fw1 = sb("fw1", [P, HID])
        fw2 = sb("fw2", [P, CHUNKS, P])
        frow = sb("frow", [P, 3, P])
        fcol = sb("fcol", [P, CHUNKS])
        crow = sb("crow", [P, 4, P])
        pos = sb("pos", [P, TPB, P])
        ident = sb("ident", [P, P])
        mask_win = sb("mask_win", [P, 2 * P], BF16)
        mask_win0 = sb("mask_win0", [P, 2 * P], BF16)
        mask_cau = sb("mask_cau", [P, TOKENS], BF16)
        hm = sb("hm", [P, 4])
        rev = sb("rev", [P, EXPERTS])
        zero = sb("zero", [P, P])
        ones = sb("ones", [P, P])
        rt = [sb(f"rt{i}", [P, TILES, EXPERTS]) for i in range(4)]
        C = sb("C", [P, TILES, EXPERTS])
        LG = sb("LG", [P, TILES, EXPERTS])
        r1 = sb("r1", [P, TILES])
        r2 = sb("r2", [P, TILES])
        stats = sb("stats", [P, TILES, 6])
        mv = sb("mv", [P, TILES, 2])
        rstd = sb("rstd", [P, TILES])
        nv = sb("nv", [P, TILES])
        nt = sb("nt", [P, TILES])
        nmax = sb("nmax", [P, 8, 2])
        orec = sb("orec", [P, HEADS])

        arena = sb("arena", [P, 34048])
        at = [0]

        def take(*shape):
            n = int(np.prod(shape))
            v = arena[:, at[0]:at[0] + n]
            at[0] += n
            assert at[0] <= 34048
            if len(shape) == 2:
                v = v.rearrange("p (a b) -> p a b", b=shape[1])
            if len(shape) == 3:
                v = v.rearrange("p (a b c) -> p a b c", b=shape[1], c=shape[2])
            return v

        A = take(TILES, P)
        H = take(TILES, P)
        Pr = take(8, 512)
        PT = take(4, 512)
        Qe = [take(4, TOKENS) for _ in range(2)]
        Ke = [take(4, P + TOKENS) for _ in range(2)]
        Vx = [take(TPB + 1, HEADS, HD + 1) for _ in range(2)]
        On = [take(TPB, P) for _ in range(2)]
        OT = take(TPB, P)
        zs = [take(TPB, P) for _ in range(2)]
        zT = [take(TPB * P) for _ in range(2)]
        hid = [take(512) for _ in range(2)]
        at[0] = 0
        KW = take(TOKENS, 2, HD)
        UA = take(TOKENS, 2, HD)
        FD = take(HD, TOKENS)
        VD = take(HD, TOKENS)
        TMP = take(HD, TOKENS)
        QD = take(HD, SEEN)
        G1 = take(TOKENS)
        N2 = take(TOKENS)
        RN = take(TOKENS)
        T1 = take(TOKENS)
        C1 = take(TOKENS)
        GATE = take(BATCHES, OUT)
        KD = UA.rearrange("p a b c -> p (a b c)")[:, 0:HD * TOKENS].rearrange("p (a b) -> p a b", b=TOKENS)
        at[0] = 4 * HD * TOKENS + 2 * HD * TOKENS
        MM = take(STEP_RING, HD * HD, 4)
        SH = take(STEP_RING, HD, HD)
        M1 = take(2 * HD, HD)
        XY = take(2, HD)
        OQ = take(STEP_RING, HD, HD)
        at[0] = 4 * HD * TOKENS + 3 * HD * TOKENS + HD * SEEN
        OD = take(HD, SEEN)
        at[0] = 0
        OF = take(BATCHES, SEEN)
        O1 = take(BATCHES, OUT)
        O2 = take(BATCHES, OUT)
        O3 = take(BATCHES, OUT)
        O4 = take(BATCHES, OUT)
        at[0] = 2 * HD * TOKENS * 2
        EX = take(BATCHES, TOKENS)
        at[0] = 2 * TILES * P
        sgk, sgv, sgq, stf, stg = (take(TOKENS) for _ in range(5))
        stk, stv, stq = (take(TOKENS) for _ in range(3))
        f1s, g1s = take(TOKENS), take(TOKENS)

        scr_k = nc.dram_tensor("scr_k", [BATCHES, P, TOKENS], F32, kind="Internal").ap()
        scr_v = nc.dram_tensor("scr_v", [BATCHES, P, TOKENS], F32, kind="Internal").ap()
        scr_f = nc.dram_tensor("scr_f", [BATCHES, P, TOKENS], F32, kind="Internal").ap()
        scr_q = nc.dram_tensor("scr_q", [BATCHES, P, SEEN], F32, kind="Internal").ap()
        scr_g = nc.dram_tensor("scr_g", [BATCHES, HEADS, TOKENS], F32, kind="Internal").ap()
        scr_o = nc.dram_tensor("scr_o", [BATCHES, P, SEEN], F32, kind="Internal").ap()

        loaded = sem("loaded")
        stored = sem("stored")
        phase = sem("phase")
        const_ready = sem("const_ready")
        sink = sem("sink")
        v_chain = sem("v_chain")
        g_chain = sem("g_chain")
        a_chain = sem("a_chain")
        var_ready = sem("var_ready")
        rstd_ready = sem("rstd_ready")
        win = AttentionPhase(sem, "w_", windowed_groups(), A)
        cau = AttentionPhase(sem, "c_", causal_groups(), H)
        ffn = ExpertPhase(sem, "f_", 1, A)
        moe = ExpertPhase(sem, "m_", EXPERTS, H)
        h_ready = sem("h_ready")
        pT_done = sem("pT_done")
        pT_ev = sem("pT_ev")
        lg_done = sem("lg_done")
        d_ready = sem("d_ready")
        e_ready = sem("e_ready")
        c_ready = sem("c_ready")
        cT_done = sem("cT_done")
        cT_ev = sem("cT_ev")
        yb_done = sem("yb_done")
        yb_ev = sem("yb_ev")
        R = RecurrencePhase(sem)

        ENGINES = 5

        def gate(eng):
            eng.sem_inc(sink, 1)

        def barrier(eng, n):
            gate(eng)
            eng.drain().then_inc(phase, 1)
            eng.wait_ge(phase, (n + 1) * ENGINES)
            gate(eng)

        PH_SETUP = 0
        PH_MOE1 = 1
        PH_INIT = 3
        PH_LAYER = 4
        PH_MOE2 = PH_LAYER + 2 * LAYERS
        PH_CAUSAL1 = PH_MOE2 + 2
        PH_REC = PH_CAUSAL1 + 4
        PH_CAUSAL2 = PH_REC + 3
        PH_END = PH_CAUSAL2 + 4

        def tiles(arr, b):
            return arr[:, bass.ts(b, TPB), :]

        def row(r):
            return r.unsqueeze(1).broadcast_to([P, TPB, P])

        block = ctx.enter_context(nc.Block())

        @block.sync
        def _(sp):
            n = [0]

            def load(dst, src):
                sp.dma_start(dst, src).then_inc(loaded, 16)
                n[0] += 16

            def load_attention(layer):
                load(aw[:], d["attn_w"][layer])
                load(arow[:], d["attn_row"][layer].partition_broadcast(P))
                load(acol[:], d["attn_col"][layer])

            def load_experts(a):
                load(w1[:], d[a + "_w1"].rearrange("e d f -> d e f"))
                load(w2[:], d[a + "_w2"].rearrange("e (c f) d -> f e c d", f=P))
                with nc.allow_non_contiguous_dma(reason="small bias columns"):
                    load(eb1[:], d[a + "_b1"].rearrange("e (c f) -> f e c", f=P))
                load(eb2[:], d[a + "_b2"])
                load(gate_w[:], d[a + "_gate"])

            load(X[:], d["x"].rearrange("b (i p) f -> p (b i) f", p=P))
            load_experts("L0")
            load(crow[:], d["crow"].partition_broadcast(P))
            load(pos[:], d["pos"].rearrange("(i p) f -> p i f", p=P))
            load(hm[:], d["hm"])
            load(rev[:], d["rev"].partition_broadcast(P))
            load(brow[:], d["L1_br"].partition_broadcast(P))
            sp.wait_ge(loaded, n[0])
            barrier(sp, PH_SETUP)
            barrier(sp, PH_MOE1)
            barrier(sp, PH_MOE1 + 1)
            load_attention(0)
            sp.wait_ge(loaded, n[0])
            barrier(sp, PH_INIT)
            base = n[0]
            with sp.Fori(0, LAYERS) as l:
                n[0] = 0
                load(fw1[:], d["ffn_w1"][l])
                load(fw2[:], d["ffn_w2"][l])
                load(frow[:], d["ffn_row"][l].partition_broadcast(P))
                load(fcol[:], d["ffn_col"][l])
                per = n[0] + 48
                sp.wait_ge(loaded, base + l * per + n[0])
                barrier(sp, PH_LAYER + 2 * l)
                load_attention(l + 1)
                sp.wait_ge(loaded, base + l * per + n[0])
                barrier(sp, PH_LAYER + 2 * l + 1)
                assert n[0] == per
            n[0] = base + LAYERS * per
            barrier(sp, PH_MOE2)
            barrier(sp, PH_MOE2 + 1)
            load_experts("L1")
            sp.wait_ge(loaded, n[0])
            barrier(sp, PH_CAUSAL1)
            barrier(sp, PH_CAUSAL1 + 1)
            load(aw[:], d["rec_w"])
            load(fw1[:, 0:8], d["rec_f1"])
            load(fw1[:, 8:16], d["rec_o1"])
            load(fw1[:, 16:32], d["rec_g"])
            load(fw2[0:8, 0, :], d["rec_f2"])
            load(fw2[0:8, 1, :], d["rec_o2"])
            load(fcol[:, 0:1], d["rec_lnw"].rearrange("(p a) -> p a", a=1))
            sp.wait_ge(loaded, n[0])
            barrier(sp, PH_CAUSAL1 + 2)
            barrier(sp, PH_CAUSAL1 + 3)
            with sp.Fori(0, BATCHES) as b:
                sp.wait_ge(R.st_ready, 3 * b + 3 + START)
                sp.wait_ge(R.fg_ready, 2 * b + 2 + START)
                sp.dma_start(scr_k[b], stk).then_inc(R.st_out, 16)
                sp.dma_start(scr_v[b], stv).then_inc(R.st_out, 16)
                sp.dma_start(scr_q[b], stq[:, 0:SEEN]).then_inc(R.st_out, 16)
                sp.dma_start(scr_f[b], stf).then_inc(R.st_out, 16)
                sp.dma_start(scr_g[b], stg[0:HEADS, :]).then_inc(R.st_out, 16)
                sp.wait_ge(R.st_out, 80 * b + 80 + START)
                gate(sp)
            barrier(sp, PH_REC)
            for dst, src in ((KD, scr_k), (FD, scr_f), (VD, scr_v), (QD, scr_q)):
                sp.dma_start(dst, src.rearrange("b (h k) t -> (b h) k t", k=HD)).then_inc(R.scan_in, 16)
            sp.dma_start(G1, scr_g.rearrange("b h t -> (b h) t")).then_inc(R.scan_in, 16)
            sp.wait_ge(R.od_ready, 1)
            sp.dma_start(scr_o.rearrange("b (h k) t -> (b h) k t", k=HD), OD).then_inc(R.o_out, 16)
            sp.wait_ge(R.o_out, 16)
            sp.dma_start(OF, scr_o.rearrange("b p t -> p b t")).then_inc(R.of_in, 16)
            sp.wait_ge(R.of_in, 16)
            barrier(sp, PH_REC + 1)
            barrier(sp, PH_REC + 2)
            load(aw[:], d["attn_w"][LAYERS])
            sp.wait_ge(loaded, n[0])
            for k in range(4):
                barrier(sp, PH_CAUSAL2 + k)
            sp.dma_start(out.rearrange("b (i p) f -> p (b i) f", p=P), X[:]).then_inc(stored, 16)
            sp.wait_ge(stored, 16)

        @block.gpsimd
        def _(pool):
            chain = Chain(pool, g_chain)
            norms = Tally()

            pool.memset(ident[:], 0.0).then_inc(const_ready, 1)
            pool.memset(mask_win[:], 0.0).then_inc(const_ready, 1)
            pool.memset(mask_win0[:, 0:P - 1], BIG).then_inc(const_ready, 1)
            pool.memset(mask_win0[:, P - 1:], 0.0).then_inc(const_ready, 1)
            pool.memset(mask_cau[:], 0.0).then_inc(const_ready, 1)
            pool.memset(zero[:], 0.0).then_inc(const_ready, 1)

            def constant_parts():
                for k in Ke:
                    pool.memset(k, 0.0).then_inc(const_ready, 1)
                for v in Vx:
                    pool.memset(v[:, :, :, HD:], 1.0).then_inc(const_ready, 1)

            constant_parts()
            pool.wait_ge(const_ready, 10)
            pool.affine_select(out=ident[:], in_=ident[:], compare_op=ALU.not_equal, fill=1.0, base=0,
                               pattern=[[-1, P]], channel_multiplier=1).then_inc(const_ready, 1)
            m = mask_win[:, 0:P]
            pool.affine_select(out=m, in_=m, compare_op=ALU.is_ge, fill=BIG, base=PAST - P,
                               pattern=[[1, P]], channel_multiplier=-1).then_inc(const_ready, 1)
            m = mask_win0[:, P - 1:P]
            pool.affine_select(out=m, in_=m, compare_op=ALU.is_ge, fill=BIG, base=PAST - 1,
                               pattern=[[0, 1]], channel_multiplier=-1).then_inc(const_ready, 1)
            for m in (mask_win[:, P:], mask_win0[:, P:], mask_cau[:, TOKENS - P:]):
                pool.affine_select(out=m, in_=m, compare_op=ALU.is_ge, fill=BIG, base=0,
                                   pattern=[[-1, P]], channel_multiplier=1).then_inc(const_ready, 1)
            pool.wait_ge(const_ready, 16)
            gate(pool)

            def rsqrt(n, at=0):
                pool.wait_ge(var_ready, norms.value() + 1)
                gate(pool)
                w, t, y = nv[:, 0:n], nt[:, 0:n], rstd[:, at:at + n]
                chain.add(pool.tensor_scalar(w, mv[:, at:at + n, 1], EPS, None, ALU.add))
                chain.join()
                gate(pool)
                chain.add(pool.tensor_scalar(y.bitcast(I32), w.bitcast(I32), -0.5, MAGIC, ALU.mult, ALU.add))
                for k in range(3):
                    chain.join()
                    chain.link(pool.tensor_tensor(t, y, y, ALU.mult))
                    chain.add(pool.tensor_tensor(t, t, w, ALU.mult))
                    chain.join()
                    gate(pool)
                    chain.link(pool.tensor_scalar(t, t, -0.5, 1.5, ALU.mult, ALU.add))
                    if k < 2:
                        chain.add(pool.tensor_tensor(y, y, t, ALU.mult))
                    else:
                        pool.tensor_tensor(y, y, t, ALU.mult).then_inc(rstd_ready, 1)
                norms.n += 1

            def attention(S, u0, name):
                def rows(b, p):
                    pool.tensor_copy(zs[p], tiles(S.src, b)).then_inc(S.zs_ready, 1)

                rows(0, 0)
                rows(1, 1)
                with counted_loop(pool, name, BATCHES // 2 - 1, (chain, norms)) as it:
                    for p in range(2):
                        b = 2 * it + p
                        pool.wait_ge(S.zT_done, u0 + b + 1)
                        gate(pool)
                        rows(b + 2, p)
                        if S is win:
                            rsqrt(TPB)
                if S is win:
                    for b in (BATCHES - 2, BATCHES - 1):
                        rsqrt(TPB)

            def expert_main(S, v0, name):
                def rows(b, p):
                    pool.tensor_copy(zs[p], tiles(S.src, b)).then_inc(S.x_ready, 1)

                rows(0, 0)
                rows(1, 1)
                with counted_loop(pool, name, BATCHES // 2 - 1, (chain, norms)) as it:
                    for p in range(2):
                        b = 2 * it + p
                        pool.wait_ge(S.T_done, v0 + b + 1)
                        gate(pool)
                        rows(b + 2, p)
                        if S is ffn:
                            rsqrt(TPB, p * TPB)
                if S is ffn:
                    for p in range(2):
                        rsqrt(TPB, p * TPB)

            for S in (win, cau):
                for s in (S.wo_ev, S.norm_done, S.evac_act, S.evac_dve):
                    pool.sem_inc(s, START)
            for S in (ffn, moe):
                for s in (S.T_ev, S.gelu_done, S.acc_done):
                    pool.sem_inc(s, START)
            for s in (R.T_done, R.st_ready, R.fg_ready, R.st_out):
                pool.sem_inc(s, START)
            barrier(pool, PH_SETUP)
            rsqrt(TILES)
            barrier(pool, PH_MOE1)
            expert_main(moe, 0, "pool moe")
            barrier(pool, PH_MOE1 + 1)
            rsqrt(TILES)
            rsqrt(TILES)
            barrier(pool, PH_INIT)
            with counted_loop(pool, "pool layer", LAYERS, (chain, norms)) as l:
                attention(win, l * BATCHES, "pool window")
                barrier(pool, PH_LAYER + 2 * l)
                expert_main(ffn, l * BATCHES, "pool ffn")
                barrier(pool, PH_LAYER + 2 * l + 1)
            rsqrt(TILES)
            barrier(pool, PH_MOE2)
            expert_main(moe, BATCHES, "pool moe")
            barrier(pool, PH_MOE2 + 1)

            def causal_block(use, ph):
                rsqrt(TILES)
                rsqrt(TILES)
                barrier(pool, ph)
                attention(cau, use * BATCHES, "pool causal")
                barrier(pool, ph + 1)
                rsqrt(TILES)
                barrier(pool, ph + 2)
                expert_main(moe, (2 + use) * BATCHES, "pool moe")
                barrier(pool, ph + 3)

            causal_block(0, PH_CAUSAL1)
            rsqrt(TILES)
            with pool.Fori(0, BATCHES) as b:
                pool.wait_ge(R.T_done, b + START)
                pool.wait_ge(R.h_ready, 1)
                gate(pool)
                pool.tensor_copy(zs[0], tiles(H, b)).then_inc(R.x_ready, 1)
            barrier(pool, PH_REC)
            half = STEP_RING // 2
            pool.wait_ge(R.scan_in, 80)
            pool.wait_ge(R.step, 1)
            gate(pool)
            with pool.Fori(0, TOKENS // STEP_RING) as it:
                for c in range(2):
                    pool.wait_ge(R.step, STEP_RING * it + half * c + 1)
                    gate(pool)
                    t0 = STEP_RING * it + half * c
                    slot = MM[:, half * c:half * (c + 1), :, 0].rearrange("p s (v k) -> p s v k", k=HD)
                    vv = VD[:, :, bass.ds(t0, half)].rearrange("p v t -> p t v").unsqueeze(3)\
                        .broadcast_to([P, half, HD, HD])
                    kk = KW[:, bass.ds(t0, half), 0, :].unsqueeze(2).broadcast_to([P, half, HD, HD])
                    pool.tensor_tensor(slot, vv, kk, ALU.mult).then_inc(R.kv_ready, 1)
            barrier(pool, PH_REC + 1)
            barrier(pool, PH_REC + 2)
            constant_parts()
            causal_block(1, PH_CAUSAL2)

        @block.tensor
        def _(pe):
            def turn_rows(bank, rows, done):
                for i in range(TPB):
                    m = pe.transpose(ps[:, bank, i * P:(i + 1) * P], rows[:, i, :], ident[:])
                m.then_inc(done, 1)

            def attention(S, u0):
                G = len(S.groups)
                units = S.units
                n = len(units)

                def prep_turn(b, p):
                    pe.wait_ge(S.zs_ready, u0 + b + 1)
                    turn_rows(7, zs[p], S.zT_done)

                def prep_queries(b, p):
                    pe.wait_ge(S.zT_ev, u0 + b + 1)
                    pe.matmul(ps[:, 7, :], aw[:, 0, :], zT[p], start=True, stop=True).then_inc(S.q_done, 1)

                def prep_keys(b, p):
                    pe.wait_ge(S.q_ev, u0 + b + 1)
                    pe.matmul(ps[:, 7, :], aw[:, 1, :], zT[p], start=True, stop=True).then_inc(S.k_done, 1)

                def prep_values(b, p):
                    pe.wait_ge(S.k_ev, u0 + b + 1)
                    for i in range(TPB):
                        m = pe.matmul(ps[:, 7, i * P:(i + 1) * P], zT[p][:, i * P:(i + 1) * P],
                                      aw[:, 2, :], start=(i == 0), stop=(i == TPB - 1),
                                      skip_group_check=True)
                    m.then_inc(S.v_done, 1)

                def post_turn(b, p):
                    pe.wait_ge(S.norm_done, (u0 + b + 1) * TPB + START)
                    turn_rows(7, On[p], S.oT_done)

                def post_project(b):
                    pe.wait_ge(S.oT_ev, u0 + b + 1)
                    for i in range(TPB):
                        m = pe.matmul(ps[:, 7, i * P:(i + 1) * P], OT[:, i, :], aw[:, 3, :],
                                      start=(i == 0), stop=(i == TPB - 1), skip_group_check=True)
                    m.then_inc(S.wo_done, 1)

                def scores(b, p, k, g):
                    gr = S.groups[k]
                    kw = P * len(gr.blocks)
                    k0 = P * gr.blocks[0]
                    q0 = P * gr.tile
                    pe.wait_ge(S.max_done, ((u0 + b) * G + k) * 4 + g + 1)
                    for j, h in enumerate(gr.heads[g]):
                        m = pe.matmul(ps[:, g, j * kw:(j + 1) * kw], Qe[p][:, h % 4, q0:q0 + P],
                                      Ke[p][:, g, k0:k0 + kw], start=True, stop=True, skip_group_check=True)
                    m.then_inc(S.scores_done, 1)

                def turn_probs(b, p, k, g):
                    gr = S.groups[k]
                    n = ((u0 + b) * G + k) * 4 + g
                    half = ((u0 + b) * G + k) * 2 + g // 2
                    pe.wait_ge(S.exp_done, n + 1)
                    pe.wait_ge(S.evac_dve if g % 2 else S.evac_act, half + START)
                    nb = len(gr.heads[g]) * len(gr.blocks)
                    for c in range(nb):
                        m = pe.transpose(ps[:, 4 + g % 2, c * P:(c + 1) * P],
                                         Pr[:, 4 * (k % 2) + g, c * P:(c + 1) * P], ident[:])
                    m.then_inc(S.t_done, 1)

                def values(b, p, k, g):
                    gr = S.groups[k]
                    tile = (u0 + b) * TPB + gr.tile
                    half = ((u0 + b) * G + k) * 2 + g // 2
                    pe.wait_ge(S.evac_dve if g % 2 else S.evac_act, half + 1 + START)
                    first = g == 0 and (k == 0 or S.groups[k - 1].tile != gr.tile)
                    if first:
                        pe.wait_ge(S.norm_done, tile + START)
                    for j, h in enumerate(gr.heads[g]):
                        for c, blk in enumerate(gr.blocks):
                            cc = j * len(gr.blocks) + c
                            m = pe.matmul(ps[:, 6, h * (HD + 1):(h + 1) * (HD + 1)],
                                          PT[:, g, cc * P:(cc + 1) * P], Vx[p][:, blk, h, :],
                                          start=first and cc == 0, stop=True, skip_group_check=True)
                    if gr.last_of_tile and g == 3:
                        m.then_inc(S.av_done, 1)

                def stage(b, p, first=False, last=False):
                    for s in range(n + (TURN_LAG + 1 if last else 0)):
                        if s == POST_TURN and not first:
                            pe.wait_ge(S.v_ev, u0 + b + 1)
                            post_turn(b - 1, 1 - p)
                        if s == POST_PROJECT and not first:
                            post_project(b - 1)
                        if not last:
                            if s == PREP_TURN:
                                if first:
                                    pe.wait_ge(S.v_ev, u0 + b + 1)
                                else:
                                    pe.wait_ge(S.wo_ev, u0 + b + START)
                                prep_turn(b + 1, 1 - p)
                            if s == PREP_QUERIES:
                                prep_queries(b + 1, 1 - p)
                            if s == PREP_KEYS:
                                prep_keys(b + 1, 1 - p)
                            if s == PREP_VALUES:
                                prep_values(b + 1, 1 - p)
                        if s == 0:
                            pe.wait_ge(S.v_ev, u0 + b + 1)
                            pe.wait_ge(S.pad_done, 2 * (u0 + b) + 2)
                        if s < n:
                            scores(b, p, *units[s])
                        unit = lagged(units, b, p, s, TURN_LAG, first)
                        if unit:
                            turn_probs(*unit)
                        unit = lagged(units, b, p, s, TURN_LAG + 1, first)
                        if unit:
                            values(*unit)

                prep_turn(0, 0)
                prep_queries(0, 0)
                prep_keys(0, 0)
                prep_values(0, 0)
                run_batches(pe, "pe attention", (), stage)
                b = BATCHES - 1
                pe.wait_ge(S.wo_ev, u0 + b + START)
                post_turn(b, 1)
                post_project(b)

            def expert_main(S, v0, W1, W2):
                E = S.experts
                order = [(e, c) for e in range(E) for c in range(CHUNKS)]

                def turn(b, p):
                    pe.wait_ge(S.x_ready, v0 + b + 1)
                    pe.wait_ge(S.T_ev, v0 + b + START)
                    turn_rows(5, zs[p], S.T_done)

                def up(b, p, e, c):
                    n = ((v0 + b) * E + e) * CHUNKS + c
                    if e == 0 and c == 0:
                        pe.wait_ge(S.T_ev, v0 + b + 1 + START)
                    pe.wait_ge(S.gelu_done, n + START)
                    pe.matmul(ps[:, c % 2, :], W1(e)[:, c * P:(c + 1) * P], zT[p], start=True, stop=True)\
                        .then_inc(S.up_done, 1)

                def down(b, p, e, c):
                    n = ((v0 + b) * E + e) * CHUNKS + c
                    pe.wait_ge(S.gelu_done, n + 2 + START)
                    if c == 0:
                        pe.wait_ge(S.acc_done, (v0 + b) * E + e + START)
                    for i in range(TPB):
                        m = pe.matmul(ps[:, 2 + (p * E + e) % 2, i * P:(i + 1) * P],
                                      hid[c % 2][:, i * P:(i + 1) * P], W2(e)[:, c, :],
                                      start=(c == 0 and i == 0), stop=(c == CHUNKS - 1),
                                      skip_group_check=True)
                    if c == CHUNKS - 1:
                        m.then_inc(S.y_done, 1)

                def stage(b, p, first=False, last=False):
                    for s, (e, c) in enumerate(order):
                        up(b, p, e, c)
                        if s == 1 and not last:
                            turn(b + 1, 1 - p)
                        if s:
                            down(b, p, *order[s - 1])
                        elif not first:
                            down(b - 1, 1 - p, *order[-1])

                turn(0, 0)
                run_batches(pe, "pe experts", (), stage)
                down(BATCHES - 1, 1, *order[-1])

            def expert_pre(v0):
                def logits(b):
                    pe.wait_ge(pT_ev, v0 + b + 1)
                    for t in range(TPB * b, TPB * (b + 1)):
                        m = pe.matmul(ps[:, 6, t * EXPERTS:(t + 1) * EXPERTS],
                                      zT[b % 2][:, t % TPB * P:(t % TPB + 1) * P], gate_w[:],
                                      start=(t == 0), stop=(t == TILES - 1), skip_group_check=True)
                    return m

                for b in range(BATCHES):
                    pe.wait_ge(h_ready, v0 + b + 1)
                    if b >= 2:
                        pe.wait_ge(pT_ev, v0 + b - 1)
                    turn_rows(5 + 2 * (b % 2), H[:, TPB * b:TPB * (b + 1), :], pT_done)
                    if b:
                        logits(b - 1)
                logits(BATCHES - 1).then_inc(lg_done, 1)
                pe.wait_ge(c_ready, v0 // BATCHES + 1)
                for b in range(BATCHES):
                    for i in range(TPB):
                        m = pe.transpose(ps[0:EXPERTS, b % 2, i * P:(i + 1) * P], C[:, TPB * b + i, :], ident[:])
                    m.then_inc(cT_done, 1)
                    pe.wait_ge(cT_ev, v0 + b + 1)
                    if b >= 2:
                        pe.wait_ge(yb_ev, v0 + b - 1)
                    for i in range(TPB):
                        m = pe.matmul(ps[:, 2 + b % 2, i * P:(i + 1) * P],
                                      zT[b % 2][0:EXPERTS, i * P:(i + 1) * P], eb2[:],
                                      start=(i == 0), stop=(i == TPB - 1), skip_group_check=True)
                    m.then_inc(yb_done, 1)

            E1, E2 = (lambda e: w1[:, e, :]), (lambda e: w2[:, e])
            pe.wait_ge(const_ready, 16)
            barrier(pe, PH_SETUP)
            expert_pre(0)
            barrier(pe, PH_MOE1)
            expert_main(moe, 0, E1, E2)
            barrier(pe, PH_MOE1 + 1)
            barrier(pe, PH_INIT)
            with pe.Fori(0, LAYERS) as l:
                attention(win, l * BATCHES)
                barrier(pe, PH_LAYER + 2 * l)
                expert_main(ffn, l * BATCHES, lambda e: fw1[:], lambda e: fw2[:])
                barrier(pe, PH_LAYER + 2 * l + 1)
            expert_pre(BATCHES)
            barrier(pe, PH_MOE2)
            expert_main(moe, BATCHES, E1, E2)
            barrier(pe, PH_MOE2 + 1)

            def causal_block(use, ph):
                barrier(pe, ph)
                attention(cau, use * BATCHES)
                barrier(pe, ph + 1)
                expert_pre((2 + use) * BATCHES)
                barrier(pe, ph + 2)
                expert_main(moe, (2 + use) * BATCHES, E1, E2)
                barrier(pe, ph + 3)

            causal_block(0, PH_CAUSAL1)
            with pe.Fori(0, BATCHES) as b:
                pe.wait_ge(R.x_ready, b + 1)
                turn_rows(5, zs[0], R.T_done)
                pe.wait_ge(R.T_ev, b + 1)
                pe.wait_ge(R.st_ready, 3 * b + START)
                pe.wait_ge(R.fg_ready, 2 * b + START)
                pe.matmul(ps[:, 0, :], aw[:, 1, :], zT[0], start=True, stop=True).then_inc(R.kvqg_done, 1)
                pe.matmul(ps[:, 1, :], aw[:, 2, :], zT[0], start=True, stop=True).then_inc(R.kvqg_done, 1)
                pe.matmul(ps[:, 2, 0:SEEN], aw[:, 0, :], zT[0][:, TOKENS - SEEN:], start=True, stop=True)\
                    .then_inc(R.kvqg_done, 1)
                pe.matmul(ps[0:8, 3, :], fw1[:, 0:8], zT[0], start=True, stop=True).then_inc(R.kvqg_done, 1)
                pe.matmul(ps[0:8, 4, 0:OUT], fw1[:, 8:16], zT[0][:, 1::3], start=True, stop=True)\
                    .then_inc(R.kvqg_done, 1)
                pe.matmul(ps[0:HEADS, 6, :], fw1[:, 16:32], zT[0], start=True, stop=True).then_inc(R.kvqg_done, 1)
                pe.wait_ge(R.f1_ev, b + 1)
                pe.matmul(ps[:, 3, :], fw2[0:8, 0, :], f1s[0:8, :], start=True, stop=True).then_inc(R.f_done, 1)
                pe.wait_ge(R.g1_ev, b + 1)
                pe.matmul(ps[:, 7, 0:OUT], fw2[0:8, 1, :], g1s[0:8, 0:OUT], start=True, stop=True)\
                    .then_inc(R.gate_done, 1)
            barrier(pe, PH_REC)
            barrier(pe, PH_REC + 1)
            for src, ready, done, bank in ((O1, R.o1_ready, R.mean_done, 0), (O3, R.sq_ready, R.msq_done, 4)):
                pe.wait_ge(ready, 1)
                for k in range(4):
                    m = pe.matmul(ps[:, bank + k, 0:2 * OUT], ones[:], src[:, 2 * k:2 * k + 2, :]
                                  .rearrange("p a b -> p (a b)"), start=True, stop=True)
                m.then_inc(done, 1)
            pe.wait_ge(R.ex_ready, 1)
            for b in range(BATCHES):
                if b >= 2:
                    pe.wait_ge(R.x_done, b - 1)
                for i in range(TPB):
                    m = pe.matmul(ps[:, b % 2, i * P:(i + 1) * P], EX[:, b, i * P:(i + 1) * P], aw[:, 3, :],
                                  start=(i == 0), stop=(i == TPB - 1), skip_group_check=True)
                m.then_inc(R.y_done, 1)
            barrier(pe, PH_REC + 2)
            causal_block(1, PH_CAUSAL2)

        @block.scalar
        def _(act):
            chain = Chain(act, a_chain)
            copy, exp, gelu, sigmoid = ACT.Copy, ACT.Exp, ACT.Gelu, ACT.Sigmoid
            act.sem_inc(win.max_done, 4)
            act.sem_inc(cau.max_done, 4)
            act.sem_inc(ffn.gelu_done, 1)
            act.sem_inc(moe.gelu_done, 1)

            def attention(S, u0):
                G = len(S.groups)
                units = S.units
                n = len(units)

                def prep_turn(b, p):
                    act.wait_ge(S.zT_done, u0 + b + 1)
                    act.activation(zT[p], ps[:, 7, :], copy).then_inc(S.zT_ev, 1)

                def prep_keys(b, p):
                    act.wait_ge(S.k_done, u0 + b + 1)
                    for g in range(4):
                        rows = slice(32 * g, 32 * g + 32)
                        m = act.activation(Ke[p][rows, g, P:], ps[rows, 7, :], ACT.Identity,
                                           bias=acol[rows, 1:2])
                    m.then_inc(S.k_ev, 1)

                def prep_pad(p):
                    for g in range(4):
                        rows = slice(32 * g, 32 * g + 32)
                        m = act.activation(Ke[p][rows, g, 0:P], zero[rows, :], ACT.Identity,
                                           bias=acol[rows, 1:2])
                    m.then_inc(S.pad_done, 1)

                def post_turn(b):
                    act.wait_ge(S.oT_done, u0 + b + 1)
                    act.activation(OT.rearrange("p a b -> p (a b)"), ps[:, 7, :], copy).then_inc(S.oT_ev, 1)

                def probs(b, p, k, g):
                    gr = S.groups[k]
                    kw = P * len(gr.blocks)
                    act.wait_ge(S.max_done, ((u0 + b) * G + k) * 4 + g + 5)
                    slot = 4 * (k % 2) + g
                    for j in range(len(gr.heads[g])):
                        m = act.activation(Pr[:, slot, j * kw:(j + 1) * kw], Pr[:, slot, j * kw:(j + 1) * kw],
                                           exp, bias=nmax[:, slot, j:j + 1], scale=-1.0)
                    m.then_inc(S.exp_done, 1)

                def evac(b, p, k, g):
                    gr = S.groups[k]
                    act.wait_ge(S.t_done, ((u0 + b) * G + k) * 4 + g + 1)
                    w = P * len(gr.blocks) * len(gr.heads[g])
                    act.activation(PT[:, g, 0:w], ps[:, 4 + g % 2, 0:w], copy).then_inc(S.evac_act, 1)

                def stage(b, p, first=False, last=False):
                    for s in range(n + (TURN_LAG if last else 0)):
                        if s == POST_TURN + 1 and not first:
                            post_turn(b - 1)
                        if s == PREP_TURN + 1 and not last:
                            prep_turn(b + 1, 1 - p)
                        if s == PREP_KEYS + 1 and not last:
                            prep_keys(b + 1, 1 - p)
                        if s == PREP_KEYS + 3 and not last:
                            prep_pad(1 - p)
                        unit = lagged(units, b, p, s, TURN_LAG, first)
                        if unit and unit[3] % 2 == 0:
                            evac(*unit)
                        if s < n:
                            probs(b, p, *units[s])

                prep_turn(0, 0)
                prep_keys(0, 0)
                prep_pad(0)
                run_batches(act, "act attention", (), stage)
                post_turn(BATCHES - 1)

            def expert_main(S, v0, b1):
                E = S.experts

                def turn(b, p):
                    act.wait_ge(S.T_done, v0 + b + 1)
                    act.activation(zT[p], ps[:, 5, :], copy).then_inc(S.T_ev, 1)

                def stage(b, p, first=False, last=False):
                    for e in range(E):
                        for c in range(CHUNKS):
                            act.wait_ge(S.up_done, ((v0 + b) * E + e) * CHUNKS + c + 1)
                            act.activation(hid[c % 2], ps[:, c % 2, :], gelu, bias=b1(e)[:, c:c + 1])\
                                .then_inc(S.gelu_done, 1)
                            if (e, c) == (0, 1) and not last:
                                turn(b + 1, 1 - p)

                turn(0, 0)
                run_batches(act, "act experts", (), stage)

            def expert_pre(v0):
                for b in range(BATCHES):
                    act.wait_ge(pT_done, v0 + b + 1)
                    act.activation(zT[b % 2], ps[:, 5 + 2 * (b % 2), :], copy).then_inc(pT_ev, 1)
                act.wait_ge(d_ready, v0 // BATCHES + 1)
                act.activation(rt[1][:], rt[0][:], exp).then_inc(e_ready, 1)
                for b in range(BATCHES):
                    act.wait_ge(cT_done, v0 + b + 1)
                    act.activation(zT[b % 2][0:EXPERTS, :], ps[0:EXPERTS, b % 2, :], copy).then_inc(cT_ev, 1)

            B1 = lambda e: eb1[:, e, :]
            barrier(act, PH_SETUP)
            expert_pre(0)
            barrier(act, PH_MOE1)
            expert_main(moe, 0, B1)
            barrier(act, PH_MOE1 + 1)
            barrier(act, PH_INIT)
            with act.Fori(0, LAYERS) as l:
                attention(win, l * BATCHES)
                barrier(act, PH_LAYER + 2 * l)
                expert_main(ffn, l * BATCHES, lambda e: fcol[:])
                barrier(act, PH_LAYER + 2 * l + 1)
            expert_pre(BATCHES)
            barrier(act, PH_MOE2)
            expert_main(moe, BATCHES, B1)
            barrier(act, PH_MOE2 + 1)

            def causal_block(use, ph):
                barrier(act, ph)
                attention(cau, use * BATCHES)
                barrier(act, ph + 1)
                expert_pre((2 + use) * BATCHES)
                barrier(act, ph + 2)
                expert_main(moe, (2 + use) * BATCHES, B1)
                barrier(act, ph + 3)

            causal_block(0, PH_CAUSAL1)
            with act.Fori(0, BATCHES) as b:
                act.wait_ge(R.T_done, b + 1 + START)
                act.activation(zT[0], ps[:, 5, :], copy).then_inc(R.T_ev, 1)
                act.wait_ge(R.kvqg_done, 6 * b + 5)
                act.wait_ge(R.st_out, 80 * b + START)
                act.activation(f1s[0:8, :], ps[0:8, 3, :], copy).then_inc(R.f1_ev, 1)
                act.activation(g1s[0:8, 0:OUT], ps[0:8, 4, 0:OUT], copy).then_inc(R.g1_ev, 1)
                for s, bank, w in ((sgk, 0, TOKENS), (sgv, 1, TOKENS), (sgq, 2, SEEN)):
                    act.activation(s[:, 0:w], ps[:, bank, 0:w], sigmoid).then_inc(R.sg_ready, 1)
                act.wait_ge(R.kvqg_done, 6 * b + 6)
                act.activation(stg[0:HEADS, :], ps[0:HEADS, 6, :], sigmoid).then_inc(R.fg_ready, 1)
                act.wait_ge(R.gate_done, b + 1)
                gate(act)
                act.activation(GATE[:, b, :], ps[:, 7, 0:OUT], sigmoid).then_inc(R.psum_free, 1)
                act.wait_ge(R.f_done, b + 1)
                act.activation(stf, ps[:, 3, :], sigmoid).then_inc(R.fg_ready, 1)
            barrier(act, PH_REC)
            barrier(act, PH_REC + 1)
            barrier(act, PH_REC + 2)
            causal_block(1, PH_CAUSAL2)

        @block.vector
        def _(dve):
            chain = Chain(dve, v_chain)
            norms = Tally()
            for S in (ffn, moe):
                dve.sem_inc(S.acc_done, 1)

            def norm_stats(get, n, at=0):
                gate(dve)
                for t in range(n):
                    chain.add(dve.bn_stats(stats[:, at + t, :], get(t)))
                chain.join()
                gate(dve)
                for t in range(n):
                    m = dve.bn_aggr(mv[:, at + t, :], stats[:, at + t, :])
                m.then_inc(var_ready, 1)

            def norm_wait():
                dve.wait_ge(rstd_ready, norms.value() + 1)
                gate(dve)
                norms.n += 1

            def norm_apply(dst, get, n, at=0):
                for t in range(n):
                    chain.add(dve.tensor_scalar(dst(t), get(t), mv[:, at + t, 0:1], rstd[:, at + t:at + t + 1],
                                                ALU.subtract, ALU.mult))
                chain.join()

            def affine(dst, src, g, b):
                chain.link(dve.tensor_tensor(dst, src, row(g), ALU.mult))
                return dve.tensor_tensor(dst, dst, row(b), ALU.add)

            def norm_all(src, dst):
                norm_stats(lambda t: src[:, t, :], TILES)
                norm_wait()
                norm_apply(lambda t: dst[:, t, :], lambda t: src[:, t, :], TILES)

            def attention(S, u0, name):
                G = len(S.groups)
                units = S.units
                n = len(units)

                def prep_queries(b, p, slots):
                    dve.wait_ge(S.q_done, u0 + b + 1)
                    for j in slots:
                        m = dve.tensor_scalar(Qe[p][:, j, :], ps[:, 7, :], acol[:, 0:1], hm[:, j:j + 1],
                                              ALU.add, ALU.mult)
                    if slots[-1] == 3:
                        m.then_inc(S.q_ev, 1)

                def prep_values(b, p):
                    bv = arow[:, 0, :].rearrange("p (h k) -> p h k", k=HD)
                    dve.wait_ge(S.v_done, u0 + b + 1)
                    dve.tensor_tensor(Vx[p][:, 1:, :, 0:HD],
                                      ps[:, 7, :].rearrange("p (i h k) -> p i h k", h=HEADS, k=HD),
                                      bv.unsqueeze(1).broadcast_to([P, TPB, HEADS, HD]), ALU.add)\
                        .then_inc(S.v_ev, 1)
                    dve.tensor_tensor(Vx[p][:, 0, :, 0:HD], bv,
                                      zero[:].rearrange("p (h k) -> p h k", k=HD), ALU.add).then_inc(S.pad_done, 1)

                def post_add(b):
                    x = tiles(A, b)
                    dve.wait_ge(S.wo_done, u0 + b + 1)
                    dve.tensor_tensor(x, ps[:, 7, :].rearrange("p (i k) -> p i k", k=P), x, ALU.add)\
                        .then_inc(S.wo_ev, 1)
                    dve.wait_ge(S.wo_ev, u0 + b + 1 + START)
                    chain.link(dve.tensor_tensor(x, x, row(arow[:, 1, :]), ALU.add))

                def post_stats(b):
                    if S is win:
                        norm_stats(lambda t: A[:, b * TPB + t, :], TPB)

                def post_apply(b):
                    if S is win:
                        norm_wait()
                        norm_apply(lambda t: A[:, b * TPB + t, :], lambda t: A[:, b * TPB + t, :], TPB)

                def post_gain(b):
                    if S is win:
                        x = tiles(A, b)
                        chain.link(dve.tensor_tensor(x, x, row(arow[:, 2, :]), ALU.mult))

                def post_bias(b):
                    if S is win:
                        x = tiles(A, b)
                        chain.link(dve.tensor_tensor(x, x, row(arow[:, 3, :]), ALU.add))

                posts = {POST_PROJECT + 1: post_add, POST_PROJECT + 2: post_stats, POST_PROJECT + 6: post_apply,
                         POST_PROJECT + 10: post_gain, POST_PROJECT + 12: post_bias}

                def maxima(b, p, k, g):
                    gr = S.groups[k]
                    kw = P * len(gr.blocks)
                    nh = len(gr.heads[g])
                    dve.wait_ge(S.scores_done, ((u0 + b) * G + k) * 4 + g + 1)
                    gate(dve)
                    slot = 4 * (k % 2) + g
                    if gr.windowed:
                        mask = mask_win0[:] if gr.first else mask_win[:]
                    else:
                        mask = mask_cau[:, TOKENS - kw:]
                    for j in range(nh):
                        m = dve.tensor_tensor_reduce(out=Pr[:, slot, j * kw:(j + 1) * kw],
                                                     in0=ps[:, g, j * kw:(j + 1) * kw], in1=mask,
                                                     scale=1.0, scalar=NO_SCORE, op0=ALU.add, op1=ALU.min,
                                                     accum_out=nmax[:, slot, j:j + 1])
                    m.then_inc(S.max_done, 1)

                def evac(b, p, k, g):
                    gr = S.groups[k]
                    dve.wait_ge(S.t_done, ((u0 + b) * G + k) * 4 + g + 1)
                    w = P * len(gr.blocks) * len(gr.heads[g])
                    dve.tensor_copy(PT[:, g, 0:w], ps[:, 4 + g % 2, 0:w]).then_inc(S.evac_dve, 1)

                def normalise(b, p, i):
                    dve.wait_ge(S.av_done, (u0 + b) * TPB + i + 1)
                    o = ps[:, 6, 0:HEADS * (HD + 1)].rearrange("p (h k) -> p h k", k=HD + 1)
                    chain.link(dve.reciprocal(orec[:], o[:, :, HD]))
                    dve.tensor_tensor(On[p][:, i, :].rearrange("p (h k) -> p h k", k=HD), o[:, :, 0:HD],
                                      orec[:].unsqueeze(2).broadcast_to([P, HEADS, HD]), ALU.mult)\
                        .then_inc(S.norm_done, 1)

                def stage(b, p, first=False, last=False):
                    for s in range(n + (TURN_LAG + 3 if last else 0)):
                        if s in posts and not first:
                            posts[s](b - 1)
                        if not last:
                            if s == PREP_QUERIES + 1:
                                prep_queries(b + 1, 1 - p, (0, 1))
                            if s == PREP_QUERIES + 2:
                                prep_queries(b + 1, 1 - p, (2, 3))
                            if s == PREP_VALUES + 1:
                                prep_values(b + 1, 1 - p)
                        unit = lagged(units, b, p, s, TURN_LAG + 2, first)
                        if unit and unit[3] == 3 and S.groups[unit[2]].last_of_tile:
                            normalise(unit[0], unit[1], S.groups[unit[2]].tile)
                        if s < n:
                            maxima(b, p, *units[s])
                        unit = lagged(units, b, p, s, TURN_LAG, first)
                        if unit and unit[3] % 2:
                            evac(*unit)

                prep_queries(0, 0, (0, 1, 2, 3))
                prep_values(0, 0)
                run_batches(dve, name, (chain, norms), stage)
                for step in posts.values():
                    step(BATCHES - 1)

            def feed_forward(v0):
                S = ffn

                def apply(b, p):
                    x = tiles(A, b)
                    norm_wait()
                    norm_apply(lambda t: A[:, b * TPB + t, :], lambda t: A[:, b * TPB + t, :], TPB, p * TPB)
                    chain.link(affine(x, x, frow[:, 1, :], frow[:, 2, :]))

                def stage(b, p, first=False, last=False):
                    x = tiles(A, b)
                    dve.wait_ge(S.y_done, v0 + b + 1)
                    dve.tensor_tensor(x, ps[:, 2 + p, :].rearrange("p (i k) -> p i k", k=P), x, ALU.add)\
                        .then_inc(S.acc_done, 1)
                    dve.wait_ge(S.acc_done, v0 + b + 2 + START)
                    chain.link(dve.tensor_tensor(x, x, row(frow[:, 0, :]), ALU.add))
                    norm_stats(lambda t: A[:, b * TPB + t, :], TPB, p * TPB)
                    if not first:
                        apply(b - 1, 1 - p)

                run_batches(dve, "dve ffn", (chain, norms), stage)
                apply(BATCHES - 1, 1)

            def expert_main(v0):
                S = moe
                with dve.Fori(0, BATCHES // 2) as it:
                    for p in range(2):
                        for e in range(EXPERTS):
                            n = (v0 + 2 * it + p) * EXPERTS + e
                            dve.wait_ge(S.y_done, n + 1)
                            dve.wait_ge(S.acc_done, n + 1 + START)
                            gate(dve)
                            for i in range(TPB):
                                t = (2 * it + p) * TPB + i
                                m = dve.scalar_tensor_tensor(
                                    out=X[:, t, :], in0=ps[:, 2 + e % 2, i * P:(i + 1) * P],
                                    scalar=C[:, t, e:e + 1], in1=X[:, t, :], op0=ALU.mult, op1=ALU.add)
                            m.then_inc(S.acc_done, 1)

            def expert_pre(v0, first):
                use = v0 // BATCHES
                top1 = use < 2
                if not first:
                    chain.link(dve.scalar_tensor_tensor(out=X[:], in0=A, scalar=1.0 if top1 else 0.5, in1=X[:],
                                                        op0=ALU.mult, op1=ALU.add))
                src = X if top1 else A
                norm_stats(lambda t: src[:, t, :], TILES)
                norm_wait()
                for b in range(BATCHES):
                    t0 = TPB * b
                    x = H[:, t0:t0 + TPB, :]
                    norm_apply(lambda t: H[:, t0 + t, :], lambda t: src[:, t0 + t, :], TPB, t0)
                    if top1:
                        dve.engine_nop().then_inc(h_ready, 1)
                    else:
                        affine(x, x, crow[:, 2, :], crow[:, 3, :]).then_inc(h_ready, 1)
                dve.wait_ge(lg_done, use + 1)
                lg = ps[:, 6, 0:TILES * EXPERTS].rearrange("p (a b) -> p a b", b=EXPERTS)
                if top1:
                    chain.link(dve.tensor_copy(LG[:], lg))
                else:
                    chain.link(dve.tensor_tensor(LG[:], lg, brow[:].unsqueeze(1)
                                                 .broadcast_to([P, TILES, EXPERTS]), ALU.add))
                wide = lambda a: a[:].unsqueeze(2).broadcast_to([P, TILES, EXPERTS])
                chain.link(dve.tensor_reduce(r1[:], LG[:], AX_X, ALU.max))
                dve.tensor_tensor(rt[0][:], LG[:], wide(r1), ALU.subtract).then_inc(d_ready, 1)
                chain.link(dve.tensor_tensor(rt[2][:], LG[:], wide(r1), ALU.is_equal))
                chain.link(dve.tensor_tensor(rt[2][:], rt[2][:], rev[:].unsqueeze(1)
                                             .broadcast_to([P, TILES, EXPERTS]), ALU.mult))
                chain.link(dve.tensor_reduce(r2[:], rt[2][:], AX_X, ALU.max))
                chain.link(dve.tensor_tensor(rt[3][:], rt[2][:], wide(r2), ALU.is_equal))
                dve.wait_ge(e_ready, use + 1)
                if top1:
                    chain.link(dve.tensor_reduce(r1[:], rt[1][:], AX_X, ALU.add))
                    chain.link(dve.reciprocal(r2[:], r1[:]))
                else:
                    chain.link(dve.scalar_tensor_tensor(out=rt[2][:], in0=rt[3][:], scalar=-BIG, in1=LG[:],
                                                        op0=ALU.mult, op1=ALU.add))
                    chain.link(dve.tensor_reduce(r2[:], rt[2][:], AX_X, ALU.max))
                    chain.link(dve.tensor_tensor(rt[2][:], LG[:], wide(r2), ALU.is_ge))
                    chain.link(dve.tensor_tensor(rt[3][:], rt[1][:], rt[2][:], ALU.mult))
                    chain.link(dve.tensor_reduce(r1[:], rt[3][:], AX_X, ALU.add))
                    chain.link(dve.reciprocal(r2[:], r1[:]))
                chain.link(dve.tensor_scalar(r1[:], r2[:], 0.5, None, ALU.mult))
                dve.tensor_tensor(C[:], rt[3][:], wide(r1), ALU.mult).then_inc(c_ready, 1)
                for b in range(BATCHES):
                    dve.wait_ge(yb_done, v0 + b + 1)
                    x = X[:, TPB * b:TPB * (b + 1), :]
                    dve.tensor_tensor(x, ps[:, 2 + b % 2, :].rearrange("p (i k) -> p i k", k=P), x, ALU.add)\
                        .then_inc(yb_ev, 1)

            dve.memset(ones[:], 1.0 / P).then_inc(v_chain, 1)
            chain.n += 1
            barrier(dve, PH_SETUP)
            expert_pre(0, True)
            barrier(dve, PH_MOE1)
            expert_main(0)
            barrier(dve, PH_MOE1 + 1)
            norm_all(X, A)
            norm_all(A, A)
            for b in range(BATCHES):
                x = A[:, TPB * b:TPB * (b + 1), :]
                chain.link(affine(x, x, crow[:, 0, :], crow[:, 1, :]))
                chain.link(dve.tensor_tensor(x, x, pos[:], ALU.add))
            barrier(dve, PH_INIT)
            with counted_loop(dve, "dve layer", LAYERS, (chain, norms)) as l:
                attention(win, l * BATCHES, "dve window")
                barrier(dve, PH_LAYER + 2 * l)
                feed_forward(l * BATCHES)
                barrier(dve, PH_LAYER + 2 * l + 1)
            expert_pre(BATCHES, False)
            barrier(dve, PH_MOE2)
            expert_main(BATCHES)
            barrier(dve, PH_MOE2 + 1)

            def causal_block(use, ph):
                norm_all(X, A)
                norm_stats(lambda t: A[:, t, :], TILES)
                norm_wait()
                norm_apply(lambda t: H[:, t, :], lambda t: A[:, t, :], TILES)
                for b in range(BATCHES):
                    x = H[:, TPB * b:TPB * (b + 1), :]
                    chain.link(affine(x, x, arow[:, 2, :], arow[:, 3, :]))
                barrier(dve, ph)
                attention(cau, use * BATCHES, "dve causal")
                barrier(dve, ph + 1)
                expert_pre((2 + use) * BATCHES, False)
                barrier(dve, ph + 2)
                expert_main((2 + use) * BATCHES)
                barrier(dve, ph + 3)

            causal_block(0, PH_CAUSAL1)
            norm_stats(lambda t: X[:, t, :], TILES)
            norm_wait()
            norm_apply(lambda t: H[:, t, :], lambda t: X[:, t, :], TILES)
            dve.engine_nop().then_inc(R.h_ready, 1)
            with dve.Fori(0, BATCHES) as b:
                dve.wait_ge(R.st_out, 80 * b + START)
                for n, (s, sg, bank, w) in enumerate(((stk, sgk, 0, TOKENS), (stv, sgv, 1, TOKENS),
                                                      (stq, sgq, 2, SEEN))):
                    dve.wait_ge(R.sg_ready, 3 * b + n + 1)
                    dve.tensor_tensor(s[:, 0:w], ps[:, bank, 0:w], sg[:, 0:w], ALU.mult).then_inc(R.st_ready, 1)
            barrier(dve, PH_REC)
            dve.wait_ge(R.scan_in, 80)
            gate(dve)
            by_time = lambda a: a.rearrange("p k t -> p t k")
            over_k = lambda a: a.unsqueeze(1).broadcast_to([P, HD, TOKENS])
            kn, wv, ua, av = KW[:, :, 0, :], KW[:, :, 1, :], UA[:, :, 0, :], UA[:, :, 1, :]
            chain.link(dve.tensor_tensor(TMP, KD, KD, ALU.mult))
            chain.link(dve.tensor_reduce(N2, by_time(TMP), AX_X, ALU.add))
            chain.link(dve.tensor_scalar(N2, N2, 1e-24, None, ALU.max))
            newton(dve, chain, RN, N2, T1)
            chain.link(dve.tensor_tensor(TMP, KD, over_k(RN), ALU.mult))
            chain.link(dve.tensor_copy(kn, by_time(TMP)))
            chain.link(dve.tensor_scalar(G1, G1, -1.0, None, ALU.mult))
            chain.link(dve.tensor_tensor(av, kn, G1.unsqueeze(2).broadcast_to([P, TOKENS, HD]), ALU.mult))
            chain.link(dve.tensor_tensor(wv, kn, by_time(FD), ALU.mult))
            chain.link(dve.tensor_tensor(ua, av, by_time(FD), ALU.mult))
            chain.link(dve.tensor_tensor(by_time(TMP), kn, ua, ALU.mult))
            chain.link(dve.tensor_reduce(C1, by_time(TMP), AX_X, ALU.add))
            chain.link(dve.tensor_tensor(by_time(TMP), av, C1.unsqueeze(2).broadcast_to([P, TOKENS, HD]), ALU.mult))
            chain.link(dve.tensor_tensor(ua, ua, by_time(TMP), ALU.add))
            dve.memset(SH[:, STEP_RING - 1], 0.0).then_inc(R.step, 1)
            dve.wait_ge(R.step, 1)
            dve.sem_inc(R.step, STEP_RING // 2)
            last_turn = TOKENS // STEP_RING
            seen_turn = (TOKENS - SEEN) // STEP_RING
            for lo, hi, name in ((0, seen_turn, "scan"), (seen_turn, last_turn, "scan seen")):
                with counted_loop(dve, name, hi - lo, (chain,)) as i:
                    it = lo + i
                    for j in range(STEP_RING):
                        t = STEP_RING * it + j
                        s = SH[:, (j - 1) % STEP_RING]
                        new = SH[:, j]
                        mj = MM[:, j]
                        at_t = lambda a: a[:, bass.ds(t, 1), :, :].rearrange("p a b c -> p (a b) c")
                        if j % 4 == 0:
                            dve.wait_ge(R.kv_ready, 2 * it + j // 4 + 1)
                        chain.add(dve.tensor_tensor(
                            M1.rearrange("p (a v) k -> p a v k", a=2),
                            s.unsqueeze(1).broadcast_to([P, 2, HD, HD]),
                            at_t(KW).unsqueeze(2).broadcast_to([P, 2, HD, HD]), ALU.mult))
                        chain.add(dve.tensor_tensor(
                            mj[:, :, 1].rearrange("p (v k) -> p v k", k=HD), s,
                            FD[:, :, bass.ds(t, 1)].rearrange("p k a -> p (a k)").unsqueeze(1)
                            .broadcast_to([P, HD, HD]), ALU.mult))
                        dve.wait_ge(v_chain, chain.value() - 1)
                        chain.link(dve.tensor_reduce(XY.rearrange("p a b -> p (a b)"), M1, AX_X, ALU.add))
                        chain.link(dve.tensor_tensor(
                            mj[:, :, 2:4].rearrange("p (v k) r -> p r v k", k=HD),
                            at_t(UA).unsqueeze(2).broadcast_to([P, 2, HD, HD]),
                            XY.unsqueeze(3).broadcast_to([P, 2, HD, HD]), ALU.mult))
                        dve.tensor_reduce(new.rearrange("p v k -> p (v k)"), mj, AX_X, ALU.add).then_inc(R.step, 1)
                        dve.wait_ge(R.step, t + 2 + STEP_RING // 2)
                    if lo:
                        q = QD[:, :, bass.ds(STEP_RING * i, STEP_RING)].rearrange("p k t -> p t k").unsqueeze(2)\
                            .broadcast_to([P, STEP_RING, HD, HD])
                        chain.link(dve.tensor_tensor(OQ, SH, q, ALU.mult))
                        gate(dve)
                        chain.link(dve.tensor_reduce(
                            OD[:, :, bass.ds(STEP_RING * i, STEP_RING)].rearrange("p v t -> p t v"),
                            OQ, AX_X, ALU.add))
            dve.engine_nop().then_inc(R.od_ready, 1)
            barrier(dve, PH_REC + 1)
            half_banks = lambda b0: ps[:, b0:b0 + 4, 0:2 * OUT]
            quad = lambda a: a.rearrange("p (c a) b -> p c (a b)", a=2)
            dve.tensor_tensor(O1, OF[:, :, SEEN - OUT:], GATE, ALU.mult).then_inc(R.o1_ready, 1)
            chain.link(dve.memset(EX, 0.0))
            dve.wait_ge(R.o1_ready, 1)
            dve.wait_ge(R.mean_done, 1)
            chain.link(dve.tensor_tensor(quad(O2), quad(O1), half_banks(0), ALU.subtract))
            dve.tensor_tensor(O3, O2, O2, ALU.mult).then_inc(R.sq_ready, 1)
            dve.wait_ge(R.msq_done, 1)
            chain.link(dve.tensor_scalar(quad(O1), half_banks(4), EPS, None, ALU.add))
            flat = lambda a: a.rearrange("p a b -> p (a b)")
            newton(dve, chain, flat(O4), flat(O1), flat(O3))
            dve.scalar_tensor_tensor(out=EX[:, :, 1::3], in0=O2, scalar=fcol[:, 0:1], in1=O4,
                                     op0=ALU.mult, op1=ALU.mult).then_inc(R.ex_ready, 1)
            for b in range(BATCHES):
                dve.wait_ge(R.y_done, b + 1)
                x = X[:, TPB * b:TPB * (b + 1), :]
                dve.tensor_tensor(x, ps[:, b % 2, :].rearrange("p (i k) -> p i k", k=P), x, ALU.add)\
                    .then_inc(R.x_done, 1)
            barrier(dve, PH_REC + 2)
            causal_block(1, PH_CAUSAL2)

    if wrong:
        raise AssertionError(f"PER_TURN: {wrong}")


def newton(eng, chain, y, w, t):
    chain.link(eng.tensor_scalar(y.bitcast(I32), w.bitcast(I32), -0.5, MAGIC, ALU.mult, ALU.add))
    for _ in range(3):
        chain.link(eng.tensor_tensor(t, y, y, ALU.mult))
        chain.link(eng.tensor_tensor(t, t, w, ALU.mult))
        chain.link(eng.tensor_scalar(t, t, -0.5, 1.5, ALU.mult, ALU.add))
        chain.link(eng.tensor_tensor(y, y, t, ALU.mult))


def _lay_out(x):
    a = {k: np.asarray(v) for k, v in x.items()}
    d = {"x": a["L0_attn_x"]}
    wqkv = a["L0_attn_Wqkv"].reshape(LAYERS, 3, P, P).transpose(0, 3, 1, 2)
    wo = a["L0_attn_Wo"].transpose(0, 2, 1)[:, :, None, :]
    causal = np.stack([a["L1_ffn_" + n] for n in ("Wq", "Wk", "Wv", "Wo")], 1)[None]
    d["attn_w"] = np.concatenate([np.concatenate([wqkv, wo], 2), causal])
    bqkv = a["L0_attn_bqkv"].reshape(LAYERS, 3, P)
    row = np.stack([bqkv[:, 2], a["L0_attn_bo"], a["L0_attn_ln1_g"], a["L0_attn_ln1_b"]], 1)
    crow = np.stack([a["L1_ffn_" + n] for n in ("bv", "bo", "ln1_g", "ln1_b")])[None]
    d["attn_row"] = np.concatenate([row, crow])
    col = np.stack([bqkv[:, 0], bqkv[:, 1]], 2)
    ccol = np.stack([a["L1_ffn_bq"], a["L1_ffn_bk"]], 1)[None]
    d["attn_col"] = np.concatenate([col, ccol])
    d["ffn_w1"] = a["L0_attn_W1"].transpose(0, 2, 1)
    d["ffn_w2"] = a["L0_attn_W2"].transpose(0, 2, 1).reshape(LAYERS, CHUNKS, P, P).transpose(0, 2, 1, 3)
    d["ffn_row"] = np.stack([a["L0_attn_b2"], a["L0_attn_ln2_g"], a["L0_attn_ln2_b"]], 1)
    d["ffn_col"] = a["L0_attn_b1"].reshape(LAYERS, CHUNKS, P).transpose(0, 2, 1)
    d["crow"] = np.stack([a["L0_attn_norm_in_g"], a["L0_attn_norm_in_b"], a["L1_ffn_ln2_g"], a["L1_ffn_ln2_b"]])
    for n in ("w1", "w2", "b1", "b2"):
        d["L0_" + n], d["L1_" + n] = a["L0_ffn_" + n], a["L1_ffn_e_" + n]
    d["L0_gate"], d["L1_gate"], d["L1_br"] = a["L0_ffn_gate_w"], a["L1_ffn_Wr"], a["L1_ffn_br"]
    d["rec_w"] = np.stack([a["L1_attn_" + n] for n in ("Wq", "Wk", "Wv", "Wout")], 1)
    for n, m in (("f1", "Wf1"), ("f2", "Wf2"), ("o1", "Wo1"), ("o2", "Wo2"), ("g", "Wg"), ("lnw", "ln_w")):
        d["rec_" + n] = a["L1_attn_" + m]
    half = P // 2
    where = np.arange(TOKENS, dtype=np.float32)[:, None]
    turn = where / np.float32(10000.0) ** (np.arange(half, dtype=np.float32)[None] / np.float32(half - 1))
    d["pos"] = np.concatenate([np.cos(turn), np.sin(turn)], 1).astype(np.float32)
    own = (np.arange(P)[:, None] // HD) % 4 == np.arange(4)[None]
    d["hm"] = np.where(own, -1.0 / np.sqrt(HD), 0.0).astype(np.float32)
    d["rev"] = np.arange(EXPERTS, 0, -1).astype(np.float32)
    return {k: np.ascontiguousarray(v) for k, v in d.items()}


def kernel(**inputs):
    import concourse.bacc as _bacc
    from concourse.bass_utils import run_bass_kernel_spmd as _run

    nc = _bacc.Bacc("TRN2", target_bir_lowering=False, num_devices=1)
    arrays = {f"in_{k}_dram": v for k, v in _lay_out(inputs).items()}
    d = {k[3:-5]: nc.dram_tensor(k, v.shape, mybir.dt.from_np(v.dtype), kind="ExternalInput").ap()
         for k, v in arrays.items()}
    out = nc.dram_tensor("out_0_dram", (BATCHES, TOKENS, P), F32, kind="ExternalOutput").ap()
    build(nc, d, out)
    r = _run(nc, [arrays], core_ids=[0])
    return r.results[0]["out_0_dram"]
```

```python
from contextlib import ExitStack, contextmanager

import numpy as np

import concourse.bass as bass
from concourse import mybir

F32 = mybir.dt.float32
BF16 = mybir.dt.bfloat16
I32 = mybir.dt.int32
ALU = mybir.AluOpType
ACT = mybir.ActivationFunctionType
AX_X = mybir.AxisListType.X

P = 128
BATCHES, TOKENS = 8, 512
TPB = TOKENS // P
TILES = BATCHES * TPB
HEADS, HD = 16, 8
LAYERS = 6
HID = 512
CHUNKS = HID // P
EXPERTS = 8
PAST = 125
EPS = 1e-5
BIG = 1e30
NO_SCORE = 3e38
MAGIC = 1597463007.0
SEEN = 176
OUT = 171
TURN_LAG = 3
POST_TURN, POST_PROJECT = 5, 8
PREP_TURN, PREP_QUERIES, PREP_KEYS, PREP_VALUES = 12, 15, 19, 22
START = 1
STEP_RING = 8

PER_TURN = {'pool window': (26, 2), 'pool ffn': (26, 2), 'dve window': (28, 2), 'dve ffn': (20, 2), 'dve causal': (30, 2), 'pool causal': (26, 2), 'scan': (40,), 'scan seen': (42,),
            'pool layer': (208, 16), 'pool moe 2': (52, 4), 'pool moe 1': (26, 2), 'dve moe input': (38, 4),
            'dve moe causal': (36, 4), 'dve moe rows': (16, 2), 'dve layer': (192, 16)}


class Tally:

    def __init__(self):
        self.base, self.n = 0, 0

    def value(self):
        return self.base + self.n


class Chain(Tally):

    def __init__(self, eng, sem):
        super().__init__()
        self.eng, self.sem = eng, sem

    def add(self, ins):
        ins.then_inc(self.sem, 1)
        self.n += 1

    def join(self):
        self.eng.wait_ge(self.sem, self.value())

    def link(self, ins):
        self.add(ins)
        self.join()


def lagged(units, b, p, s, lag, first):
    i = s - lag
    if i >= len(units) or (i < 0 and first):
        return None
    return (b, p, *units[i]) if i >= 0 else (b - 1, 1 - p, *units[i])


wrong = {}


@contextmanager
def counted_loop(eng, name, count, tallies):
    per = PER_TURN.get(name, (0,) * len(tallies))
    before = [(t.base, t.n) for t in tallies]
    with eng.Fori(0, count) as i:
        for t, k in zip(tallies, per):
            t.base = t.base + i * k
        yield i
        got = tuple(t.n - n for t, (_, n) in zip(tallies, before))
        if got != tuple(per):
            wrong[name] = got
    for t, (base, n), k in zip(tallies, before, got):
        t.base, t.n = base, n + count * k


def run_batches(eng, name, tallies, stage):
    stage(0, 0, first=True)
    with counted_loop(eng, name, BATCHES // 2 - 1, tallies) as it:
        stage(2 * it + 1, 1)
        stage(2 * it + 2, 0)
    stage(BATCHES - 1, 1, last=True)


class Group:

    def __init__(self, tile, heads, blocks, windowed, last_of_tile):
        self.tile, self.heads, self.blocks = tile, heads, blocks
        self.windowed, self.last_of_tile = windowed, last_of_tile
        self.first = tile == 0


def windowed_groups():
    return [Group(i, [[4 * g + 2 * j, 4 * g + 2 * j + 1] for g in range(4)], [i, i + 1], True, j == 1)
            for i in range(TPB) for j in range(2)]


def causal_groups():
    groups = []
    for i in range(TPB):
        n = 2 if i < 2 else 1
        for j in range(4 // n):
            groups.append(Group(i, [[4 * g + n * j + h for h in range(n)] for g in range(4)],
                                list(range(1, i + 2)), False, j == 4 // n - 1))
    return groups


class AttentionPhase:

    def __init__(self, sem, tag, groups, src):
        self.groups = groups
        self.units = [(k, g) for k in range(len(groups)) for g in range(4)]
        self.src = src
        self.zs_ready = sem(tag + "zs_ready")
        self.zT_done = sem(tag + "zT_done")
        self.zT_ev = sem(tag + "zT_ev")
        self.q_done = sem(tag + "q_done")
        self.q_ev = sem(tag + "q_ev")
        self.k_done = sem(tag + "k_done")
        self.k_ev = sem(tag + "k_ev")
        self.v_done = sem(tag + "v_done")
        self.v_ev = sem(tag + "v_ev")
        self.pad_done = sem(tag + "pad_done")
        self.scores_done = sem(tag + "scores_done")
        self.max_done = sem(tag + "max_done")
        self.exp_done = sem(tag + "exp_done")
        self.t_done = sem(tag + "t_done")
        self.evac_act = sem(tag + "evac_act")
        self.evac_dve = sem(tag + "evac_dve")
        self.av_done = sem(tag + "av_done")
        self.norm_done = sem(tag + "norm_done")
        self.oT_done = sem(tag + "oT_done")
        self.oT_ev = sem(tag + "oT_ev")
        self.wo_done = sem(tag + "wo_done")
        self.wo_ev = sem(tag + "wo_ev")


class ExpertPhase:

    def __init__(self, sem, tag, experts, src):
        self.experts = experts
        self.src = src
        self.x_ready = sem(tag + "x_ready")
        self.T_done = sem(tag + "T_done")
        self.T_ev = sem(tag + "T_ev")
        self.up_done = sem(tag + "up_done")
        self.gelu_done = sem(tag + "gelu_done")
        self.y_done = sem(tag + "y_done")
        self.acc_done = sem(tag + "acc_done")


class RecurrencePhase:

    def __init__(self, sem):
        self.h_ready = sem("r_h_ready")
        self.x_ready = sem("r_x_ready")
        self.T_done = sem("r_T_done")
        self.T_ev = sem("r_T_ev")
        self.kvqg_done = sem("r_kvqg_done")
        self.f1_ev = sem("r_f1_ev")
        self.g1_ev = sem("r_g1_ev")
        self.f_done = sem("r_f_done")
        self.gate_done = sem("r_gate_done")
        self.sg_ready = sem("r_sg_ready")
        self.fg_ready = sem("r_fg_ready")
        self.st_ready = sem("r_st_ready")
        self.st_out = sem("r_st_out")
        self.k_in = sem("r_k_in")
        self.scan_in = sem("r_scan_in")
        self.kv_ready = sem("r_kv_ready")
        self.staged = sem("r_staged")
        self.step = sem("r_step")
        self.od_ready = sem("r_od_ready")
        self.o_out = sem("r_o_out")
        self.of_in = sem("r_of_in")
        self.o1_ready = sem("r_o1_ready")
        self.mean_done = sem("r_mean_done")
        self.sq_ready = sem("r_sq_ready")
        self.msq_done = sem("r_msq_done")
        self.ex_ready = sem("r_ex_ready")
        self.y_done = sem("r_y_done")
        self.x_done = sem("r_x_done")


def build(nc, d, out):
    ctx = ExitStack()
    with ctx:
        def sb(name, shape, dt=F32):
            return ctx.enter_context(nc.sbuf_tensor(name, shape, dt))

        def sem(name):
            return ctx.enter_context(nc.semaphore(name))

        ps = ctx.enter_context(nc.psum_tensor("ps", [P, 8, 512], F32))
        X = sb("X", [P, TILES, P])
        w1 = sb("w1", [P, EXPERTS, HID])
        w2 = sb("w2", [P, EXPERTS, CHUNKS, P])
        eb1 = sb("eb1", [P, EXPERTS, CHUNKS])
        eb2 = sb("eb2", [EXPERTS, P])
        gate_w = sb("gate_w", [P, EXPERTS])
        brow = sb("brow", [P, EXPERTS])
        aw = sb("aw", [P, 4, P])
        arow = sb("arow", [P, 4, P])
        acol = sb("acol", [P, 2])
        fw1 = sb("fw1", [P, HID])
        fw2 = sb("fw2", [P, CHUNKS, P])
        frow = sb("frow", [P, 3, P])
        fcol = sb("fcol", [P, CHUNKS])
        crow = sb("crow", [P, 4, P])
        pos = sb("pos", [P, TPB, P])
        ident = sb("ident", [P, P])
        mask_win = sb("mask_win", [P, 2 * P], BF16)
        mask_win0 = sb("mask_win0", [P, 2 * P], BF16)
        mask_cau = sb("mask_cau", [P, TOKENS], BF16)
        hm = sb("hm", [P, 4])
        rev = sb("rev", [P, EXPERTS])
        zero = sb("zero", [P, P])
        ones = sb("ones", [P, P])
        rt = [sb(f"rt{i}", [P, TILES, EXPERTS]) for i in range(4)]
        C = sb("C", [P, TILES, EXPERTS])
        LG = sb("LG", [P, TILES, EXPERTS])
        r1 = sb("r1", [P, TILES])
        r2 = sb("r2", [P, TILES])
        stats = sb("stats", [P, TILES, 6])
        mv = sb("mv", [P, TILES, 2])
        rstd = sb("rstd", [P, TILES])
        nv = sb("nv", [P, TILES])
        nt = sb("nt", [P, TILES])
        nmax = sb("nmax", [P, 8, 2])
        orec = sb("orec", [P, HEADS])

        arena = sb("arena", [P, 34048])
        at = [0]

        def take(*shape):
            n = int(np.prod(shape))
            v = arena[:, at[0]:at[0] + n]
            at[0] += n
            assert at[0] <= 34048
            if len(shape) == 2:
                v = v.rearrange("p (a b) -> p a b", b=shape[1])
            if len(shape) == 3:
                v = v.rearrange("p (a b c) -> p a b c", b=shape[1], c=shape[2])
            return v

        A = take(TILES, P)
        H = take(TILES, P)
        Pr = take(8, 512)
        PT = take(4, 512)
        Qe = [take(4, TOKENS) for _ in range(2)]
        Ke = [take(4, P + TOKENS) for _ in range(2)]
        Vx = [take(TPB + 1, HEADS, HD + 1) for _ in range(2)]
        On = [take(TPB, P) for _ in range(2)]
        OT = take(TPB, P)
        zs = [take(TPB, P) for _ in range(2)]
        zT = [take(TPB * P) for _ in range(2)]
        hid = [take(512) for _ in range(2)]
        Cs = [take(TPB, EXPERTS) for _ in range(2)]
        cT = [take(TPB * P) for _ in range(2)]
        at[0] = 0
        KW = take(TOKENS, 2, HD)
        UA = take(TOKENS, 2, HD)
        FD = take(HD, TOKENS)
        VD = take(HD, TOKENS)
        TMP = take(HD, TOKENS)
        QD = take(HD, SEEN)
        G1 = take(TOKENS)
        N2 = take(TOKENS)
        RN = take(TOKENS)
        T1 = take(TOKENS)
        C1 = take(TOKENS)
        GATE = take(BATCHES, OUT)
        KD = UA.rearrange("p a b c -> p (a b c)")[:, 0:HD * TOKENS].rearrange("p (a b) -> p a b", b=TOKENS)
        at[0] = 4 * HD * TOKENS + 2 * HD * TOKENS
        KV = take(STEP_RING, HD, HD)
        FS = take(HD, HD)
        MJ = take(HD * HD, 3)
        SH = take(STEP_RING, HD, HD)
        M1 = take(2 * HD, HD)
        XY = take(2, HD)
        OQ = take(STEP_RING, HD, HD)
        KWs = take(STEP_RING, 2, HD)
        UAs = take(STEP_RING, 2, HD)
        Fs = take(STEP_RING, HD)
        at[0] = 4 * HD * TOKENS + 3 * HD * TOKENS + HD * SEEN
        OD = take(HD, SEEN)
        at[0] = 0
        OF = take(BATCHES, SEEN)
        O1 = take(BATCHES, OUT)
        O2 = take(BATCHES, OUT)
        O3 = take(BATCHES, OUT)
        O4 = take(BATCHES, OUT)
        at[0] = 2 * HD * TOKENS * 2
        EX = take(BATCHES, TOKENS)
        at[0] = 2 * TILES * P
        sgk, sgv, sgq, stf, stg = (take(TOKENS) for _ in range(5))
        stk, stv, stq = (take(TOKENS) for _ in range(3))
        f1s, g1s = take(TOKENS), take(TOKENS)

        scr_k = nc.dram_tensor("scr_k", [BATCHES, P, TOKENS], F32, kind="Internal").ap()
        scr_v = nc.dram_tensor("scr_v", [BATCHES, P, TOKENS], F32, kind="Internal").ap()
        scr_f = nc.dram_tensor("scr_f", [BATCHES, P, TOKENS], F32, kind="Internal").ap()
        scr_q = nc.dram_tensor("scr_q", [BATCHES, P, SEEN], F32, kind="Internal").ap()
        scr_g = nc.dram_tensor("scr_g", [BATCHES, HEADS, TOKENS], F32, kind="Internal").ap()
        scr_o = nc.dram_tensor("scr_o", [BATCHES, P, SEEN], F32, kind="Internal").ap()

        loaded = sem("loaded")
        stored = sem("stored")
        phase = sem("phase")
        const_ready = sem("const_ready")
        sink = sem("sink")
        v_chain = sem("v_chain")
        g_chain = sem("g_chain")
        a_chain = sem("a_chain")
        var_ready = sem("var_ready")
        rstd_ready = sem("rstd_ready")
        win = AttentionPhase(sem, "w_", windowed_groups(), A)
        cau = AttentionPhase(sem, "c_", causal_groups(), H)
        ffn = ExpertPhase(sem, "f_", 1, A)
        moe = ExpertPhase(sem, "m_", EXPERTS, H)
        attn_out = sem("attn_out")
        ffn_out = sem("ffn_out")
        h_ready = sem("h_ready")
        pT_done = sem("pT_done")
        pT_ev = sem("pT_ev")
        lg_done = sem("lg_done")
        d_ready = sem("d_ready")
        e_ready = sem("e_ready")
        yb_done = sem("yb_done")
        yb_ev = sem("yb_ev")
        R = RecurrencePhase(sem)

        ENGINES = 5

        def gate(eng):
            eng.sem_inc(sink, 1)

        def barrier(eng, n):
            gate(eng)
            eng.drain().then_inc(phase, 1)
            eng.wait_ge(phase, (n + 1) * ENGINES)
            gate(eng)

        PH_SETUP = 0
        PH_MOE1 = 1
        PH_INIT = 3
        PH_LAYERS = 4
        PH_MOE2 = PH_LAYERS + 1
        PH_CAUSAL1 = PH_MOE2 + 2
        PH_REC = PH_CAUSAL1 + 4
        PH_CAUSAL2 = PH_REC + 3
        PH_END = PH_CAUSAL2 + 4

        LOADED_AHEAD, ATTENTION_LOADS, FFN_LOADS = 14 * 16, 3 * 16, 4 * 16

        def attention_loaded(l):
            return LOADED_AHEAD + l * (ATTENTION_LOADS + FFN_LOADS)

        def tiles(arr, b):
            return arr[:, bass.ts(b, TPB), :]

        def row(r):
            return r.unsqueeze(1).broadcast_to([P, TPB, P])

        block = ctx.enter_context(nc.Block())

        @block.sync
        def _(sp):
            n = [0]

            def load(dst, src):
                sp.dma_start(dst, src).then_inc(loaded, 16)
                n[0] += 16

            def load_attention(layer):
                load(aw[:], d["attn_w"][layer])
                load(arow[:], d["attn_row"][layer].partition_broadcast(P))
                load(acol[:], d["attn_col"][layer])

            def load_router(a):
                load(eb2[:], d[a + "_b2"])
                load(gate_w[:], d[a + "_gate"])

            def load_experts(a):
                load(w1[:], d[a + "_w1"].rearrange("e d f -> d e f"))
                load(w2[:], d[a + "_w2"].rearrange("e (c f) d -> f e c d", f=P))
                with nc.allow_non_contiguous_dma(reason="small bias columns"):
                    load(eb1[:], d[a + "_b1"].rearrange("e (c f) -> f e c", f=P))

            load(X[:], d["x"].rearrange("b (i p) f -> p (b i) f", p=P))
            load_router("L0")
            load(crow[:], d["crow"].partition_broadcast(P))
            load(pos[:], d["pos"].rearrange("(i p) f -> p i f", p=P))
            load(hm[:], d["hm"])
            load(rev[:], d["rev"].partition_broadcast(P))
            load(brow[:], d["L1_br"].partition_broadcast(P))
            sp.wait_ge(loaded, n[0])
            barrier(sp, PH_SETUP)
            load_experts("L0")
            sp.wait_ge(loaded, n[0])
            barrier(sp, PH_MOE1)
            load_attention(0)
            sp.wait_ge(loaded, n[0])
            barrier(sp, PH_MOE1 + 1)
            barrier(sp, PH_INIT)
            base = n[0]
            with sp.Fori(0, LAYERS) as l:
                n[0] = 0
                sp.wait_ge(ffn_out, (l + 1) * BATCHES)
                gate(sp)
                load(fw1[:], d["ffn_w1"][l])
                load(fw2[:], d["ffn_w2"][l])
                load(frow[:], d["ffn_row"][l].partition_broadcast(P))
                load(fcol[:], d["ffn_col"][l])
                per = n[0] + ATTENTION_LOADS
                sp.wait_ge(loaded, base + l * per + n[0])
                sp.wait_ge(attn_out, (l + 1) * BATCHES)
                gate(sp)
                load_attention(l + 1)
                sp.wait_ge(loaded, base + l * per + n[0])
                gate(sp)
                assert (base, n[0], per) == (LOADED_AHEAD, per, ATTENTION_LOADS + FFN_LOADS)
            n[0] = base + LAYERS * per
            barrier(sp, PH_LAYERS)
            barrier(sp, PH_MOE2)
            barrier(sp, PH_MOE2 + 1)
            barrier(sp, PH_CAUSAL1)
            load_router("L1")
            load_experts("L1")
            sp.wait_ge(loaded, n[0])
            barrier(sp, PH_CAUSAL1 + 1)
            load(aw[:], d["rec_w"])
            load(fw1[:, 0:8], d["rec_f1"])
            load(fw1[:, 8:16], d["rec_o1"])
            load(fw1[:, 16:32], d["rec_g"])
            load(fw2[0:8, 0, :], d["rec_f2"])
            load(fw2[0:8, 1, :], d["rec_o2"])
            load(fcol[:, 0:1], d["rec_lnw"].rearrange("(p a) -> p a", a=1))
            sp.wait_ge(loaded, n[0])
            barrier(sp, PH_CAUSAL1 + 2)
            barrier(sp, PH_CAUSAL1 + 3)
            with sp.Fori(0, BATCHES) as b:
                sp.wait_ge(R.st_ready, 3 * b + 3 + START)
                sp.wait_ge(R.fg_ready, 2 * b + 2 + START)
                sp.dma_start(scr_k[b], stk).then_inc(R.st_out, 16)
                sp.dma_start(scr_v[b], stv).then_inc(R.st_out, 16)
                sp.dma_start(scr_q[b], stq[:, 0:SEEN]).then_inc(R.st_out, 16)
                sp.dma_start(scr_f[b], stf).then_inc(R.st_out, 16)
                sp.dma_start(scr_g[b], stg[0:HEADS, :]).then_inc(R.st_out, 16)
                sp.wait_ge(R.st_out, 80 * b + 80 + START)
                gate(sp)
            barrier(sp, PH_REC)
            for dst, src, there in ((KD, scr_k, R.k_in), (FD, scr_f, R.scan_in), (VD, scr_v, R.scan_in),
                                    (QD, scr_q, R.scan_in)):
                sp.dma_start(dst, src.rearrange("b (h k) t -> (b h) k t", k=HD)).then_inc(there, 16)
            sp.dma_start(G1, scr_g.rearrange("b h t -> (b h) t")).then_inc(R.scan_in, 16)
            sp.wait_ge(R.od_ready, 1)
            sp.dma_start(scr_o.rearrange("b (h k) t -> (b h) k t", k=HD), OD).then_inc(R.o_out, 16)
            sp.wait_ge(R.o_out, 16)
            sp.dma_start(OF, scr_o.rearrange("b p t -> p b t")).then_inc(R.of_in, 16)
            sp.wait_ge(R.of_in, 16)
            barrier(sp, PH_REC + 1)
            barrier(sp, PH_REC + 2)
            load(aw[:], d["attn_w"][LAYERS])
            sp.wait_ge(loaded, n[0])
            for k in range(4):
                barrier(sp, PH_CAUSAL2 + k)
            sp.dma_start(out.rearrange("b (i p) f -> p (b i) f", p=P), X[:]).then_inc(stored, 16)
            sp.wait_ge(stored, 16)

        @block.gpsimd
        def _(pool):
            chain = Chain(pool, g_chain)
            norms = Tally()

            pool.memset(ident[:], 0.0).then_inc(const_ready, 1)
            pool.memset(mask_win[:], 0.0).then_inc(const_ready, 1)
            pool.memset(mask_win0[:, 0:P - 1], BIG).then_inc(const_ready, 1)
            pool.memset(mask_win0[:, P - 1:], 0.0).then_inc(const_ready, 1)
            pool.memset(mask_cau[:], 0.0).then_inc(const_ready, 1)
            pool.memset(zero[:], 0.0).then_inc(const_ready, 1)

            def constant_parts():
                for k in Ke:
                    pool.memset(k, 0.0).then_inc(const_ready, 1)
                for v in Vx:
                    pool.memset(v[:, :, :, HD:], 1.0).then_inc(const_ready, 1)

            constant_parts()
            pool.wait_ge(const_ready, 10)
            pool.affine_select(out=ident[:], in_=ident[:], compare_op=ALU.not_equal, fill=1.0, base=0,
                               pattern=[[-1, P]], channel_multiplier=1).then_inc(const_ready, 1)
            m = mask_win[:, 0:P]
            pool.affine_select(out=m, in_=m, compare_op=ALU.is_ge, fill=BIG, base=PAST - P,
                               pattern=[[1, P]], channel_multiplier=-1).then_inc(const_ready, 1)
            m = mask_win0[:, P - 1:P]
            pool.affine_select(out=m, in_=m, compare_op=ALU.is_ge, fill=BIG, base=PAST - 1,
                               pattern=[[0, 1]], channel_multiplier=-1).then_inc(const_ready, 1)
            for m in (mask_win[:, P:], mask_win0[:, P:], mask_cau[:, TOKENS - P:]):
                pool.affine_select(out=m, in_=m, compare_op=ALU.is_ge, fill=BIG, base=0,
                                   pattern=[[-1, P]], channel_multiplier=1).then_inc(const_ready, 1)
            pool.wait_ge(const_ready, 16)
            gate(pool)

            def rsqrt(n, at=0):
                pool.wait_ge(var_ready, norms.value() + 1)
                gate(pool)
                w, t, y = nv[:, 0:n], nt[:, 0:n], rstd[:, at:at + n]
                chain.add(pool.tensor_scalar(w, mv[:, at:at + n, 1], EPS, None, ALU.add))
                chain.join()
                gate(pool)
                chain.add(pool.tensor_scalar(y.bitcast(I32), w.bitcast(I32), -0.5, MAGIC, ALU.mult, ALU.add))
                for k in range(3):
                    chain.join()
                    chain.link(pool.tensor_tensor(t, y, y, ALU.mult))
                    chain.add(pool.tensor_tensor(t, t, w, ALU.mult))
                    chain.join()
                    gate(pool)
                    chain.link(pool.tensor_scalar(t, t, -0.5, 1.5, ALU.mult, ALU.add))
                    if k < 2:
                        chain.add(pool.tensor_tensor(y, y, t, ALU.mult))
                    else:
                        pool.tensor_tensor(y, y, t, ALU.mult).then_inc(rstd_ready, 1)
                norms.n += 1

            def attention(S, u0, name):
                def rows(b, p):
                    pool.tensor_copy(zs[p], tiles(S.src, b)).then_inc(S.zs_ready, 1)

                if S is cau:
                    rows(0, 0)
                    rows(1, 1)
                with counted_loop(pool, name, BATCHES // 2 - 1, (chain, norms)) as it:
                    for p in range(2):
                        b = 2 * it + p
                        pool.wait_ge(S.zT_done, u0 + b + 1)
                        if S is win:
                            pool.wait_ge(ffn_out, u0 + b + 3)
                        gate(pool)
                        rows(b + 2, p)
                        rsqrt(TPB)
                rsqrt(TPB)
                if S is win:
                    pool.wait_ge(S.zT_done, u0 + BATCHES)
                    for b in range(2):
                        pool.wait_ge(attn_out, u0 + b + 1)
                        gate(pool)
                        pool.tensor_copy(zs[b], tiles(A, b)).then_inc(ffn.x_ready, 1)
                rsqrt(TPB)

            def first_rows():
                for b in range(2):
                    pool.tensor_copy(zs[b], A[:, TPB * b:TPB * (b + 1), :]).then_inc(win.zs_ready, 1)

            def expert_main(S, v0, name, roots):
                def rows(b, p):
                    if S is moe:
                        pool.tensor_copy(Cs[p], tiles(C, b))
                    pool.tensor_copy(zs[p], tiles(S.src, b)).then_inc(S.x_ready, 1)

                if S is moe:
                    rows(0, 0)
                    rows(1, 1)
                with counted_loop(pool, name, BATCHES // 2 - 1, (chain, norms)) as it:
                    for p in range(2):
                        b = 2 * it + p
                        pool.wait_ge(S.T_done, v0 + b + 1 + START)
                        if S is ffn:
                            pool.wait_ge(attn_out, v0 + b + 3)
                        gate(pool)
                        rows(b + 2, p)
                        for _ in range(roots):
                            rsqrt(TPB, p * TPB)
                for p in range(2):
                    if p and S is ffn:
                        pool.wait_ge(ffn.T_done, v0 + BATCHES + START)
                        pool.wait_ge(ffn_out, v0 + BATCHES + 2)
                        gate(pool)
                        first_rows()
                    for _ in range(roots):
                        rsqrt(TPB, p * TPB)

            for S in (win, cau):
                for s in (S.wo_ev, S.norm_done, S.evac_act, S.evac_dve):
                    pool.sem_inc(s, START)
            for S in (ffn, moe):
                for s in (S.T_done, S.T_ev, S.gelu_done, S.acc_done):
                    pool.sem_inc(s, START)
            pool.sem_inc(ffn_out, BATCHES)
            for s in (yb_ev, R.T_done, R.st_ready, R.fg_ready, R.st_out):
                pool.sem_inc(s, START)
            barrier(pool, PH_SETUP)
            rsqrt(TILES)
            barrier(pool, PH_MOE1)
            expert_main(moe, 0, "pool moe 2", 2)
            barrier(pool, PH_MOE1 + 1)
            barrier(pool, PH_INIT)
            first_rows()
            with counted_loop(pool, "pool layer", LAYERS, (chain, norms)) as l:
                attention(win, l * BATCHES, "pool window")
                expert_main(ffn, l * BATCHES, "pool ffn", 1)
            barrier(pool, PH_LAYERS)
            rsqrt(TILES)
            barrier(pool, PH_MOE2)
            expert_main(moe, BATCHES, "pool moe 2", 2)
            barrier(pool, PH_MOE2 + 1)

            def causal_block(use, ph):
                if use:
                    rsqrt(TILES)
                    rsqrt(TILES)
                barrier(pool, ph)
                attention(cau, use * BATCHES, "pool causal")
                barrier(pool, ph + 1)
                barrier(pool, ph + 2)
                expert_main(moe, (2 + use) * BATCHES, "pool moe 0" if use else "pool moe 1", 1 - use)
                barrier(pool, ph + 3)

            causal_block(0, PH_CAUSAL1)
            with pool.Fori(0, BATCHES) as b:
                pool.wait_ge(R.T_done, b + START)
                pool.wait_ge(R.h_ready, 1)
                gate(pool)
                pool.tensor_copy(zs[0], tiles(H, b)).then_inc(R.x_ready, 1)
            barrier(pool, PH_REC)
            half = STEP_RING // 2
            pool.wait_ge(R.scan_in, 64)
            pool.wait_ge(R.step, 1)
            gate(pool)
            with pool.Fori(0, TOKENS // STEP_RING) as it:
                for c in range(2):
                    pool.wait_ge(R.step, STEP_RING * it + half * c + 1)
                    gate(pool)
                    t0 = STEP_RING * it + half * c
                    slot = KV[:, half * c:half * (c + 1)]
                    vv = VD[:, :, bass.ds(t0, half)].rearrange("p v t -> p t v").unsqueeze(3)\
                        .broadcast_to([P, half, HD, HD])
                    kk = KW[:, bass.ds(t0, half), 0, :].unsqueeze(2).broadcast_to([P, half, HD, HD])
                    pool.tensor_tensor(slot, vv, kk, ALU.mult).then_inc(R.kv_ready, 1)
            barrier(pool, PH_REC + 1)
            barrier(pool, PH_REC + 2)
            constant_parts()
            causal_block(1, PH_CAUSAL2)

        @block.tensor
        def _(pe):
            def turn_rows(bank, rows, done):
                for i in range(TPB):
                    m = pe.transpose(ps[:, bank, i * P:(i + 1) * P], rows[:, i, :], ident[:])
                m.then_inc(done, 1)

            def attention(S, u0):
                G = len(S.groups)
                units = S.units
                n = len(units)

                def prep_turn(b, p):
                    pe.wait_ge(S.zs_ready, u0 + b + 1)
                    turn_rows(7, zs[p], S.zT_done)

                def prep_queries(b, p):
                    pe.wait_ge(S.zT_ev, u0 + b + 1)
                    pe.matmul(ps[:, 7, :], aw[:, 0, :], zT[p], start=True, stop=True).then_inc(S.q_done, 1)

                def prep_keys(b, p):
                    pe.wait_ge(S.q_ev, u0 + b + 1)
                    pe.matmul(ps[:, 7, :], aw[:, 1, :], zT[p], start=True, stop=True).then_inc(S.k_done, 1)

                def prep_values(b, p):
                    pe.wait_ge(S.k_ev, u0 + b + 1)
                    for i in range(TPB):
                        m = pe.matmul(ps[:, 7, i * P:(i + 1) * P], zT[p][:, i * P:(i + 1) * P],
                                      aw[:, 2, :], start=(i == 0), stop=(i == TPB - 1),
                                      skip_group_check=True)
                    m.then_inc(S.v_done, 1)

                def post_turn(b, p):
                    pe.wait_ge(S.norm_done, (u0 + b + 1) * TPB + START)
                    turn_rows(7, On[p], S.oT_done)

                def post_project(b):
                    pe.wait_ge(S.oT_ev, u0 + b + 1)
                    for i in range(TPB):
                        m = pe.matmul(ps[:, 7, i * P:(i + 1) * P], OT[:, i, :], aw[:, 3, :],
                                      start=(i == 0), stop=(i == TPB - 1), skip_group_check=True)
                    m.then_inc(S.wo_done, 1)

                def scores(b, p, k, g):
                    gr = S.groups[k]
                    kw = P * len(gr.blocks)
                    k0 = P * gr.blocks[0]
                    q0 = P * gr.tile
                    pe.wait_ge(S.max_done, ((u0 + b) * G + k) * 4 + g + 1)
                    for j, h in enumerate(gr.heads[g]):
                        m = pe.matmul(ps[:, g, j * kw:(j + 1) * kw], Qe[p][:, h % 4, q0:q0 + P],
                                      Ke[p][:, g, k0:k0 + kw], start=True, stop=True, skip_group_check=True)
                    m.then_inc(S.scores_done, 1)

                def turn_probs(b, p, k, g):
                    gr = S.groups[k]
                    n = ((u0 + b) * G + k) * 4 + g
                    half = ((u0 + b) * G + k) * 2 + g // 2
                    pe.wait_ge(S.exp_done, n + 1)
                    pe.wait_ge(S.evac_dve if g % 2 else S.evac_act, half + START)
                    nb = len(gr.heads[g]) * len(gr.blocks)
                    for c in range(nb):
                        m = pe.transpose(ps[:, 4 + g % 2, c * P:(c + 1) * P],
                                         Pr[:, 4 * (k % 2) + g, c * P:(c + 1) * P], ident[:])
                    m.then_inc(S.t_done, 1)

                def values(b, p, k, g):
                    gr = S.groups[k]
                    tile = (u0 + b) * TPB + gr.tile
                    half = ((u0 + b) * G + k) * 2 + g // 2
                    pe.wait_ge(S.evac_dve if g % 2 else S.evac_act, half + 1 + START)
                    first = g == 0 and (k == 0 or S.groups[k - 1].tile != gr.tile)
                    if first:
                        pe.wait_ge(S.norm_done, tile + START)
                    for j, h in enumerate(gr.heads[g]):
                        for c, blk in enumerate(gr.blocks):
                            cc = j * len(gr.blocks) + c
                            m = pe.matmul(ps[:, 6, h * (HD + 1):(h + 1) * (HD + 1)],
                                          PT[:, g, cc * P:(cc + 1) * P], Vx[p][:, blk, h, :],
                                          start=first and cc == 0, stop=True, skip_group_check=True)
                    if gr.last_of_tile and g == 3:
                        m.then_inc(S.av_done, 1)

                def stage(b, p, first=False, last=False):
                    for s in range(n + (TURN_LAG + 1 if last else 0)):
                        if s == POST_TURN and not first:
                            pe.wait_ge(S.v_ev, u0 + b + 1)
                            post_turn(b - 1, 1 - p)
                        if s == POST_PROJECT and not first:
                            post_project(b - 1)
                        if not last:
                            if s == PREP_TURN:
                                if first:
                                    pe.wait_ge(S.v_ev, u0 + b + 1)
                                else:
                                    pe.wait_ge(S.wo_ev, u0 + b + START)
                                prep_turn(b + 1, 1 - p)
                            if s == PREP_QUERIES:
                                prep_queries(b + 1, 1 - p)
                            if s == PREP_KEYS:
                                prep_keys(b + 1, 1 - p)
                            if s == PREP_VALUES:
                                prep_values(b + 1, 1 - p)
                        if s == 0:
                            pe.wait_ge(S.v_ev, u0 + b + 1)
                            pe.wait_ge(S.pad_done, 2 * (u0 + b) + 2)
                        if s < n:
                            scores(b, p, *units[s])
                        unit = lagged(units, b, p, s, TURN_LAG, first)
                        if unit:
                            turn_probs(*unit)
                        unit = lagged(units, b, p, s, TURN_LAG + 1, first)
                        if unit:
                            values(*unit)

                prep_turn(0, 0)
                prep_queries(0, 0)
                prep_keys(0, 0)
                prep_values(0, 0)
                run_batches(pe, "pe attention", (), stage)
                b = BATCHES - 1
                pe.wait_ge(S.wo_ev, u0 + b + START)
                post_turn(b, 1)
                post_project(b)

            def expert_main(S, v0, W1, W2):
                E = S.experts
                order = [(e, c) for e in range(E) for c in range(CHUNKS)]

                def turn(b, p):
                    pe.wait_ge(S.x_ready, v0 + b + 1)
                    pe.wait_ge(S.T_ev, v0 + b + START)
                    if S is moe:
                        for i in range(TPB):
                            pe.transpose(ps[0:EXPERTS, 6, i * P:(i + 1) * P], Cs[p][:, i, :], ident[:])
                    turn_rows(5, zs[p], S.T_done)

                def biases(b, p):
                    pe.wait_ge(yb_ev, v0 + b + START)
                    for i in range(TPB):
                        m = pe.matmul(ps[:, 7, i * P:(i + 1) * P], cT[p][0:EXPERTS, i * P:(i + 1) * P], eb2[:],
                                      start=(i == 0), stop=(i == TPB - 1), skip_group_check=True)
                    m.then_inc(yb_done, 1)

                def up(b, p, e, c):
                    n = ((v0 + b) * E + e) * CHUNKS + c
                    if e == 0 and c == 0:
                        pe.wait_ge(S.T_ev, v0 + b + 1 + START)
                    pe.wait_ge(S.gelu_done, n + START)
                    pe.matmul(ps[:, c % 2, :], W1(e)[:, c * P:(c + 1) * P], zT[p], start=True, stop=True)\
                        .then_inc(S.up_done, 1)

                def down(b, p, e, c):
                    n = ((v0 + b) * E + e) * CHUNKS + c
                    pe.wait_ge(S.gelu_done, n + 2 + START)
                    if c == 0:
                        pe.wait_ge(S.acc_done, (v0 + b) * E + e + START)
                    for i in range(TPB):
                        m = pe.matmul(ps[:, 2 + (p * E + e) % 2, i * P:(i + 1) * P],
                                      hid[c % 2][:, i * P:(i + 1) * P], W2(e)[:, c, :],
                                      start=(c == 0 and i == 0), stop=(c == CHUNKS - 1),
                                      skip_group_check=True)
                    if c == CHUNKS - 1:
                        m.then_inc(S.y_done, 1)

                def stage(b, p, first=False, last=False):
                    for s, (e, c) in enumerate(order):
                        up(b, p, e, c)
                        if s == 1 and not last:
                            turn(b + 1, 1 - p)
                        if s == 2 and S is moe:
                            biases(b, p)
                        if s:
                            down(b, p, *order[s - 1])
                        elif not first:
                            down(b - 1, 1 - p, *order[-1])

                turn(0, 0)
                run_batches(pe, "pe experts", (), stage)
                down(BATCHES - 1, 1, *order[-1])

            def expert_pre(v0):
                def logits(b):
                    pe.wait_ge(pT_ev, v0 + b + 1)
                    for t in range(TPB * b, TPB * (b + 1)):
                        m = pe.matmul(ps[:, 6, t * EXPERTS:(t + 1) * EXPERTS],
                                      zT[b % 2][:, t % TPB * P:(t % TPB + 1) * P], gate_w[:],
                                      start=(t == 0), stop=(t == TILES - 1), skip_group_check=True)
                    return m

                for b in range(BATCHES):
                    pe.wait_ge(h_ready, v0 + b + 1)
                    if b >= 2:
                        pe.wait_ge(pT_ev, v0 + b - 1)
                    turn_rows(5 + 2 * (b % 2), H[:, TPB * b:TPB * (b + 1), :], pT_done)
                    if b:
                        logits(b - 1)
                logits(BATCHES - 1).then_inc(lg_done, 1)

            E1, E2 = (lambda e: w1[:, e, :]), (lambda e: w2[:, e])
            pe.wait_ge(const_ready, 16)
            barrier(pe, PH_SETUP)
            expert_pre(0)
            barrier(pe, PH_MOE1)
            expert_main(moe, 0, E1, E2)
            barrier(pe, PH_MOE1 + 1)
            barrier(pe, PH_INIT)
            with pe.Fori(0, LAYERS) as l:
                pe.wait_ge(loaded, attention_loaded(l))
                pe.wait_ge(ffn.acc_done, l * BATCHES + 1 + START)
                pe.wait_ge(win.wo_ev, l * BATCHES + START)
                attention(win, l * BATCHES)
                pe.wait_ge(loaded, attention_loaded(l) + FFN_LOADS)
                expert_main(ffn, l * BATCHES, lambda e: fw1[:], lambda e: fw2[:])
            barrier(pe, PH_LAYERS)
            expert_pre(BATCHES)
            barrier(pe, PH_MOE2)
            expert_main(moe, BATCHES, E1, E2)
            barrier(pe, PH_MOE2 + 1)

            def causal_block(use, ph):
                barrier(pe, ph)
                attention(cau, use * BATCHES)
                barrier(pe, ph + 1)
                expert_pre((2 + use) * BATCHES)
                barrier(pe, ph + 2)
                expert_main(moe, (2 + use) * BATCHES, E1, E2)
                barrier(pe, ph + 3)

            causal_block(0, PH_CAUSAL1)
            with pe.Fori(0, BATCHES) as b:
                pe.wait_ge(R.x_ready, b + 1)
                turn_rows(5, zs[0], R.T_done)
                pe.wait_ge(R.T_ev, b + 1)
                pe.wait_ge(R.st_ready, 3 * b + START)
                pe.wait_ge(R.fg_ready, 2 * b + START)
                pe.matmul(ps[:, 0, :], aw[:, 1, :], zT[0], start=True, stop=True).then_inc(R.kvqg_done, 1)
                pe.matmul(ps[:, 1, :], aw[:, 2, :], zT[0], start=True, stop=True).then_inc(R.kvqg_done, 1)
                pe.matmul(ps[:, 2, 0:SEEN], aw[:, 0, :], zT[0][:, TOKENS - SEEN:], start=True, stop=True)\
                    .then_inc(R.kvqg_done, 1)
                pe.matmul(ps[0:8, 3, :], fw1[:, 0:8], zT[0], start=True, stop=True).then_inc(R.kvqg_done, 1)
                pe.matmul(ps[0:8, 4, 0:OUT], fw1[:, 8:16], zT[0][:, 1::3], start=True, stop=True)\
                    .then_inc(R.kvqg_done, 1)
                pe.matmul(ps[0:HEADS, 6, :], fw1[:, 16:32], zT[0], start=True, stop=True).then_inc(R.kvqg_done, 1)
                pe.wait_ge(R.f1_ev, b + 1)
                pe.matmul(ps[:, 3, :], fw2[0:8, 0, :], f1s[0:8, :], start=True, stop=True).then_inc(R.f_done, 1)
                pe.wait_ge(R.g1_ev, b + 1)
                pe.matmul(ps[:, 7, 0:OUT], fw2[0:8, 1, :], g1s[0:8, 0:OUT], start=True, stop=True)\
                    .then_inc(R.gate_done, 1)
            barrier(pe, PH_REC)
            barrier(pe, PH_REC + 1)
            for src, ready, done, bank in ((O1, R.o1_ready, R.mean_done, 0), (O3, R.sq_ready, R.msq_done, 4)):
                pe.wait_ge(ready, 1)
                for k in range(4):
                    m = pe.matmul(ps[:, bank + k, 0:2 * OUT], ones[:], src[:, 2 * k:2 * k + 2, :]
                                  .rearrange("p a b -> p (a b)"), start=True, stop=True)
                m.then_inc(done, 1)
            pe.wait_ge(R.ex_ready, 1)
            for b in range(BATCHES):
                if b >= 2:
                    pe.wait_ge(R.x_done, b - 1)
                for i in range(TPB):
                    m = pe.matmul(ps[:, b % 2, i * P:(i + 1) * P], EX[:, b, i * P:(i + 1) * P], aw[:, 3, :],
                                  start=(i == 0), stop=(i == TPB - 1), skip_group_check=True)
                m.then_inc(R.y_done, 1)
            barrier(pe, PH_REC + 2)
            causal_block(1, PH_CAUSAL2)

        @block.scalar
        def _(act):
            chain = Chain(act, a_chain)
            copy, exp, gelu, sigmoid = ACT.Copy, ACT.Exp, ACT.Gelu, ACT.Sigmoid
            act.sem_inc(win.max_done, 4)
            act.sem_inc(cau.max_done, 4)
            act.sem_inc(ffn.gelu_done, 1)
            act.sem_inc(moe.gelu_done, 1)

            def attention(S, u0):
                G = len(S.groups)
                units = S.units
                n = len(units)

                def prep_turn(b, p):
                    act.wait_ge(S.zT_done, u0 + b + 1)
                    act.activation(zT[p], ps[:, 7, :], copy).then_inc(S.zT_ev, 1)

                def prep_keys(b, p):
                    act.wait_ge(S.k_done, u0 + b + 1)
                    for g in range(4):
                        rows = slice(32 * g, 32 * g + 32)
                        m = act.activation(Ke[p][rows, g, P:], ps[rows, 7, :], ACT.Identity,
                                           bias=acol[rows, 1:2])
                    m.then_inc(S.k_ev, 1)

                def prep_pad(p):
                    for g in range(4):
                        rows = slice(32 * g, 32 * g + 32)
                        m = act.activation(Ke[p][rows, g, 0:P], zero[rows, :], ACT.Identity,
                                           bias=acol[rows, 1:2])
                    m.then_inc(S.pad_done, 1)

                def post_turn(b):
                    act.wait_ge(S.oT_done, u0 + b + 1)
                    act.activation(OT.rearrange("p a b -> p (a b)"), ps[:, 7, :], copy).then_inc(S.oT_ev, 1)

                def probs(b, p, k, g):
                    gr = S.groups[k]
                    kw = P * len(gr.blocks)
                    act.wait_ge(S.max_done, ((u0 + b) * G + k) * 4 + g + 5)
                    slot = 4 * (k % 2) + g
                    for j in range(len(gr.heads[g])):
                        m = act.activation(Pr[:, slot, j * kw:(j + 1) * kw], Pr[:, slot, j * kw:(j + 1) * kw],
                                           exp, bias=nmax[:, slot, j:j + 1], scale=-1.0)
                    m.then_inc(S.exp_done, 1)

                def evac(b, p, k, g):
                    gr = S.groups[k]
                    act.wait_ge(S.t_done, ((u0 + b) * G + k) * 4 + g + 1)
                    w = P * len(gr.blocks) * len(gr.heads[g])
                    act.activation(PT[:, g, 0:w], ps[:, 4 + g % 2, 0:w], copy).then_inc(S.evac_act, 1)

                def stage(b, p, first=False, last=False):
                    for s in range(n + (TURN_LAG if last else 0)):
                        if s == POST_TURN + 1 and not first:
                            post_turn(b - 1)
                        if s == PREP_TURN + 1 and not last:
                            prep_turn(b + 1, 1 - p)
                        if s == PREP_KEYS + 1 and not last:
                            prep_keys(b + 1, 1 - p)
                        if s == PREP_KEYS + 3 and not last:
                            prep_pad(1 - p)
                        unit = lagged(units, b, p, s, TURN_LAG, first)
                        if unit and unit[3] % 2 == 0:
                            evac(*unit)
                        if s < n:
                            probs(b, p, *units[s])

                prep_turn(0, 0)
                prep_keys(0, 0)
                prep_pad(0)
                run_batches(act, "act attention", (), stage)
                post_turn(BATCHES - 1)

            def expert_main(S, v0, b1):
                E = S.experts

                def turn(b, p):
                    act.wait_ge(S.T_done, v0 + b + 1 + START)
                    if S is moe:
                        act.activation(cT[p][0:EXPERTS, :], ps[0:EXPERTS, 6, :], copy)
                    act.activation(zT[p], ps[:, 5, :], copy).then_inc(S.T_ev, 1)

                def stage(b, p, first=False, last=False):
                    for e in range(E):
                        for c in range(CHUNKS):
                            act.wait_ge(S.up_done, ((v0 + b) * E + e) * CHUNKS + c + 1)
                            act.activation(hid[c % 2], ps[:, c % 2, :], gelu, bias=b1(e)[:, c:c + 1])\
                                .then_inc(S.gelu_done, 1)
                            if (e, c) == (0, 1) and not last:
                                turn(b + 1, 1 - p)

                turn(0, 0)
                run_batches(act, "act experts", (), stage)

            def expert_pre(v0):
                for b in range(BATCHES):
                    act.wait_ge(pT_done, v0 + b + 1)
                    act.activation(zT[b % 2], ps[:, 5 + 2 * (b % 2), :], copy).then_inc(pT_ev, 1)
                act.wait_ge(d_ready, v0 // BATCHES + 1)
                act.activation(rt[1][:], rt[0][:], exp).then_inc(e_ready, 1)

            B1 = lambda e: eb1[:, e, :]
            barrier(act, PH_SETUP)
            expert_pre(0)
            barrier(act, PH_MOE1)
            expert_main(moe, 0, B1)
            barrier(act, PH_MOE1 + 1)
            barrier(act, PH_INIT)
            with act.Fori(0, LAYERS) as l:
                act.wait_ge(loaded, attention_loaded(l))
                gate(act)
                attention(win, l * BATCHES)
                act.wait_ge(loaded, attention_loaded(l) + FFN_LOADS)
                gate(act)
                expert_main(ffn, l * BATCHES, lambda e: fcol[:])
            barrier(act, PH_LAYERS)
            expert_pre(BATCHES)
            barrier(act, PH_MOE2)
            expert_main(moe, BATCHES, B1)
            barrier(act, PH_MOE2 + 1)

            def causal_block(use, ph):
                barrier(act, ph)
                attention(cau, use * BATCHES)
                barrier(act, ph + 1)
                expert_pre((2 + use) * BATCHES)
                barrier(act, ph + 2)
                expert_main(moe, (2 + use) * BATCHES, B1)
                barrier(act, ph + 3)

            causal_block(0, PH_CAUSAL1)
            with act.Fori(0, BATCHES) as b:
                act.wait_ge(R.kvqg_done, 6 * b + 3)
                act.wait_ge(R.st_out, 80 * b + START)
                for s, bank, w in ((sgk, 0, TOKENS), (sgv, 1, TOKENS), (sgq, 2, SEEN)):
                    act.activation(s[:, 0:w], ps[:, bank, 0:w], sigmoid).then_inc(R.sg_ready, 1)
                act.wait_ge(R.kvqg_done, 6 * b + 6)
                act.activation(stg[0:HEADS, :], ps[0:HEADS, 6, :], sigmoid).then_inc(R.fg_ready, 1)
                act.wait_ge(R.gate_done, b + 1)
                gate(act)
                act.activation(GATE[:, b, :], ps[:, 7, 0:OUT], sigmoid)
                act.wait_ge(R.f_done, b + 1)
                act.activation(stf, ps[:, 3, :], sigmoid).then_inc(R.fg_ready, 1)
            barrier(act, PH_REC)
            half = STEP_RING // 2
            act.wait_ge(R.step, 1)
            gate(act)
            with act.Fori(0, TOKENS // STEP_RING) as it:
                for c in range(2):
                    act.wait_ge(R.step, STEP_RING * it + half * c + 1)
                    gate(act)
                    t0 = STEP_RING * it + half * c
                    ring = slice(half * c, half * (c + 1))
                    act.activation(KWs[:, ring], KW[:, bass.ds(t0, half)], copy)
                    act.activation(UAs[:, ring], UA[:, bass.ds(t0, half)], copy)
                    act.activation(Fs[:, ring], FD[:, :, bass.ds(t0, half)].rearrange("p k t -> p t k"), copy)\
                        .then_inc(R.staged, 1)
            barrier(act, PH_REC + 1)
            barrier(act, PH_REC + 2)
            causal_block(1, PH_CAUSAL2)

        @block.vector
        def _(dve):
            chain = Chain(dve, v_chain)
            norms = Tally()
            for S in (ffn, moe):
                dve.sem_inc(S.acc_done, 1)

            def norm_stats(get, n, at=0):
                gate(dve)
                for t in range(n):
                    chain.add(dve.bn_stats(stats[:, at + t, :], get(t)))
                chain.join()
                gate(dve)
                for t in range(n):
                    m = dve.bn_aggr(mv[:, at + t, :], stats[:, at + t, :])
                m.then_inc(var_ready, 1)

            def norm_wait():
                dve.wait_ge(rstd_ready, norms.value() + 1)
                gate(dve)
                norms.n += 1

            def norm_apply(dst, get, n, at=0):
                for t in range(n):
                    chain.add(dve.tensor_scalar(dst(t), get(t), mv[:, at + t, 0:1], rstd[:, at + t:at + t + 1],
                                                ALU.subtract, ALU.mult))
                chain.join()

            def affine(dst, src, g, b):
                chain.link(dve.tensor_tensor(dst, src, row(g), ALU.mult))
                return dve.tensor_tensor(dst, dst, row(b), ALU.add)

            def norm_all(src, dst):
                norm_stats(lambda t: src[:, t, :], TILES)
                norm_wait()
                norm_apply(lambda t: dst[:, t, :], lambda t: src[:, t, :], TILES)

            def attention(S, u0, name):
                G = len(S.groups)
                units = S.units
                n = len(units)

                def prep_queries(b, p, slots):
                    dve.wait_ge(S.q_done, u0 + b + 1)
                    for j in slots:
                        m = dve.tensor_scalar(Qe[p][:, j, :], ps[:, 7, :], acol[:, 0:1], hm[:, j:j + 1],
                                              ALU.add, ALU.mult)
                    if slots[-1] == 3:
                        m.then_inc(S.q_ev, 1)

                def prep_values(b, p):
                    bv = arow[:, 0, :].rearrange("p (h k) -> p h k", k=HD)
                    dve.wait_ge(S.v_done, u0 + b + 1)
                    dve.tensor_tensor(Vx[p][:, 1:, :, 0:HD],
                                      ps[:, 7, :].rearrange("p (i h k) -> p i h k", h=HEADS, k=HD),
                                      bv.unsqueeze(1).broadcast_to([P, TPB, HEADS, HD]), ALU.add)\
                        .then_inc(S.v_ev, 1)
                    dve.tensor_tensor(Vx[p][:, 0, :, 0:HD], bv,
                                      zero[:].rearrange("p (h k) -> p h k", k=HD), ALU.add).then_inc(S.pad_done, 1)

                def post_add(b):
                    x = tiles(A, b)
                    dve.wait_ge(S.wo_done, u0 + b + 1)
                    dve.tensor_tensor(x, ps[:, 7, :].rearrange("p (i k) -> p i k", k=P), x, ALU.add)\
                        .then_inc(S.wo_ev, 1)
                    dve.wait_ge(S.wo_ev, u0 + b + 1 + START)
                    chain.link(dve.tensor_tensor(x, x, row(arow[:, 1, :]), ALU.add))

                normed = A if S is win else H
                gain, bias = (arow[:, 2, :], arow[:, 3, :]) if S is win else (crow[:, 2, :], crow[:, 3, :])

                def post_share(b):
                    if S is cau:
                        gate(dve)
                        chain.link(dve.scalar_tensor_tensor(out=tiles(X, b), in0=tiles(A, b), scalar=0.5,
                                                            in1=tiles(X, b), op0=ALU.mult, op1=ALU.add))

                def post_stats(b):
                    norm_stats(lambda t: A[:, b * TPB + t, :], TPB)

                def post_apply(b):
                    norm_wait()
                    norm_apply(lambda t: normed[:, b * TPB + t, :], lambda t: A[:, b * TPB + t, :], TPB)

                def post_gain(b):
                    x = tiles(normed, b)
                    chain.link(dve.tensor_tensor(x, x, row(gain), ALU.mult))

                def post_bias(b):
                    x = tiles(normed, b)
                    dve.tensor_tensor(x, x, row(bias), ALU.add).then_inc(attn_out if S is win else h_ready, 1)

                posts = {POST_PROJECT + 1: post_add, POST_PROJECT + 2: post_stats, POST_PROJECT + 6: post_apply,
                         POST_PROJECT + 10: post_gain, POST_PROJECT + 12: post_bias,
                         POST_PROJECT + 13: post_share}

                def maxima(b, p, k, g):
                    gr = S.groups[k]
                    kw = P * len(gr.blocks)
                    nh = len(gr.heads[g])
                    dve.wait_ge(S.scores_done, ((u0 + b) * G + k) * 4 + g + 1)
                    gate(dve)
                    slot = 4 * (k % 2) + g
                    if gr.windowed:
                        mask = mask_win0[:] if gr.first else mask_win[:]
                    else:
                        mask = mask_cau[:, TOKENS - kw:]
                    for j in range(nh):
                        m = dve.tensor_tensor_reduce(out=Pr[:, slot, j * kw:(j + 1) * kw],
                                                     in0=ps[:, g, j * kw:(j + 1) * kw], in1=mask,
                                                     scale=1.0, scalar=NO_SCORE, op0=ALU.add, op1=ALU.min,
                                                     accum_out=nmax[:, slot, j:j + 1])
                    m.then_inc(S.max_done, 1)

                def evac(b, p, k, g):
                    gr = S.groups[k]
                    dve.wait_ge(S.t_done, ((u0 + b) * G + k) * 4 + g + 1)
                    w = P * len(gr.blocks) * len(gr.heads[g])
                    dve.tensor_copy(PT[:, g, 0:w], ps[:, 4 + g % 2, 0:w]).then_inc(S.evac_dve, 1)

                def normalise(b, p, i):
                    dve.wait_ge(S.av_done, (u0 + b) * TPB + i + 1)
                    o = ps[:, 6, 0:HEADS * (HD + 1)].rearrange("p (h k) -> p h k", k=HD + 1)
                    chain.link(dve.reciprocal(orec[:], o[:, :, HD]))
                    dve.tensor_tensor(On[p][:, i, :].rearrange("p (h k) -> p h k", k=HD), o[:, :, 0:HD],
                                      orec[:].unsqueeze(2).broadcast_to([P, HEADS, HD]), ALU.mult)\
                        .then_inc(S.norm_done, 1)

                def stage(b, p, first=False, last=False):
                    for s in range(n + (TURN_LAG + 3 if last else 0)):
                        if s in posts and not first:
                            posts[s](b - 1)
                        if not last:
                            if s == PREP_QUERIES + 1:
                                prep_queries(b + 1, 1 - p, (0, 1))
                            if s == PREP_QUERIES + 2:
                                prep_queries(b + 1, 1 - p, (2, 3))
                            if s == PREP_VALUES + 1:
                                prep_values(b + 1, 1 - p)
                        unit = lagged(units, b, p, s, TURN_LAG + 2, first)
                        if unit and unit[3] == 3 and S.groups[unit[2]].last_of_tile:
                            normalise(unit[0], unit[1], S.groups[unit[2]].tile)
                        if s < n:
                            maxima(b, p, *units[s])
                        unit = lagged(units, b, p, s, TURN_LAG, first)
                        if unit and unit[3] % 2:
                            evac(*unit)

                prep_queries(0, 0, (0, 1, 2, 3))
                prep_values(0, 0)
                run_batches(dve, name, (chain, norms), stage)
                for step in posts.values():
                    step(BATCHES - 1)

            def feed_forward(v0):
                S = ffn

                def apply(b, p):
                    x = tiles(A, b)
                    norm_wait()
                    norm_apply(lambda t: A[:, b * TPB + t, :], lambda t: A[:, b * TPB + t, :], TPB, p * TPB)
                    affine(x, x, frow[:, 1, :], frow[:, 2, :]).then_inc(ffn_out, 1)

                def stage(b, p, first=False, last=False):
                    x = tiles(A, b)
                    dve.wait_ge(S.y_done, v0 + b + 1)
                    dve.tensor_tensor(x, ps[:, 2 + p, :].rearrange("p (i k) -> p i k", k=P), x, ALU.add)\
                        .then_inc(S.acc_done, 1)
                    dve.wait_ge(S.acc_done, v0 + b + 2 + START)
                    chain.link(dve.tensor_tensor(x, x, row(frow[:, 0, :]), ALU.add))
                    norm_stats(lambda t: A[:, b * TPB + t, :], TPB, p * TPB)
                    if not first:
                        apply(b - 1, 1 - p)

                run_batches(dve, "dve ffn", (chain, norms), stage)
                apply(BATCHES - 1, 1)

            def expert_main(v0, name, follow):
                S = moe

                def stage(b, p, first=False, last=False):
                    for e in range(EXPERTS):
                        n = (v0 + b) * EXPERTS + e
                        dve.wait_ge(S.y_done, n + 1)
                        dve.wait_ge(S.acc_done, n + 1 + START)
                        gate(dve)
                        for i in range(TPB):
                            t = b * TPB + i
                            m = dve.scalar_tensor_tensor(
                                out=X[:, t, :], in0=ps[:, 2 + e % 2, i * P:(i + 1) * P],
                                scalar=C[:, t, e:e + 1], in1=X[:, t, :], op0=ALU.mult, op1=ALU.add)
                        m.then_inc(S.acc_done, 1)
                        if e == 1:
                            dve.wait_ge(yb_done, v0 + b + 1)
                            dve.wait_ge(S.acc_done, n + 2 + START)
                            x = tiles(X, b)
                            dve.tensor_tensor(x, ps[:, 7, :].rearrange("p (i k) -> p i k", k=P), x, ALU.add)\
                                .then_inc(yb_ev, 1)
                            dve.wait_ge(yb_ev, v0 + b + 1 + START)
                            gate(dve)
                        if e in follow and not first:
                            follow[e](b - 1, 1 - p)

                run_batches(dve, name, (chain, norms), stage)
                dve.wait_ge(S.acc_done, (v0 + BATCHES) * EXPERTS + 1 + START)
                for step in follow.values():
                    step(BATCHES - 1, 1)

            def stats_of(src):
                def step(b, p):
                    norm_stats(lambda t: src[:, b * TPB + t, :], TPB, p * TPB)
                return step

            def applied(dst, src):
                def step(b, p):
                    norm_wait()
                    norm_apply(lambda t: dst[:, b * TPB + t, :], lambda t: src[:, b * TPB + t, :], TPB, p * TPB)
                return step

            def affine_by(dst, rows, k, more=None):
                def step(b, p):
                    x = tiles(dst, b)
                    chain.link(affine(x, x, rows[:, k, :], rows[:, k + 1, :]))
                    if more is not None:
                        chain.link(dve.tensor_tensor(x, x, more, ALU.add))
                return step

            def expert_pre(v0, first):
                use = v0 // BATCHES
                top1 = use < 2
                if top1:
                    if not first:
                        chain.link(dve.tensor_tensor(X[:], X[:], A, ALU.add))
                    norm_stats(lambda t: X[:, t, :], TILES)
                    norm_wait()
                    for b in range(BATCHES):
                        t0 = TPB * b
                        norm_apply(lambda t: H[:, t0 + t, :], lambda t: X[:, t0 + t, :], TPB, t0)
                        dve.engine_nop().then_inc(h_ready, 1)
                dve.wait_ge(lg_done, use + 1)
                lg = ps[:, 6, 0:TILES * EXPERTS].rearrange("p (a b) -> p a b", b=EXPERTS)
                if top1:
                    chain.link(dve.tensor_copy(LG[:], lg))
                else:
                    chain.link(dve.tensor_tensor(LG[:], lg, brow[:].unsqueeze(1)
                                                 .broadcast_to([P, TILES, EXPERTS]), ALU.add))
                wide = lambda a: a[:].unsqueeze(2).broadcast_to([P, TILES, EXPERTS])
                chain.link(dve.tensor_reduce(r1[:], LG[:], AX_X, ALU.max))
                dve.tensor_tensor(rt[0][:], LG[:], wide(r1), ALU.subtract).then_inc(d_ready, 1)
                chain.link(dve.tensor_tensor(rt[2][:], LG[:], wide(r1), ALU.is_equal))
                chain.link(dve.tensor_tensor(rt[2][:], rt[2][:], rev[:].unsqueeze(1)
                                             .broadcast_to([P, TILES, EXPERTS]), ALU.mult))
                chain.link(dve.tensor_reduce(r2[:], rt[2][:], AX_X, ALU.max))
                chain.link(dve.tensor_tensor(rt[3][:], rt[2][:], wide(r2), ALU.is_equal))
                dve.wait_ge(e_ready, use + 1)
                if top1:
                    chain.link(dve.tensor_reduce(r1[:], rt[1][:], AX_X, ALU.add))
                    chain.link(dve.reciprocal(r2[:], r1[:]))
                else:
                    chain.link(dve.scalar_tensor_tensor(out=rt[2][:], in0=rt[3][:], scalar=-BIG, in1=LG[:],
                                                        op0=ALU.mult, op1=ALU.add))
                    chain.link(dve.tensor_reduce(r2[:], rt[2][:], AX_X, ALU.max))
                    chain.link(dve.tensor_tensor(rt[2][:], LG[:], wide(r2), ALU.is_ge))
                    chain.link(dve.tensor_tensor(rt[3][:], rt[1][:], rt[2][:], ALU.mult))
                    chain.link(dve.tensor_reduce(r1[:], rt[3][:], AX_X, ALU.add))
                    chain.link(dve.reciprocal(r2[:], r1[:]))
                chain.link(dve.tensor_scalar(r1[:], r2[:], 0.5, None, ALU.mult))
                chain.link(dve.tensor_tensor(C[:], rt[3][:], wide(r1), ALU.mult))

            dve.memset(ones[:], 1.0 / P).then_inc(v_chain, 1)
            chain.n += 1
            barrier(dve, PH_SETUP)
            expert_pre(0, True)
            barrier(dve, PH_MOE1)
            expert_main(0, "dve moe input", {0: stats_of(X), 2: applied(A, X), 3: stats_of(A), 5: applied(A, A),
                                         6: affine_by(A, crow, 0, pos[:])})
            barrier(dve, PH_MOE1 + 1)
            barrier(dve, PH_INIT)
            with counted_loop(dve, "dve layer", LAYERS, (chain, norms)) as l:
                dve.wait_ge(loaded, attention_loaded(l))
                gate(dve)
                attention(win, l * BATCHES, "dve window")
                dve.wait_ge(loaded, attention_loaded(l) + FFN_LOADS)
                gate(dve)
                feed_forward(l * BATCHES)
            barrier(dve, PH_LAYERS)
            expert_pre(BATCHES, False)
            barrier(dve, PH_MOE2)
            causal_norms = {0: stats_of(X), 2: applied(A, X), 3: stats_of(A), 5: applied(H, A),
                            6: affine_by(H, arow, 2)}
            expert_main(BATCHES, "dve moe causal", causal_norms)
            barrier(dve, PH_MOE2 + 1)

            def causal_block(use, ph):
                if use:
                    norm_all(X, A)
                    norm_all(A, H)
                    for b in range(BATCHES):
                        affine_by(H, arow, 2)(b, 0)
                barrier(dve, ph)
                attention(cau, use * BATCHES, "dve causal")
                barrier(dve, ph + 1)
                expert_pre((2 + use) * BATCHES, False)
                barrier(dve, ph + 2)
                if use:
                    expert_main((2 + use) * BATCHES, "dve moe last", {})
                else:
                    expert_main((2 + use) * BATCHES, "dve moe rows", {0: stats_of(X), 2: applied(H, X)})
                barrier(dve, ph + 3)

            causal_block(0, PH_CAUSAL1)
            dve.engine_nop().then_inc(R.h_ready, 1)
            with dve.Fori(0, BATCHES) as b:
                dve.wait_ge(R.T_done, b + 1 + START)
                dve.tensor_copy(zT[0], ps[:, 5, :]).then_inc(R.T_ev, 1)
                dve.wait_ge(R.kvqg_done, 6 * b + 4)
                dve.tensor_copy(f1s[0:8, :], ps[0:8, 3, :]).then_inc(R.f1_ev, 1)
                dve.wait_ge(R.kvqg_done, 6 * b + 5)
                dve.tensor_copy(g1s[0:8, 0:OUT], ps[0:8, 4, 0:OUT]).then_inc(R.g1_ev, 1)
                dve.wait_ge(R.st_out, 80 * b + START)
                for n, (s, sg, bank, w) in enumerate(((stk, sgk, 0, TOKENS), (stv, sgv, 1, TOKENS),
                                                      (stq, sgq, 2, SEEN))):
                    dve.wait_ge(R.sg_ready, 3 * b + n + 1)
                    dve.tensor_tensor(s[:, 0:w], ps[:, bank, 0:w], sg[:, 0:w], ALU.mult).then_inc(R.st_ready, 1)
            barrier(dve, PH_REC)
            dve.wait_ge(R.k_in, 16)
            gate(dve)
            by_time = lambda a: a.rearrange("p k t -> p t k")
            over_k = lambda a: a.unsqueeze(1).broadcast_to([P, HD, TOKENS])
            kn, wv, ua, av = KW[:, :, 0, :], KW[:, :, 1, :], UA[:, :, 0, :], UA[:, :, 1, :]
            chain.link(dve.tensor_tensor(TMP, KD, KD, ALU.mult))
            chain.link(dve.tensor_reduce(N2, by_time(TMP), AX_X, ALU.add))
            chain.link(dve.tensor_scalar(N2, N2, 1e-24, None, ALU.max))
            newton(dve, chain, RN, N2, T1)
            chain.link(dve.tensor_tensor(kn.rearrange("p t k -> p k t"), KD, over_k(RN), ALU.mult))
            dve.wait_ge(R.scan_in, 64)
            gate(dve)
            chain.link(dve.tensor_scalar(G1, G1, -1.0, None, ALU.mult))
            chain.link(dve.tensor_tensor(av, kn, G1.unsqueeze(2).broadcast_to([P, TOKENS, HD]), ALU.mult))
            chain.link(dve.tensor_tensor(wv, kn, by_time(FD), ALU.mult))
            chain.link(dve.tensor_tensor(ua, av, by_time(FD), ALU.mult))
            chain.link(dve.tensor_tensor(by_time(TMP), kn, ua, ALU.mult))
            chain.link(dve.tensor_reduce(C1, by_time(TMP), AX_X, ALU.add))
            chain.link(dve.tensor_tensor(by_time(TMP), av, C1.unsqueeze(2).broadcast_to([P, TOKENS, HD]), ALU.mult))
            chain.link(dve.tensor_tensor(ua, ua, by_time(TMP), ALU.add))
            dve.memset(SH[:, STEP_RING - 1], 0.0).then_inc(R.step, 1)
            dve.wait_ge(R.step, 1)
            dve.sem_inc(R.step, STEP_RING // 2)
            half = STEP_RING // 2
            last_turn = TOKENS // STEP_RING
            seen_turn = (TOKENS - SEEN) // STEP_RING
            for lo, hi, name in ((0, seen_turn, "scan"), (seen_turn, last_turn, "scan seen")):
                with counted_loop(dve, name, hi - lo, (chain,)) as i:
                    it = lo + i
                    for j in range(STEP_RING):
                        t = STEP_RING * it + j
                        s = SH[:, (j - 1) % STEP_RING]
                        new = SH[:, j]
                        if j % half == 0:
                            dve.wait_ge(R.kv_ready, 2 * it + j // half + 1)
                            dve.wait_ge(R.staged, 2 * it + j // half + 1)
                            gate(dve)
                        chain.add(dve.tensor_tensor(
                            M1.rearrange("p (a v) k -> p a v k", a=2),
                            s.unsqueeze(1).broadcast_to([P, 2, HD, HD]),
                            KWs[:, j].unsqueeze(2).broadcast_to([P, 2, HD, HD]), ALU.mult))
                        chain.add(dve.tensor_tensor(
                            FS, s, Fs[:, j].unsqueeze(1).broadcast_to([P, HD, HD]), ALU.mult))
                        dve.wait_ge(v_chain, chain.value() - 1)
                        chain.add(dve.tensor_reduce(XY.rearrange("p a b -> p (a b)"), M1, AX_X, ALU.add))
                        dve.wait_ge(v_chain, chain.value() - 1)
                        chain.add(dve.tensor_tensor(
                            MJ[:, :, 0].rearrange("p (v k) -> p v k", k=HD), FS, KV[:, j], ALU.add))
                        dve.wait_ge(v_chain, chain.value() - 1)
                        chain.link(dve.tensor_tensor(
                            MJ[:, :, 1:3].rearrange("p (v k) r -> p r v k", k=HD),
                            UAs[:, j].unsqueeze(2).broadcast_to([P, 2, HD, HD]),
                            XY.unsqueeze(3).broadcast_to([P, 2, HD, HD]), ALU.mult))
                        dve.tensor_reduce(new.rearrange("p v k -> p (v k)"), MJ, AX_X, ALU.add).then_inc(R.step, 1)
                        dve.wait_ge(R.step, t + 2 + STEP_RING // 2)
                    if lo:
                        q = QD[:, :, bass.ds(STEP_RING * i, STEP_RING)].rearrange("p k t -> p t k").unsqueeze(2)\
                            .broadcast_to([P, STEP_RING, HD, HD])
                        chain.link(dve.tensor_tensor(OQ, SH, q, ALU.mult))
                        gate(dve)
                        chain.link(dve.tensor_reduce(
                            OD[:, :, bass.ds(STEP_RING * i, STEP_RING)].rearrange("p v t -> p t v"),
                            OQ, AX_X, ALU.add))
            dve.engine_nop().then_inc(R.od_ready, 1)
            barrier(dve, PH_REC + 1)
            half_banks = lambda b0: ps[:, b0:b0 + 4, 0:2 * OUT]
            quad = lambda a: a.rearrange("p (c a) b -> p c (a b)", a=2)
            dve.tensor_tensor(O1, OF[:, :, SEEN - OUT:], GATE, ALU.mult).then_inc(R.o1_ready, 1)
            chain.link(dve.memset(EX, 0.0))
            dve.wait_ge(R.o1_ready, 1)
            dve.wait_ge(R.mean_done, 1)
            chain.link(dve.tensor_tensor(quad(O2), quad(O1), half_banks(0), ALU.subtract))
            dve.tensor_tensor(O3, O2, O2, ALU.mult).then_inc(R.sq_ready, 1)
            dve.wait_ge(R.msq_done, 1)
            chain.link(dve.tensor_scalar(quad(O1), half_banks(4), EPS, None, ALU.add))
            flat = lambda a: a.rearrange("p a b -> p (a b)")
            newton(dve, chain, flat(O4), flat(O1), flat(O3))
            dve.scalar_tensor_tensor(out=EX[:, :, 1::3], in0=O2, scalar=fcol[:, 0:1], in1=O4,
                                     op0=ALU.mult, op1=ALU.mult).then_inc(R.ex_ready, 1)
            for b in range(BATCHES):
                dve.wait_ge(R.y_done, b + 1)
                x = X[:, TPB * b:TPB * (b + 1), :]
                dve.tensor_tensor(x, ps[:, b % 2, :].rearrange("p (i k) -> p i k", k=P), x, ALU.add)\
                    .then_inc(R.x_done, 1)
            barrier(dve, PH_REC + 2)
            causal_block(1, PH_CAUSAL2)

    if wrong:
        raise AssertionError(f"PER_TURN: {wrong}")


def newton(eng, chain, y, w, t):
    chain.link(eng.tensor_scalar(y.bitcast(I32), w.bitcast(I32), -0.5, MAGIC, ALU.mult, ALU.add))
    for _ in range(3):
        chain.link(eng.tensor_tensor(t, y, y, ALU.mult))
        chain.link(eng.tensor_tensor(t, t, w, ALU.mult))
        chain.link(eng.tensor_scalar(t, t, -0.5, 1.5, ALU.mult, ALU.add))
        chain.link(eng.tensor_tensor(y, y, t, ALU.mult))


def _lay_out(x):
    a = {k: np.asarray(v) for k, v in x.items()}
    d = {"x": a["L0_attn_x"]}
    wqkv = a["L0_attn_Wqkv"].reshape(LAYERS, 3, P, P).transpose(0, 3, 1, 2)
    wo = a["L0_attn_Wo"].transpose(0, 2, 1)[:, :, None, :]
    causal = np.stack([a["L1_ffn_" + n] for n in ("Wq", "Wk", "Wv", "Wo")], 1)[None]
    d["attn_w"] = np.concatenate([np.concatenate([wqkv, wo], 2), causal])
    bqkv = a["L0_attn_bqkv"].reshape(LAYERS, 3, P)
    row = np.stack([bqkv[:, 2], a["L0_attn_bo"], a["L0_attn_ln1_g"], a["L0_attn_ln1_b"]], 1)
    crow = np.stack([a["L1_ffn_" + n] for n in ("bv", "bo", "ln1_g", "ln1_b")])[None]
    d["attn_row"] = np.concatenate([row, crow])
    col = np.stack([bqkv[:, 0], bqkv[:, 1]], 2)
    ccol = np.stack([a["L1_ffn_bq"], a["L1_ffn_bk"]], 1)[None]
    d["attn_col"] = np.concatenate([col, ccol])
    d["ffn_w1"] = a["L0_attn_W1"].transpose(0, 2, 1)
    d["ffn_w2"] = a["L0_attn_W2"].transpose(0, 2, 1).reshape(LAYERS, CHUNKS, P, P).transpose(0, 2, 1, 3)
    d["ffn_row"] = np.stack([a["L0_attn_b2"], a["L0_attn_ln2_g"], a["L0_attn_ln2_b"]], 1)
    d["ffn_col"] = a["L0_attn_b1"].reshape(LAYERS, CHUNKS, P).transpose(0, 2, 1)
    d["crow"] = np.stack([a["L0_attn_norm_in_g"], a["L0_attn_norm_in_b"], a["L1_ffn_ln2_g"], a["L1_ffn_ln2_b"]])
    for n in ("w1", "w2", "b1", "b2"):
        d["L0_" + n], d["L1_" + n] = a["L0_ffn_" + n], a["L1_ffn_e_" + n]
    d["L0_gate"], d["L1_gate"], d["L1_br"] = a["L0_ffn_gate_w"], a["L1_ffn_Wr"], a["L1_ffn_br"]
    d["rec_w"] = np.stack([a["L1_attn_" + n] for n in ("Wq", "Wk", "Wv", "Wout")], 1)
    for n, m in (("f1", "Wf1"), ("f2", "Wf2"), ("o1", "Wo1"), ("o2", "Wo2"), ("g", "Wg"), ("lnw", "ln_w")):
        d["rec_" + n] = a["L1_attn_" + m]
    half = P // 2
    where = np.arange(TOKENS, dtype=np.float32)[:, None]
    turn = where / np.float32(10000.0) ** (np.arange(half, dtype=np.float32)[None] / np.float32(half - 1))
    d["pos"] = np.concatenate([np.cos(turn), np.sin(turn)], 1).astype(np.float32)
    own = (np.arange(P)[:, None] // HD) % 4 == np.arange(4)[None]
    d["hm"] = np.where(own, -1.0 / np.sqrt(HD), 0.0).astype(np.float32)
    d["rev"] = np.arange(EXPERTS, 0, -1).astype(np.float32)
    return {k: np.ascontiguousarray(v) for k, v in d.items()}


def kernel(**inputs):
    import concourse.bacc as _bacc
    from concourse.bass_utils import run_bass_kernel_spmd as _run

    nc = _bacc.Bacc("TRN2", target_bir_lowering=False, num_devices=1)
    arrays = {f"in_{k}_dram": v for k, v in _lay_out(inputs).items()}
    d = {k[3:-5]: nc.dram_tensor(k, v.shape, mybir.dt.from_np(v.dtype), kind="ExternalInput").ap()
         for k, v in arrays.items()}
    out = nc.dram_tensor("out_0_dram", (BATCHES, TOKENS, P), F32, kind="ExternalOutput").ap()
    build(nc, d, out)
    r = _run(nc, [arrays], core_ids=[0])
    return r.results[0]["out_0_dram"]
```
